# Optimizing a Trainium2 kernel written in Bass

```python
import numpy as np
import jax
import jax.numpy as jnp

def _softmax(x, axis=-1):
    return jax.nn.softmax(x, axis=axis)

def _gelu(x):
    return jax.nn.gelu(x, approximate=True)

def _silu(x):
    return jax.nn.silu(x)

def _sigmoid(x):
    return jax.nn.sigmoid(x)

def _layernorm(x, axis=-1, eps=1e-05):
    m = jnp.mean(x, axis=axis, keepdims=True)
    v = jnp.var(x, axis=axis, keepdims=True)
    return (x - m) / jnp.sqrt(v + eps)

def _scatter_add(tgt, idx, src, axis=0):
    return tgt.at[idx].add(src)

def _segment_sum(src, seg, n):
    return jax.ops.segment_sum(src, seg, n)
kernel_name = 'mk_conv_attn_hybrid_d4_conv_nchw128_r4_6cc230'

def setup_inputs(seed: int=0):
    np.random.seed(seed)
    _w = jnp.asarray

    def _rec_inputs():
        import jax
        import jax.numpy as jnp
        _gk = jax.random.key(seed)
        x = -0.0003929 + 0.9999 * jax.random.normal(jax.random.fold_in(_gk, 1), (32, 32, 16, 16), jnp.float32)
        return x
    x = _rec_inputs()

    def _L0_conv_setup():
        import jax, jax.numpy as jnp
        import numpy as np
        HEADS = 4
        DIM_HEAD = 32
        key = jax.random.key(seed)
        k0, k1, k2, k3 = jax.random.split(key, 4)
        b, C, H, W = (32, 32, 16, 16)
        hidden = HEADS * DIM_HEAD
        x = jax.random.normal(k0, (b, C, H, W), dtype=jnp.float32)
        g = jnp.ones((C,), dtype=jnp.float32)
        w_qkv = jax.random.normal(k1, (3 * hidden, C), dtype=jnp.float32) * 0.05
        mem_kv = jax.random.normal(k2, (2, HEADS, DIM_HEAD, 4), dtype=jnp.float32)
        w_out = jax.random.normal(k3, (C, hidden), dtype=jnp.float32) * 0.05
        b_out = jnp.zeros((C,), dtype=jnp.float32)
        return {'x': x, 'g': g, 'w_qkv': w_qkv, 'mem_kv': mem_kv, 'w_out': w_out, 'b_out': b_out}
    _L0_conv_all = _L0_conv_setup()
    _L0_conv_in = {k: v for k, v in _L0_conv_all.items() if k in ('g', 'w_qkv', 'mem_kv', 'w_out', 'b_out')}
    del _L0_conv_all

    def _L1_conv_setup():
        import jax, jax.numpy as jnp
        import numpy as np
        KS = 51
        DENSE_INNER = 2
        DIM = 32
        B, H, W = (16, 16, 16)

        def _make_peripheral_coords(radius, dense_inner=2):
            coords = list(range(0, min(radius, dense_inner) + 1))
            v = 1
            while v < radius:
                v *= 2
                if v > dense_inner and v < radius:
                    coords.append(v)
            if radius not in coords:
                coords.append(radius)
            return sorted(set(coords))

        def _quantise(a, coords):
            q = 0
            for c in coords:
                if c <= a:
                    q = c
                else:
                    break
            return q

        def _build_idx(kernel_size, dense_inner):
            radius = kernel_size // 2
            coords = _make_peripheral_coords(radius, dense_inner)
            signed = [-c for c in reversed(coords[1:])] + list(coords)
            P = len(signed)
            c2i = {c: i for i, c in enumerate(signed)}
            idx = []
            for i in range(kernel_size):
                oi = i - radius
                qi = _quantise(abs(oi), coords)
                ii = c2i[-qi if oi < 0 else qi]
                for j in range(kernel_size):
                    oj = j - radius
                    qj = _quantise(abs(oj), coords)
                    jj = c2i[-qj if oj < 0 else qj]
                    idx.append(ii * P + jj)
            return (np.asarray(idx, dtype=np.int32), P)
        IDX_MAP, P = _build_idx(KS, DENSE_INNER)
        key = jax.random.key(seed)
        k1, k2, k3 = jax.random.split(key, 3)
        x = jax.random.normal(k1, (B, DIM, H, W), dtype=jnp.float32)
        weight_comp = jax.random.normal(k2, (DIM, P * P), dtype=jnp.float32) * 0.02
        kpe = jax.random.normal(k3, (1, 1, KS, KS), dtype=jnp.float32) * 0.02
        return {'x': x, 'weight_comp': weight_comp, 'kpe': kpe}
    _L1_conv_all = _L1_conv_setup()
    _L1_conv_in = {k: v for k, v in _L1_conv_all.items() if k in ('weight_comp', 'kpe')}
    del _L1_conv_all

    def _L2_attn_setup():
        import jax, jax.numpy as jnp
        import numpy as np
        B, N, D = (8, 512, 32)
        N_LAYER, N_HEAD = (4, 8)
        PARAMS_STD = 0.05

        def _attention(V, Q, Z):
            n = Z.shape[1]
            Attn = jnp.einsum('bni,ij,bmj->bnm', Z, Q, Z)
            values = jnp.einsum('ij,bnj->bni', V, Z)
            return jnp.einsum('bnm,bmi->bni', Attn, values) / n
        key = jax.random.key(seed)
        kz, kv, kq = jax.random.split(key, 3)
        Z = jax.random.normal(kz, (B, N, D), dtype=jnp.float32)
        v_matrix = PARAMS_STD * jax.random.normal(kv, (N_LAYER, N_HEAD, 1, D, D), dtype=jnp.float32)
        q_matrix = PARAMS_STD * jax.random.normal(kq, (N_LAYER, N_HEAD, 1, D, D), dtype=jnp.float32)
        return {'Z': Z, 'v_matrix': v_matrix, 'q_matrix': q_matrix}
    _L2_attn_all = _L2_attn_setup()
    _L2_attn_in = {k: v for k, v in _L2_attn_all.items() if k in ('v_matrix', 'q_matrix')}
    del _L2_attn_all

    def _L2_ffn_setup():
        import jax, jax.numpy as jnp
        import numpy as np
        B, N, D, C, E, K = (8, 2048, 32, 32, 8, 2)
        key = jax.random.key(seed)
        k0, k1, k2 = jax.random.split(key, 3)
        x = jax.random.normal(k0, (B, N, D), dtype=jnp.float32)
        router_w = jax.random.normal(k1, (D, E), dtype=jnp.float32) * 0.05
        router_b = jnp.zeros((E,), dtype=jnp.float32)
        expert_w = jax.random.normal(k2, (E, D, C), dtype=jnp.float32) * (1.0 / np.sqrt(D))
        expert_b = jnp.zeros((E, C), dtype=jnp.float32)
        return {'x': x, 'router_w': router_w, 'router_b': router_b, 'expert_w': expert_w, 'expert_b': expert_b}
    _L2_ffn_all = _L2_ffn_setup()
    _L2_ffn_in = {k: v for k, v in _L2_ffn_all.items() if k in ('router_w', 'router_b', 'expert_w', 'expert_b')}
    del _L2_ffn_all

    def _L3_attn_setup():
        import jax, jax.numpy as jnp
        import numpy as np
        N_HEADS = 4
        LN_EPS = 0.001
        key = jax.random.key(seed)
        ks = jax.random.split(key, 9)
        B, S, D = (4, 512, 32)
        w = 0.08
        return {'x': jax.random.normal(ks[0], (B, S, D), jnp.float32), 'Wq': jax.random.normal(ks[1], (D, D), jnp.float32) * w, 'bq': jnp.zeros((D,), jnp.float32), 'Wk': jax.random.normal(ks[2], (D, D), jnp.float32) * w, 'bk': jnp.zeros((D,), jnp.float32), 'Wv': jax.random.normal(ks[3], (D, D), jnp.float32) * w, 'bv': jnp.zeros((D,), jnp.float32), 'Wu': jax.random.normal(ks[4], (D, 2 * D), jnp.float32) * w, 'bu': jnp.zeros((2 * D,), jnp.float32), 'pos_w': jax.random.normal(ks[5], (2 * S - 1,), jnp.float32) * 0.02, 'ln_gamma': 1.0 + jax.random.normal(ks[6], (2 * D,), jnp.float32) * 0.3, 'ln_beta': jax.random.normal(ks[7], (2 * D,), jnp.float32) * 0.0001, 'Wf': jax.random.normal(ks[8], (2 * D, D), jnp.float32) * w, 'bf': jnp.zeros((D,), jnp.float32)}
    _L3_attn_all = _L3_attn_setup()
    _L3_attn_in = {k: v for k, v in _L3_attn_all.items() if k in ('Wq', 'bq', 'Wk', 'bk', 'Wv', 'bv', 'Wu', 'bu', 'pos_w', 'ln_gamma', 'ln_beta', 'Wf', 'bf')}
    del _L3_attn_all

    def _L3_ffn_setup():
        import jax, jax.numpy as jnp
        import numpy as np
        NB, NOPS = (33, 19)
        D, H = (32, 128)
        B, S = (8, 256)
        CARRY_OPS = [0, 1, 2, 10, 11, 12, 13]

        def _build_masks():
            am = np.zeros((NB, NOPS), dtype=bool)
            fm = np.zeros((NB, NOPS), dtype=bool)
            fm[0, :] = True
            for b in range(1, 8):
                am[b, CARRY_OPS] = True
                fm[b, CARRY_OPS] = True
            am[8, [14, 15, 8, 9]] = True
            fm[8, [14, 15, 8, 9]] = True
            for b in range(16, 32):
                fm[b, [3, 4]] = True
            am[32, [10, 11, 12, 13]] = True
            fm[32, [5, 6, 7, 2, 4, 10, 11, 12, 13]] = True
            return (jnp.asarray(am), jnp.asarray(fm))
        key = jax.random.key(seed)
        ks = jax.random.split(key, 9)
        sd = 1.0 / np.sqrt(D)
        sh = 1.0 / np.sqrt(H)
        am, fm = _build_masks()
        return {'x': jax.random.normal(ks[0], (B, S, D), jnp.float32), 'ffn_w1': jax.random.normal(ks[1], (NB, NOPS, D, H), jnp.float32) * sd, 'ffn_b1': jnp.zeros((NB, NOPS, H), jnp.float32), 'ffn_w2': jax.random.normal(ks[2], (NB, NOPS, H, D), jnp.float32) * sh, 'ffn_b2': jnp.zeros((NB, NOPS, D), jnp.float32), 'wq': jax.random.normal(ks[3], (NB, NOPS, D, D), jnp.float32) * sd, 'wk': jax.random.normal(ks[4], (NB, NOPS, D, D), jnp.float32) * sd, 'wv': jax.random.normal(ks[5], (NB, NOPS, D, D), jnp.float32) * sd, 'wo': jax.random.normal(ks[6], (NB, NOPS, D, D), jnp.float32) * sd, 'attn_mask': am, 'ffn_mask': fm}
    _L3_ffn_all = _L3_ffn_setup()
    _L3_ffn_in = {k: v for k, v in _L3_ffn_all.items() if k in ('ffn_w1', 'ffn_b1', 'ffn_w2', 'ffn_b2', 'wq', 'wk', 'wv', 'wo', 'attn_mask', 'ffn_mask')}
    del _L3_ffn_all
    return {'x': x, 'L0_conv_g': _L0_conv_in['g'], 'L0_conv_w_qkv': _L0_conv_in['w_qkv'], 'L0_conv_mem_kv': _L0_conv_in['mem_kv'], 'L0_conv_w_out': _L0_conv_in['w_out'], 'L0_conv_b_out': _L0_conv_in['b_out'], 'L1_conv_weight_comp': _L1_conv_in['weight_comp'], 'L1_conv_kpe': _L1_conv_in['kpe'], 'L2_attn_v_matrix': _L2_attn_in['v_matrix'], 'L2_attn_q_matrix': _L2_attn_in['q_matrix'], 'L2_ffn_router_w': _L2_ffn_in['router_w'], 'L2_ffn_router_b': _L2_ffn_in['router_b'], 'L2_ffn_expert_w': _L2_ffn_in['expert_w'], 'L2_ffn_expert_b': _L2_ffn_in['expert_b'], 'L3_attn_Wq': _L3_attn_in['Wq'], 'L3_attn_bq': _L3_attn_in['bq'], 'L3_attn_Wk': _L3_attn_in['Wk'], 'L3_attn_bk': _L3_attn_in['bk'], 'L3_attn_Wv': _L3_attn_in['Wv'], 'L3_attn_bv': _L3_attn_in['bv'], 'L3_attn_Wu': _L3_attn_in['Wu'], 'L3_attn_bu': _L3_attn_in['bu'], 'L3_attn_pos_w': _L3_attn_in['pos_w'], 'L3_attn_ln_gamma': _L3_attn_in['ln_gamma'], 'L3_attn_ln_beta': _L3_attn_in['ln_beta'], 'L3_attn_Wf': _L3_attn_in['Wf'], 'L3_attn_bf': _L3_attn_in['bf'], 'L3_ffn_ffn_w1': _L3_ffn_in['ffn_w1'], 'L3_ffn_ffn_b1': _L3_ffn_in['ffn_b1'], 'L3_ffn_ffn_w2': _L3_ffn_in['ffn_w2'], 'L3_ffn_ffn_b2': _L3_ffn_in['ffn_b2'], 'L3_ffn_wq': _L3_ffn_in['wq'], 'L3_ffn_wk': _L3_ffn_in['wk'], 'L3_ffn_wv': _L3_ffn_in['wv'], 'L3_ffn_wo': _L3_ffn_in['wo'], 'L3_ffn_attn_mask': _L3_ffn_in['attn_mask'], 'L3_ffn_ffn_mask': _L3_ffn_in['ffn_mask']}

def reference(x, L0_conv_g, L0_conv_w_qkv, L0_conv_mem_kv, L0_conv_w_out, L0_conv_b_out, L1_conv_weight_comp, L1_conv_kpe, L2_attn_v_matrix, L2_attn_q_matrix, L2_ffn_router_w, L2_ffn_router_b, L2_ffn_expert_w, L2_ffn_expert_b, L3_attn_Wq, L3_attn_bq, L3_attn_Wk, L3_attn_bk, L3_attn_Wv, L3_attn_bv, L3_attn_Wu, L3_attn_bu, L3_attn_pos_w, L3_attn_ln_gamma, L3_attn_ln_beta, L3_attn_Wf, L3_attn_bf, L3_ffn_ffn_w1, L3_ffn_ffn_b1, L3_ffn_ffn_w2, L3_ffn_ffn_b2, L3_ffn_wq, L3_ffn_wk, L3_ffn_wv, L3_ffn_wo, L3_ffn_attn_mask, L3_ffn_ffn_mask):
    import jax
    import jax.numpy as jnp

    def _L0_conv_ref(x, g, w_qkv, mem_kv, w_out, b_out):
        import jax, jax.numpy as jnp
        import numpy as np
        HEADS = 4
        DIM_HEAD = 32
        b, C, H, W = x.shape
        heads = mem_kv.shape[1]
        dh = mem_kv.shape[2]
        hidden = heads * dh
        scale = dh ** (-0.5)
        norm = jnp.maximum(jnp.sqrt(jnp.sum(x * x, axis=1, keepdims=True)), 1e-12)
        xn = x / norm * g[None, :, None, None] * C ** 0.5
        qkv = jnp.einsum('bchw,oc->bohw', xn, w_qkv)
        q, k, v = jnp.split(qkv, 3, axis=1)
        n = H * W
        q = q.reshape(b, heads, dh, n)
        k = k.reshape(b, heads, dh, n)
        v = v.reshape(b, heads, dh, n)
        mk = jnp.broadcast_to(mem_kv[0][None], (b, heads, dh, mem_kv.shape[3]))
        mv = jnp.broadcast_to(mem_kv[1][None], (b, heads, dh, mem_kv.shape[3]))
        k = jnp.concatenate([mk, k], axis=-1)
        v = jnp.concatenate([mv, v], axis=-1)
        q = jax.nn.softmax(q, axis=-2) * scale
        k = jax.nn.softmax(k, axis=-1)
        context = jnp.einsum('bhdn,bhen->bhde', k, v)
        out = jnp.einsum('bhde,bhdn->bhen', context, q)
        out = out.reshape(b, hidden, H, W)
        return jnp.einsum('bchw,oc->bohw', out, w_out) + b_out[None, :, None, None]

    def _L1_conv_ref(x, weight_comp, kpe):
        import jax, jax.numpy as jnp
        import numpy as np
        KS = 51
        DENSE_INNER = 2
        DIM = 32
        B, H, W = (16, 16, 16)

        def _make_peripheral_coords(radius, dense_inner=2):
            coords = list(range(0, min(radius, dense_inner) + 1))
            v = 1
            while v < radius:
                v *= 2
                if v > dense_inner and v < radius:
                    coords.append(v)
            if radius not in coords:
                coords.append(radius)
            return sorted(set(coords))

        def _quantise(a, coords):
            q = 0
            for c in coords:
                if c <= a:
                    q = c
                else:
                    break
            return q

        def _build_idx(kernel_size, dense_inner):
            radius = kernel_size // 2
            coords = _make_peripheral_coords(radius, dense_inner)
            signed = [-c for c in reversed(coords[1:])] + list(coords)
            P = len(signed)
            c2i = {c: i for i, c in enumerate(signed)}
            idx = []
            for i in range(kernel_size):
                oi = i - radius
                qi = _quantise(abs(oi), coords)
                ii = c2i[-qi if oi < 0 else qi]
                for j in range(kernel_size):
                    oj = j - radius
                    qj = _quantise(abs(oj), coords)
                    jj = c2i[-qj if oj < 0 else qj]
                    idx.append(ii * P + jj)
            return (np.asarray(idx, dtype=np.int32), P)
        IDX_MAP, P = _build_idx(KS, DENSE_INNER)
        dim = weight_comp.shape[0]
        weight = weight_comp[:, IDX_MAP].reshape(dim, 1, KS, KS) + kpe
        pad = KS // 2
        return jax.lax.conv_general_dilated(x, weight, window_strides=(1, 1), padding=[(pad, pad), (pad, pad)], dimension_numbers=('NCHW', 'OIHW', 'NCHW'), feature_group_count=dim)

    def _L2_attn_ref(Z, v_matrix, q_matrix):
        import jax, jax.numpy as jnp
        import numpy as np
        B, N, D = (8, 512, 32)
        N_LAYER, N_HEAD = (4, 8)
        PARAMS_STD = 0.05

        def _attention(V, Q, Z):
            n = Z.shape[1]
            Attn = jnp.einsum('bni,ij,bmj->bnm', Z, Q, Z)
            values = jnp.einsum('ij,bnj->bni', V, Z)
            return jnp.einsum('bnm,bmi->bni', Attn, values) / n
        n_layer, n_head = (v_matrix.shape[0], v_matrix.shape[1])
        for i in range(n_layer):
            Zi = Z
            residues = jnp.zeros_like(Zi)
            for j in range(n_head):
                Vij = v_matrix[i, j, 0]
                Qij = q_matrix[i, j, 0]
                residues = residues + _attention(Vij, Qij, Zi)
            Z = Zi + residues / n_head
        return Z

    def _L2_ffn_ref(x, router_w, router_b, expert_w, expert_b):
        import jax, jax.numpy as jnp
        import numpy as np
        B, N, D, C, E, K = (8, 2048, 32, 32, 8, 2)
        router_probs = jax.nn.softmax(x @ router_w + router_b, axis=-1)
        top_p, top_i = jax.lax.top_k(router_probs, K)
        top_p = top_p / jnp.sum(top_p, axis=-1, keepdims=True)
        expert_out = jnp.einsum('bnd,edc->bnec', x, expert_w) + expert_b
        gathered = jnp.take_along_axis(expert_out, top_i[..., None], axis=2)
        return jnp.einsum('bnk,bnkc->bnc', top_p, gathered)

    def _L3_attn_ref(x, Wq, bq, Wk, bk, Wv, bv, Wu, bu, pos_w, ln_gamma, ln_beta, Wf, bf):
        import jax, jax.numpy as jnp
        import numpy as np
        N_HEADS = 4
        LN_EPS = 0.001
        B, S, D = x.shape
        H = N_HEADS
        hd = D // H
        q = jax.nn.silu(x @ Wq + bq)
        k = jax.nn.silu(x @ Wk + bk)
        v = jax.nn.silu(x @ Wv + bv)
        u = x @ Wu + bu
        idx = S - 1 + jnp.arange(S)[None, :] - jnp.arange(S)[:, None]
        rel = pos_w[idx]
        pos_attn = jnp.einsum('nm,bmd->bnd', rel, v)
        qh = q.reshape(B, S, H, hd).transpose(0, 2, 1, 3)
        kh = k.reshape(B, S, H, hd).transpose(0, 2, 1, 3)
        vh = v.reshape(B, S, H, hd).transpose(0, 2, 1, 3)
        scores = jnp.einsum('bhnd,bhmd->bhnm', qh, kh) / jnp.sqrt(jnp.float32(hd))
        causal = jnp.tril(jnp.ones((S, S), dtype=bool))
        scores = jnp.where(causal[None, None], scores * scores, 0.0)
        self_attn = jnp.einsum('bhnm,bhmd->bhnd', jax.nn.silu(scores), vh)
        self_attn = self_attn.transpose(0, 2, 1, 3).reshape(B, S, D)
        a = jnp.concatenate([self_attn, pos_attn], axis=-1)
        mu = jnp.mean(a, axis=-1, keepdims=True)
        var = jnp.mean(jnp.square(a - mu), axis=-1, keepdims=True)
        a = (a - mu) * jax.lax.rsqrt(var + LN_EPS) * ln_gamma + ln_beta
        out = jax.nn.relu(u * a @ Wf + bf) + x
        return out

    def _L3_ffn_ref(x, ffn_w1, ffn_b1, ffn_w2, ffn_b2, wq, wk, wv, wo, attn_mask, ffn_mask):
        import jax, jax.numpy as jnp
        import numpy as np
        NB, NOPS = (33, 19)
        D, H = (32, 128)
        B, S = (8, 256)
        CARRY_OPS = [0, 1, 2, 10, 11, 12, 13]

        def _build_masks():
            am = np.zeros((NB, NOPS), dtype=bool)
            fm = np.zeros((NB, NOPS), dtype=bool)
            fm[0, :] = True
            for b in range(1, 8):
                am[b, CARRY_OPS] = True
                fm[b, CARRY_OPS] = True
            am[8, [14, 15, 8, 9]] = True
            fm[8, [14, 15, 8, 9]] = True
            for b in range(16, 32):
                fm[b, [3, 4]] = True
            am[32, [10, 11, 12, 13]] = True
            fm[32, [5, 6, 7, 2, 4, 10, 11, 12, 13]] = True
            return (jnp.asarray(am), jnp.asarray(fm))
        scale = jnp.asarray(1.0 / np.sqrt(D), x.dtype)

        def step(h, p):
            op = jnp.argmax(h[0, 0, :NOPS])
            q = h @ p['wq'][op]
            k = h @ p['wk'][op]
            v = h @ p['wv'][op]
            attn = jax.nn.softmax(jnp.einsum('bqd,bkd->bqk', q, k) * scale, axis=-1)
            y = jnp.einsum('bqk,bkd->bqd', attn, v) @ p['wo'][op]
            h = jnp.where(p['am'][op], y, h)
            z = jax.nn.relu(h @ p['w1'][op] + p['b1'][op]) @ p['w2'][op] + p['b2'][op]
            h = jnp.where(p['fm'][op], z, h)
            return (h, None)
        xs = {'w1': ffn_w1, 'b1': ffn_b1, 'w2': ffn_w2, 'b2': ffn_b2, 'wq': wq, 'wk': wk, 'wv': wv, 'wo': wo, 'am': attn_mask, 'fm': ffn_mask}
        out, _ = jax.lax.scan(step, x, xs)
        return out

    def _gn(v, G=32, eps=1e-05):
        B_, C_, H_, W_ = v.shape
        g = v.reshape(B_, G, C_ // G, H_, W_)
        m = jnp.mean(g, axis=(2, 3, 4), keepdims=True)
        s = jnp.var(g, axis=(2, 3, 4), keepdims=True)
        return ((g - m) / jnp.sqrt(s + eps)).reshape(v.shape)

    def _ln_c(v, eps=1e-06):
        m = jnp.mean(v, axis=1, keepdims=True)
        s = jnp.var(v, axis=1, keepdims=True)
        return (v - m) / jnp.sqrt(s + eps)

    def _ln_t(v, eps=1e-05):
        m = jnp.mean(v, axis=-1, keepdims=True)
        s = jnp.var(v, axis=-1, keepdims=True)
        return (v - m) / jnp.sqrt(s + eps)

    def _to_tokens(v):
        B_, C_, H_, W_ = v.shape
        return v.reshape(B_, C_, H_ * W_).transpose(0, 2, 1)

    def _from_tokens(t, like):
        B_, C_, H_, W_ = like.shape
        return t.transpose(0, 2, 1).reshape(B_, C_, H_, W_)
    x = x + _L0_conv_ref(_gn(x), L0_conv_g, L0_conv_w_qkv, L0_conv_mem_kv, L0_conv_w_out, L0_conv_b_out)
    x = x + _L1_conv_ref(_gn(x), L1_conv_weight_comp, L1_conv_kpe)
    t = _to_tokens(x)
    t = t + _L2_attn_ref(_ln_t(t), L2_attn_v_matrix, L2_attn_q_matrix)
    t = t + _L2_ffn_ref(_ln_t(t), L2_ffn_router_w, L2_ffn_router_b, L2_ffn_expert_w, L2_ffn_expert_b)
    t = t + _L3_attn_ref(_ln_t(t), L3_attn_Wq, L3_attn_bq, L3_attn_Wk, L3_attn_bk, L3_attn_Wv, L3_attn_bv, L3_attn_Wu, L3_attn_bu, L3_attn_pos_w, L3_attn_ln_gamma, L3_attn_ln_beta, L3_attn_Wf, L3_attn_bf)
    t = t + _L3_ffn_ref(_ln_t(t), L3_ffn_ffn_w1, L3_ffn_ffn_b1, L3_ffn_ffn_w2, L3_ffn_ffn_b2, L3_ffn_wq, L3_ffn_wk, L3_ffn_wv, L3_ffn_wo, L3_ffn_attn_mask, L3_ffn_ffn_mask)
    x = _from_tokens(t, x)
    return x

_drawn_inputs = setup_inputs


def setup_inputs(seed=0):
    import zlib

    import numpy as np

    out = dict(_drawn_inputs(seed))
    spreads = {'L0_conv_g': (1.0, 0.6),
     'L0_conv_b_out': (0.0, 0.1),
     'L2_ffn_router_b': (0.0, 0.1),
     'L2_ffn_expert_b': (0.0, 0.34),
     'L3_attn_bq': (0.0, 0.8),
     'L3_attn_bk': (0.0, 0.8),
     'L3_attn_bv': (0.0, 0.589),
     'L3_attn_bu': (0.0, 0.8),
     'L3_attn_bf': (0.0, 0.363),
     'L3_ffn_ffn_b1': (0.0, 0.1),
     'L3_ffn_ffn_b2': (0.0, 0.288)}
    factors = {'L0_conv_w_qkv': 8.0,
     'L0_conv_mem_kv': 6.932,
     'L0_conv_w_out': 5.532,
     'L3_attn_Wq': 3.588,
     'L3_attn_Wk': 4.613,
     'L3_attn_ln_gamma': 2.92,
     'L3_attn_ln_beta': 200.0,
     'L3_ffn_wq': 4.242,
     'L3_ffn_wk': 4.922,
     'L3_attn_pos_w': 32.705}
    for name, (base, spread) in spreads.items():
        noise = np.random.default_rng([zlib.crc32(name.encode()), seed]).standard_normal(out[name].shape)
        drawn = base * np.exp(spread * noise) if base else spread * noise
        out[name] = jnp.asarray(drawn.astype(out[name].dtype))
    for name, factor in factors.items():
        out[name] = (out[name] * factor).astype(out[name].dtype)
    return out
```

```python
import concourse.bass as bass
from concourse import mybir
from contextlib import ExitStack

F32 = mybir.dt.float32
BF16 = mybir.dt.bfloat16
I32 = mybir.dt.int32
ALU = mybir.AluOpType
ACT = mybir.ActivationFunctionType
AXX = mybir.AxisListType.X

B, C, H, W = 32, 32, 16, 16
N = H * W
J, G = 4, 8
S = N // 128
COLS = G * N
CH = 512
NCH = COLS // CH
HEADS, DH = 4, 32
MEM = 4
KS, CONV_P = 51, 13
R = H - 1
CLASSES = 9
CLASS0 = 2
CLASS_SPANS = [(-15, -8), (-7, -4), (-3, -2), (-1, -1), (0, 0), (1, 1), (2, 3), (4, 7), (8, 15)]
LAYERS, ZHEADS = 4, 8
E = 8
AH, AHD = 4, 8
NB, NOPS, HID = 33, 19, 128

EPS_GN, EPS_T, EPS_A = 1e-5, 1e-5, 1e-3


class Mem:
    pass


def normalise_tokens(nc, m, sem, name, parts, outs, eps, mean_w, gamma=None):
    n = len(parts)
    mean_ready = sem(name + "_mean_ready")
    centred = sem(name + "_centred")
    squared = sem(name + "_squared")
    var_ready = sem(name + "_var_ready")
    std_ready = sem(name + "_std_ready")
    inverted = sem(name + "_inverted")
    scaled = sem(name + "_scaled")
    ps = m.ps
    sq = [m.tmpA, m.tmpB]

    def ch(t, k):
        return t[:, k * CH:(k + 1) * CH]

    with nc.Block() as block:
        @block.tensor
        def _(pe):
            for k in range(NCH):
                for i in range(n):
                    mm = pe.matmul(ps[:, k, :], mean_w[:, :], ch(parts[i], k), start=(i == 0), stop=(i == n - 1))
                mm.then_inc(mean_ready, 1)
            for k in range(NCH):
                pe.wait_ge(squared, n * (k + 1))
                for i in range(n):
                    mm = pe.matmul(ps[:, NCH + k, :], mean_w[:, :], ch(sq[i], k), start=(i == 0), stop=(i == n - 1))
                mm.then_inc(var_ready, 1)

        @block.vector
        def _(dve):
            for k in range(NCH):
                dve.wait_ge(mean_ready, k + 1)
                for i in range(n):
                    dve.tensor_tensor(ch(outs[i], k), ch(parts[i], k), ps[:, k, :], ALU.subtract).then_inc(centred, 1)
            for k in range(NCH):
                dve.wait_ge(std_ready, k + 1)
                dve.reciprocal(m.rstd[:, k * CH:(k + 1) * CH], ps[:, k, :]).then_inc(inverted, 1)
                dve.wait_ge(inverted, k + 1)
                for i in range(n):
                    o = ch(outs[i], k)
                    dve.tensor_tensor(o, o, m.rstd[:, k * CH:(k + 1) * CH], ALU.mult).then_inc(scaled, 1)
                    if gamma:
                        dve.wait_ge(scaled, 2 * (n * k + i) + 1)
                        dve.tensor_scalar(o, o, gamma[i][0], gamma[i][1], ALU.mult, ALU.add).then_inc(scaled, 1)

        @block.scalar
        def _(act):
            for k in range(NCH):
                for i in range(n):
                    act.wait_ge(centred, n * k + i + 1)
                    act.activation(ch(sq[i], k), ch(outs[i], k), ACT.Square).then_inc(squared, 1)
            for k in range(NCH):
                act.wait_ge(var_ready, k + 1)
                act.activation(ps[:, k, :], ps[:, NCH + k, :], ACT.Sqrt, bias=eps).then_inc(std_ready, 1)


def instance_norm(nc, m, sem, name, src, dst):
    stats = sem(name + "_stats")
    moments = sem(name + "_moments")
    std = sem(name + "_std")
    inv = sem(name + "_inv")
    done = sem(name + "_done")
    with nc.Block() as block:
        @block.vector
        def _(dve):
            for g in range(G):
                dve.bn_stats(m.bst[:, 6 * g:6 * g + 6], src[:, g * N:(g + 1) * N]).then_inc(stats, 1)
            for g in range(G):
                dve.wait_ge(stats, g + 1)
                dve.bn_aggr(m.bag[:, 2 * g:2 * g + 2], m.bst[:, 6 * g:6 * g + 6]).then_inc(moments, 1)
            dve.wait_ge(std, 1)
            dve.reciprocal(m.inv8[:, :], m.std8[:, :]).then_inc(inv, 1)
            dve.wait_ge(inv, 1)
            for g in range(G):
                c = slice(g * N, (g + 1) * N)
                dve.tensor_scalar(dst[:, c], src[:, c], m.bag[:, 2 * g:2 * g + 1], m.inv8[:, g:g + 1],
                                  ALU.subtract, ALU.mult).then_inc(done, 1)

        @block.scalar
        def _(act):
            act.wait_ge(moments, G)
            act.activation(m.std8[:, :], m.bag[:, 1:2 * G:2], ACT.Sqrt, bias=m.eps[:, 0:1]).then_inc(std, 1)


def linear_attention(nc, m, sem):
    ps = m.ps
    UN = G // 2 * J
    ek, ekt, vt, qt, qf = m.r0, m.r1, m.r2, m.r3, m.r0
    xn = m.tmpA
    squared = sem("la_squared")
    norm2_ready = sem("la_norm2_ready")
    norm_ready = sem("la_norm_ready")
    inv_ready = sem("la_inv_ready")
    xn_ready = sem("la_xn_ready")
    proj_ready = sem("la_proj_ready")
    kmax_ready = sem("la_kmax_ready")
    knegmax_ready = sem("la_knegmax_ready")
    kexp_done = sem("la_kexp_done")
    kt_ready = sem("la_kt_ready")
    kt_copied = sem("la_kt_copied")
    v_copied = sem("la_v_copied")
    qmax_ready = sem("la_qmax_ready")
    qsub_done = sem("la_qsub_done")
    qexp_done = sem("la_qexp_done")
    qsum_ready = sem("la_qsum_ready")
    qinv_ready = sem("la_qinv_ready")
    qnorm_done = sem("la_qnorm_done")
    qt_ready = sem("la_qt_ready")
    qt_copied = sem("la_qt_copied")
    memmax_ready = sem("la_memmax_ready")
    memshift_done = sem("la_memshift_done")
    memexp_done = sem("la_memexp_done")
    memsum = sem("la_memsum")
    memt_ready = sem("la_memt_ready")
    memt_copied = sem("la_memt_copied")
    memv_masked = sem("la_memv_masked")
    ctx_ready = sem("la_ctx_ready")
    ctx_copied = sem("la_ctx_copied")
    w2_ready = sem("la_w2_ready")
    w2_scaled = sem("la_w2_scaled")
    out_ready = sem("la_out_ready")
    added = sem("la_added")

    def bank_free(eng, w):
        p, u = divmod(w - 4, UN)
        if w >= 4:
            if p == 0:
                eng.wait_ge(kexp_done, 2 * (u + 1))
            elif p == 1:
                eng.wait_ge(v_copied, u + 1)
            else:
                eng.wait_ge(qsub_done, u + 1)

    def unit(u):
        return u % 4, 2 * (u // 4)

    with nc.Block() as block:
        @block.tensor
        def _(pe):
            for k in range(NCH):
                pe.wait_ge(squared, k + 1)
                pe.matmul(ps[:, 4 + k, :], m.blkone[:, :], m.tmpB[:, k * CH:(k + 1) * CH],
                          start=True, stop=True).then_inc(norm2_ready, 1)
            pe.wait_ge(xn_ready, NCH)

            def project(w):
                p, u = divmod(w, UN)
                j, g = unit(u)
                rows = slice(32 * j, 32 * j + 32)
                bank_free(pe, w)
                if p == 0:
                    mm = pe.matmul(ps[:, j, :], m.wqkv[rows, 128:256], xn[rows, g * N:(g + 2) * N],
                                   start=True, stop=True)
                else:
                    wcols = m.wqkv[rows, 256:384] if p == 1 else m.wqkv[rows, 0:128]
                    for q in range(4):
                        mm = pe.matmul(ps[:, j, q * 128:(q + 1) * 128],
                                       xn[rows, g * N + q * 128:g * N + (q + 1) * 128], wcols,
                                       start=True, stop=True)
                mm.then_inc(proj_ready, 1)

            def transposes(w):
                p, u = divmod(w, UN)
                j, g = unit(u)
                if p == 0:
                    if u >= 4:
                        pe.wait_ge(kt_copied, u - 3)
                    pe.wait_ge(kexp_done, 2 * (u + 1))
                    src, ready = ek, kt_ready
                else:
                    if u < 4:
                        pe.wait_ge(kt_copied, UN)
                    else:
                        pe.wait_ge(qt_copied, u - 3)
                    pe.wait_ge(qnorm_done, u + 1)
                    src, ready = qt, qt_ready
                for q in range(4):
                    mm = pe.transpose(ps[:, 4 + j, q * 128:(q + 1) * 128],
                                      src[:, j * G + g + q // 2, (q % 2) * 128:(q % 2) * 128 + 128], m.ident[:, :])
                mm.then_inc(ready, 1)

            for w in range(3 * UN + 6):
                if w < 3 * UN:
                    project(w)
                if 4 <= w < UN + 4:
                    transposes(w - 4)
                if w == UN + 5:
                    pe.wait_ge(memexp_done, 1)
                    pe.wait_ge(kt_copied, UN)
                    pe.transpose(ps[:, 4, 0:128], m.em[:, :], m.ident[:, :]).then_inc(memt_ready, 1)
                if w == UN + 6:
                    pe.wait_ge(memt_copied, 1)
                if w >= 2 * UN + 6:
                    transposes(w - 2 * UN - 6 + UN)
            pe.wait_ge(memv_masked, 1)
            pe.wait_ge(v_copied, UN)
            pe.wait_ge(qsub_done, UN)
            for q in range(B // 4):
                bank = q % 4
                if q >= 4:
                    pe.wait_ge(ctx_copied, q - 3)
                for i in range(4):
                    b = 4 * q + i
                    o = ps[:, bank, i * 128:(i + 1) * 128]
                    for s in range(S):
                        pe.matmul(o, vt[:, b, s * 128:(s + 1) * 128], ekt[:, b, s * 128:(s + 1) * 128],
                                  start=(s == 0), stop=False)
                    mm = pe.matmul(o, m.memv_b[:, b, :], m.emt[:, :], start=False, stop=True)
                mm.then_inc(ctx_ready, 1)
            pe.wait_ge(qt_copied, UN)
            for b in range(B):
                if b % 4 == 0:
                    pe.wait_ge(ctx_copied, b // 4 + 1)
                mm = pe.matmul(ps[:, 4 + b // 16, (b % 16) * 32:(b % 16) * 32 + 32], m.ct[:, b, :], m.wo[:, :],
                               start=True, stop=True)
            mm.then_inc(w2_ready, 1)
            pe.wait_ge(w2_scaled, 1)
            for k in range(NCH):
                for h in range(2):
                    for j in range(J):
                        b = j * G + 2 * k + h
                        mm = pe.matmul(ps[32 * j:32 * j + 32, k, h * N:(h + 1) * N], m.w2[:, b, :], qf[:, b, :],
                                       start=True, stop=True)
                mm.then_inc(out_ready, 1)

        @block.vector
        def _(dve):
            own = sem("la_dve")
            dve.tensor_reduce(m.small[:, 0:1], m.memk[:, :], AXX, ALU.max).then_inc(memmax_ready, 1)
            dve.tensor_scalar(m.gs[:, :], m.gcol[:, :], float(C) ** 0.5, None, ALU.mult).then_inc(own, 1)
            for k in range(NCH):
                c = slice(k * CH, (k + 1) * CH)
                dve.wait_ge(norm_ready, k + 1)
                dve.tensor_scalar(m.rstd[:, c], ps[:, k, :], 1e-12, None, ALU.max).then_inc(inv_ready, 1)
            for k in range(NCH):
                c = slice(k * CH, (k + 1) * CH)
                dve.wait_ge(inv_ready, NCH + k if k else NCH)
                dve.reciprocal(m.rstd[:, c], m.rstd[:, c]).then_inc(inv_ready, 1)
            dve.wait_ge(own, 1)
            for k in range(NCH):
                c = slice(k * CH, (k + 1) * CH)
                dve.wait_ge(inv_ready, NCH + k + 1)
                dve.scalar_tensor_tensor(xn[:, c], m.z[:, c], m.gs[:, 0:1], m.rstd[:, c],
                                         ALU.mult, ALU.mult).then_inc(xn_ready, 1)
            dve.wait_ge(memmax_ready, 1)
            for u in range(UN):
                j, g = unit(u)
                b = j * G + g
                dve.wait_ge(proj_ready, u + 1)
                dve.tensor_reduce(m.kmax[:, b:b + 2], ps[:, j, :].rearrange("p (a n) -> p a n", a=2),
                                  AXX, ALU.max).then_inc(kmax_ready, 1)
                dve.wait_ge(kmax_ready, u + 1)
                dve.tensor_scalar(m.knegmax[:, b:b + 2], m.kmax[:, b:b + 2], m.small[:, 0:1], -1.0,
                                  ALU.max, ALU.mult).then_inc(knegmax_ready, 1)
            dve.wait_ge(knegmax_ready, UN)
            dve.tensor_tensor(m.em[:, :].rearrange("p (b m) -> p b m", m=MEM),
                              m.memk[:, None, :].broadcast_to([128, B, MEM]),
                              m.knegmax[:, :, None].broadcast_to([128, B, MEM]), ALU.add).then_inc(memshift_done, 1)

            def normalise(u):
                j, g = unit(u)
                b = j * G + g
                q = qt[:, b:b + 2, :].rearrange("p b (s h d) -> p (b s h) d", h=HEADS, d=DH)
                st = slice(16 * u, 16 * u + 16)
                dve.wait_ge(qexp_done, u + 1)
                dve.tensor_reduce(m.qsum[:, st], q, AXX, ALU.add).then_inc(qsum_ready, 1)
                dve.wait_ge(qsum_ready, u + 1)
                dve.reciprocal(m.qinv[:, st], m.qsum[:, st]).then_inc(qinv_ready, 1)
                dve.wait_ge(qinv_ready, u + 1)
                dve.tensor_tensor(q, q, m.qinv[:, st].unsqueeze(2).broadcast_to([128, 16, DH]),
                                  ALU.mult).then_inc(qnorm_done, 1)

            for u in range(UN):
                j, g = unit(u)
                b = j * G + g
                p = ps[:, j, :].rearrange("p (a d) -> p a d", d=DH)
                st = slice(16 * u, 16 * u + 16)
                dve.wait_ge(proj_ready, 2 * UN + u + 1)
                dve.tensor_reduce(m.qmax[:, st], p, AXX, ALU.max).then_inc(qmax_ready, 1)
                dve.wait_ge(qmax_ready, u + 1)
                q = qt[:, b:b + 2, :].rearrange("p b (s h d) -> p (b s h) d", h=HEADS, d=DH)
                dve.tensor_tensor(q, p, m.qmax[:, st].unsqueeze(2).broadcast_to([128, 16, DH]),
                                  ALU.subtract).then_inc(qsub_done, 1)
                if u >= 1:
                    normalise(u - 1)
            normalise(UN - 1)
            dve.wait_ge(memexp_done, 1)
            dve.tensor_reduce(m.memsum[:, :], m.em[:, :].rearrange("p (b m) -> p b m", m=MEM), AXX,
                              ALU.add).then_inc(memsum, 1)
            dve.wait_ge(memsum, 1)
            dve.wait_ge(kexp_done, 2 * UN)
            dve.tensor_tensor(m.ksum[:, :], m.ksum[:, :], m.memsum[:, :], ALU.add).then_inc(memsum, 1)
            dve.wait_ge(memsum, 2)
            dve.reciprocal(m.ksum[:, :], m.ksum[:, :]).then_inc(memsum, 1)
            dve.wait_ge(memsum, 3)
            dve.tensor_scalar(m.ksum[:, :], m.ksum[:, :], float(DH) ** -0.5, None, ALU.mult).then_inc(memsum, 1)
            for q in range(B // 4):
                dve.wait_ge(ctx_ready, q + 1)
                dve.tensor_tensor(m.ct[:, 4 * q:4 * q + 4, :], ps[:, q % 4, :].rearrange("p (b d) -> p b d", b=4),
                                  m.blkone[:, None, :].broadcast_to([128, 4, 128]), ALU.mult).then_inc(ctx_copied, 1)
            dve.wait_ge(memsum, 4)
            dve.wait_ge(w2_ready, 1)
            dve.tensor_tensor(m.w2[:, :, :], ps[:, 4:6, :].rearrange("p a (b c) -> p (a b) c", c=C),
                              m.ksum[:, :, None].broadcast_to([128, B, C]), ALU.mult).then_inc(w2_scaled, 1)
            for k in range(NCH):
                c = slice(k * CH, (k + 1) * CH)
                dve.wait_ge(out_ready, k + 1)
                dve.scalar_tensor_tensor(m.x[:, c], ps[:, k, :], m.bout[:, 0:1], m.x[:, c],
                                         ALU.add, ALU.add).then_inc(added, 1)

        @block.scalar
        def _(act):
            for k in range(NCH):
                c = slice(k * CH, (k + 1) * CH)
                act.activation(m.tmpB[:, c], m.z[:, c], ACT.Square).then_inc(squared, 1)
            for k in range(NCH):
                act.wait_ge(norm2_ready, k + 1)
                act.activation(ps[:, k, :], ps[:, 4 + k, :], ACT.Sqrt).then_inc(norm_ready, 1)

            def copy_transposed(p, u):
                j, g = unit(u)
                b = j * G + g
                ready, dst, done = (kt_ready, ekt, kt_copied) if p == 0 else (qt_ready, qf, qt_copied)
                act.wait_ge(ready, u + 1)
                act.activation(dst[:, b:b + 2, :].rearrange("p b n -> p (b n)"), ps[:, 4 + j, :],
                               ACT.Copy).then_inc(done, 1)

            for u in range(UN + 5):
                if u < UN:
                    j, g = unit(u)
                    act.wait_ge(knegmax_ready, u + 1)
                    for i in range(2):
                        b = j * G + g + i
                        act.activation(ek[:, b, :], ps[:, j, i * N:(i + 1) * N], ACT.Exp, bias=m.knegmax[:, b:b + 1],
                                       accum_out=m.ksum[:, b:b + 1]).then_inc(kexp_done, 1)
                if u >= 5:
                    copy_transposed(0, u - 5)
            act.wait_ge(memshift_done, 1)
            act.activation(m.em[:, :], m.em[:, :], ACT.Exp).then_inc(memexp_done, 1)
            for u in range(UN):
                j, g = unit(u)
                b = j * G + g
                act.wait_ge(proj_ready, UN + u + 1)
                act.activation(vt[:, b:b + 2, :].rearrange("p b n -> p (b n)"), ps[:, j, :],
                               ACT.Copy).then_inc(v_copied, 1)
                if u == 6:
                    act.wait_ge(memt_ready, 1)
                    act.activation(m.emt[:, :], ps[:, 4, 0:128], ACT.Copy).then_inc(memt_copied, 1)
            for u in range(UN + 6):
                if u < UN:
                    j, g = unit(u)
                    b = j * G + g
                    act.wait_ge(qsub_done, u + 1)
                    q = qt[:, b:b + 2, :].rearrange("p b n -> p (b n)")
                    act.activation(q, q, ACT.Exp).then_inc(qexp_done, 1)
                if u >= 6:
                    copy_transposed(1, u - 6)

        @block.gpsimd
        def _(pool):
            pool.tensor_tensor(m.memv_b[:, :, :], m.memv[:, None, :].broadcast_to([128, B, 128]),
                               m.memmask[:, :, None].broadcast_to([128, B, 128]), ALU.mult).then_inc(memv_masked, 1)


def peripheral_convolution(nc, m, sem):
    ps = m.ps
    zt = m.tmpA
    T = m.big
    yt_ready = sem("cv_zt_ready")
    yt_copied = sem("cv_zt_copied")
    classes = sem("cv_classes")
    stored = sem("cv_stored")
    loaded = sem("cv_loaded")
    t_ready = sem("cv_t_ready")
    t_copied_a = sem("cv_t_copied_a")
    t_copied_v = sem("cv_t_copied_v")
    turned = sem("cv_turned")
    turned_copied = sem("cv_turned_copied")
    out_ready = sem("cv_out_ready")
    out_copied = sem("cv_out_copied")
    out_stored = sem("cv_out_stored")
    out_loaded = sem("cv_out_loaded")
    added = sem("cv_added")
    NT = H * S

    with nc.Block() as block:
        @block.sync
        def _(sp):
            sp.wait_ge(classes, CLASSES)
            sp.dma_start(m.scratch_w, m.wclass[:, :, :]).then_inc(stored, 16)
            sp.wait_ge(stored, 16)
            for half, dst in enumerate((m.bl, m.br)):
                for q in range(8):
                    src = bass.AP(tensor=m.scratch_w.tensor, offset=m.scratch_w.offset + (q + half) * (2 * R + 1),
                                  ap=[[1, W], [CLASSES * (2 * R + 1), C], [1, W]])
                    sp.dma_start(dst[16 * q:16 * q + 16, :, :], src).then_inc(loaded, 16)
            for h in range(2):
                sp.wait_ge(out_copied, 4 * (h + 1))
                for cc in range(4):
                    dst = m.scratch_x.rearrange("b (ci cc) n -> cc b ci n", cc=4)[cc]
                    sp.dma_start(dst[:, 4 * h:4 * h + 4, :], m.co[32 * cc:32 * cc + 32, 4 * h:4 * h + 4, :])\
                        .then_inc(out_stored, 16)
            sp.wait_ge(out_stored, 8 * 16)
            for j in range(J):
                sp.dma_start(m.tmpB[32 * j:32 * j + 32, :].rearrange("c (g n) -> c g n", g=G),
                             m.scratch_x.rearrange("(g j) c n -> j c g n", j=J)[j]).then_inc(out_loaded, 16)

        @block.gpsimd
        def _(pool):
            wc = m.wcomp[:, :].rearrange("c (a b) -> c a b", a=CONV_P)
            for q, (lo, hi) in enumerate(CLASS_SPANS):
                n = hi - lo + 1
                pool.tensor_copy(m.wclass[:, :, R - hi:R - lo + 1],
                                 wc[:, CLASS0:CLASS0 + CLASSES, CLASS0 + q:CLASS0 + q + 1]
                                 .broadcast_to([C, CLASSES, n])).then_inc(classes, 1)

        @block.tensor
        def _(pe):
            for q in range(NCH):
                for i in range(4):
                    t = 4 * q + i
                    mm = pe.transpose(ps[:, q, i * 128:(i + 1) * 128], m.z[:, t * 128:(t + 1) * 128], m.ident[:, :])
                mm.then_inc(yt_ready, 1)
            for i, t in enumerate((m.kmat_rev, m.relt)):
                pe.matmul(ps[:, 4 + i, :], m.exchange[:, :], t[:, :, :].rearrange("p s n -> p (s n)"),
                          start=True, stop=True).then_inc(turned, 1)
            pe.wait_ge(loaded, 16 * 16)
            for w in range(NT):
                y, s = divmod(w, S)
                if w < 4:
                    pe.wait_ge(yt_copied, w + 1)
                else:
                    pe.wait_ge(t_copied_a if w % 2 == 0 else t_copied_v, (w - 4) // 2 + 1)
                onehot, weights = ((m.ol, m.bl), (m.orr, m.br))[s]
                pe.matmul(ps[:, w % 4, :], onehot[:, (R - y) * W:(R - y + 8) * W],
                          weights[:, :, :].rearrange("p c x -> p (c x)"), start=True, stop=True).then_inc(t_ready, 1)
            pe.wait_ge(t_copied_a, NT // 2)
            pe.wait_ge(t_copied_v, NT // 2)
            pe.wait_ge(turned_copied, 2)
            for ci in range(C // 4):
                for cc in range(4):
                    c = 4 * ci + cc
                    o = ps[32 * cc:32 * cc + 32, (4 + ci) % 8, 0:N]
                    for s in range(S):
                        lhsT = zt[:, s * G * 128 + c:(s + 1) * G * 128:C]
                        rhs = T[:, s, :, :].rearrange("p y (c x) -> p y c x", c=C)[:, :, c, :]
                        pe.matmul(o, lhsT, rhs, start=(s == 0), stop=False)
                        mm = pe.matmul(o, lhsT, m.kmat[:, s, :], start=False, stop=(s == S - 1))
                mm.then_inc(out_ready, 1)

        @block.scalar
        def _(act):
            for q in range(NCH):
                act.wait_ge(yt_ready, q + 1)
                act.activation(zt[:, :].rearrange("p (s g x) -> p g s x", s=S, g=G)[:, 2 * q:2 * q + 2],
                               ps[:, q, :].rearrange("p (g s x) -> p g s x", g=2, s=S),
                               ACT.Copy).then_inc(yt_copied, 1)
            for w in range(0, NT, 2):
                y, s = divmod(w, S)
                act.wait_ge(t_ready, w + 1)
                act.activation(T[:, s, y, :], ps[:, w % 4, :], ACT.Copy).then_inc(t_copied_a, 1)
            for ci in range(C // 4):
                act.wait_ge(out_ready, ci + 1)
                act.activation(m.co[:, ci, :], ps[:, (4 + ci) % 8, 0:N],
                               ACT.Copy).then_inc(out_copied, 1)

        @block.vector
        def _(dve):
            for i, t in enumerate((m.kmat, m.relt)):
                dve.wait_ge(turned, i + 1)
                dve.tensor_copy(t[:, :, :].rearrange("p s n -> p (s n)"), ps[:, 4 + i, :]).then_inc(turned_copied, 1)
            for w in range(1, NT, 2):
                y, s = divmod(w, S)
                dve.wait_ge(t_ready, w + 1)
                dve.tensor_copy(T[:, s, y, :], ps[:, w % 4, :]).then_inc(t_copied_v, 1)
            dve.wait_ge(out_loaded, 16 * J)
            for k in range(NCH):
                c = slice(k * CH, (k + 1) * CH)
                dve.tensor_tensor(m.x[:, c], m.x[:, c], m.tmpB[:, c], ALU.add).then_inc(added, 1)


def linear_transformer(nc, m, sem):
    ps = m.ps
    zt = m.tmpA
    zt_ready = sem("lt_zt_ready")
    zt_copied = sem("lt_zt_copied")
    g_ready = sem("lt_g_ready")
    g_masked = sem("lt_g_masked")
    p_ready = sem("lt_p_ready")
    p_copied = sem("lt_p_copied")
    m_ready = sem("lt_m_ready")
    a_made = sem("lt_a_made")
    abd_made = sem("lt_abd_made")
    r_ready = sem("lt_r_ready")
    r_copied = sem("lt_r_copied")
    wt_ready = sem("lt_wt_ready")
    wt_copied = sem("lt_wt_copied")
    wbd_made = sem("lt_wbd_made")
    w_ready = sem("lt_w_ready")
    w_copied = sem("lt_w_copied")
    out_ready = sem("lt_out_ready")
    added = sem("lt_added")
    gbd, abd = m.gbd, m.abd

    def spread(dve, dst, src, done):
        for j in range(J):
            ins = dve.tensor_tensor(dst[:, :, 32 * j:32 * j + 32], src,
                                    m.blkone[:, None, 32 * j:32 * j + 32].broadcast_to([128, G, 32]), ALU.mult)
            ins.then_inc(done, 1)

    with nc.Block() as block:
        @block.tensor
        def _(pe):
            for q in range(NCH):
                for i in range(4):
                    t = 4 * q + i
                    mm = pe.transpose(ps[:, q, i * 128:(i + 1) * 128], m.z[:, t * 128:(t + 1) * 128], m.ident[:, :])
                mm.then_inc(zt_ready, 1)
            for g in range(G):
                if g % 2 == 0:
                    pe.wait_ge(zt_copied, g // 2 + 1)
                for s in range(S):
                    t = 2 * g + s
                    mm = pe.matmul(ps[:, 4 + g // 4, (g % 4) * 128:(g % 4) * 128 + 128],
                                   zt[:, t * 128:(t + 1) * 128], zt[:, t * 128:(t + 1) * 128],
                                   start=(s == 0), stop=(s == S - 1))
            mm.then_inc(g_ready, 1)
            for L in range(LAYERS):
                pe.wait_ge(g_masked, 2 if L == 0 else 2 + J * L)
                for g in range(G):
                    mm = pe.matmul(ps[:, g // 2, (g % 2) * 256:(g % 2) * 256 + 256], gbd[:, g, :],
                                   m.vt4[:, L * 256:(L + 1) * 256], start=True, stop=True)
                    if g % 2:
                        mm.then_inc(p_ready, 1)
                pe.wait_ge(p_copied, NCH * (L + 1))
                for h in range(ZHEADS):
                    mm = pe.matmul(ps[:, 4, 0:256], m.qbd[:, L, h, :],
                                   m.pmat[:, :, h * 32:(h + 1) * 32], start=(h == 0), stop=(h == ZHEADS - 1))
                mm.then_inc(m_ready, 1)
                pe.wait_ge(abd_made, J * (L + 1))
                if L > 0:
                    pe.wait_ge(wt_copied, L)
                if L < LAYERS - 1:
                    for g in range(G):
                        mm = pe.matmul(ps[:, 5, g * 32:(g + 1) * 32], gbd[:, g, :], m.amat[:, g, :],
                                       start=True, stop=True)
                    mm.then_inc(r_ready, 1)
                for g in range(G):
                    mm = pe.matmul(ps[:, 6, g * 32:(g + 1) * 32], abd[:, g, :], m.wt[:, g, :],
                                   start=True, stop=True)
                mm.then_inc(wt_ready, 1)
                if L < LAYERS - 1:
                    pe.wait_ge(r_copied, L + 1)
                    for g in range(G):
                        mm = pe.matmul(ps[:, 7, g * 32:(g + 1) * 32], abd[:, g, :], m.rmat[:, g, :],
                                       start=True, stop=True)
                    mm.then_inc(g_ready, 1)
            pe.wait_ge(wbd_made, J)
            for g in range(G):
                mm = pe.transpose(ps[:, g // 4, (g % 4) * 128:(g % 4) * 128 + 128], abd[:, g, :], m.ident[:, :])
            mm.then_inc(w_ready, 1)
            pe.wait_ge(w_copied, 2)
            for k in range(NCH):
                for h in range(2):
                    g = 2 * k + h
                    mm = pe.matmul(ps[:, 2 + k, h * N:(h + 1) * N], gbd[:, g, :], m.z[:, g * N:(g + 1) * N],
                                   start=True, stop=True)
                mm.then_inc(out_ready, 1)

        @block.vector
        def _(dve):
            dve.wait_ge(g_ready, 1)
            for h in range(2):
                dve.tensor_tensor(gbd[:, 4 * h:4 * h + 4, :], ps[:, 4 + h, :].rearrange("p (g d) -> p g d", g=4),
                                  m.blkone[:, None, :].broadcast_to([128, 4, 128]), ALU.mult).then_inc(g_masked, 1)
            for L in range(LAYERS):
                dve.wait_ge(m_ready, L + 1)
                if L > 0:
                    dve.wait_ge(wt_ready, L)
                    dve.wait_ge(g_ready, L + 1)
                    dve.wait_ge(g_masked, 2 + J * L)
                dve.scalar_tensor_tensor(m.amat[:, :, :], ps[:, 4, 0:256].rearrange("p (g d) -> p g d", g=G),
                                         1.0 / (N * ZHEADS), m.ident32[:, None, :].broadcast_to([128, G, 32]),
                                         ALU.mult, ALU.add).then_inc(a_made, 1)
                dve.wait_ge(a_made, L + 1)
                spread(dve, abd, m.amat[:, :, :], abd_made)
                if L < LAYERS - 1:
                    dve.wait_ge(g_ready, L + 2)
                    spread(dve, gbd, ps[:, 7, 0:256].rearrange("p (g d) -> p g d", g=G), g_masked)
            dve.wait_ge(wt_copied, LAYERS)
            spread(dve, abd, m.wt[:, :, :], wbd_made)
            dve.wait_ge(w_ready, 1)
            for h in range(2):
                dve.tensor_copy(gbd[:, 4 * h:4 * h + 4, :].rearrange("p g d -> p (g d)"),
                                ps[:, h, :]).then_inc(w_copied, 1)
            for k in range(NCH):
                c = slice(k * CH, (k + 1) * CH)
                dve.wait_ge(out_ready, k + 1)
                dve.tensor_tensor(m.x[:, c], m.x[:, c], ps[:, 2 + k, :], ALU.add).then_inc(added, 1)

        @block.scalar
        def _(act):
            for q in range(NCH):
                act.wait_ge(zt_ready, q + 1)
                act.activation(zt[:, q * CH:(q + 1) * CH], ps[:, q, :], ACT.Copy).then_inc(zt_copied, 1)
            for L in range(LAYERS):
                for q in range(NCH):
                    act.wait_ge(p_ready, NCH * L + q + 1)
                    act.activation(m.pmat[:, 2 * q:2 * q + 2, :].rearrange("p g d -> p (g d)"), ps[:, q, :],
                                   ACT.Copy).then_inc(p_copied, 1)
                if L < LAYERS - 1:
                    act.wait_ge(r_ready, L + 1)
                    act.activation(m.rmat[:, :, :].rearrange("p g d -> p (g d)"), ps[:, 5, 0:256],
                                   ACT.Copy).then_inc(r_copied, 1)
                act.wait_ge(wt_ready, L + 1)
                act.activation(m.wt[:, :, :].rearrange("p g d -> p (g d)"), ps[:, 6, 0:256],
                               ACT.Copy).then_inc(wt_copied, 1)


def mixture_of_experts(nc, m, sem):
    ps = m.ps
    z = m.z
    NT = G * S * J
    logits_ready = sem("me_logits_ready")
    steps = sem("me_steps")
    exp_done = sem("me_exp_done")
    parts_made = sem("me_parts_made")
    gt_ready = sem("me_gt_ready")
    gt_copied = sem("me_gt_copied")
    gate_ready = sem("me_gate_ready")
    gated = sem("me_gated")
    out_ready = sem("me_out_ready")
    added = sem("me_added")

    def lots(t):
        return t.rearrange("p (t e) -> p t e", e=E)

    with nc.Block() as block:
        @block.tensor
        def _(pe):
            for t in range(G * S):
                mm = pe.matmul(ps[:, 0, t * 32:(t + 1) * 32], z[:, t * 128:(t + 1) * 128], m.rwbd[:, :],
                               start=True, stop=True)
            mm.then_inc(logits_ready, 1)
            pe.wait_ge(parts_made, 4)
            gt_ps = ps[:, 1:3, :].rearrange("p a n -> p (a n)").bitcast(BF16)
            for t in range(G * S):
                mm = pe.transpose(gt_ps[:, t * 128:(t + 1) * 128], m.gparts[:, t, :, :].rearrange("p a e -> p (a e)"),
                                  m.identb[:, :])
                if t % 8 == 7:
                    mm.then_inc(gt_ready, 1)
            pe.wait_ge(gt_copied, 2)

            def gate(w):
                e, k = w % E, w // E
                if w >= 3:
                    pe.wait_ge(gated, w - 2)
                pe.matmul(ps[:, 3 + w % 3, :], m.sele[:, e, :],
                          m.gt[:, k * CH:(k + 1) * CH], start=True, stop=True).then_inc(gate_ready, 1)

            gate(0)
            gate(1)
            for w in range(E * NCH):
                e, k = w % E, w // E
                if w + 2 < E * NCH:
                    gate(w + 2)
                if e == 0:
                    if k >= 2:
                        pe.wait_ge(added, k - 1)
                    for i in range(3):
                        pe.matmul(ps[:, 6 + k % 2, :], m.ebbd[:, i, :], m.gt[:, k * CH:(k + 1) * CH],
                                  start=(i == 0), stop=False)
                pe.wait_ge(gated, w + 1)
                mm = pe.matmul(ps[:, 6 + k % 2, :], m.ewbd[:, e, :], m.gz[:, w % 3, :], start=False, stop=(e == E - 1))
                mm.then_inc(out_ready, 1)

        def add(dve, k):
            c = slice(k * CH, (k + 1) * CH)
            dve.wait_ge(out_ready, E * (k + 1))
            dve.tensor_tensor(m.x[:, c], m.x[:, c], ps[:, 6 + k % 2, :], ALU.add).then_inc(added, 1)

        @block.vector
        def _(dve):
            n = 0

            def step(ins):
                nonlocal n
                ins.then_inc(steps, 1)
                n += 1
                dve.wait_ge(steps, n)

            l, k, one, sel = (lots(t) for t in (m.lg, m.key, m.one1, m.sel2))
            bc = [128, NT, E]
            st = m.stat
            dve.wait_ge(logits_ready, 1)
            step(dve.tensor_tensor(l, lots(ps[:, 0, :]), m.rb[:, None, :].broadcast_to(bc), ALU.add))
            step(dve.tensor_reduce(st[:, 0, :], l, AXX, ALU.max))
            mx = st[:, 0, :].unsqueeze(2).broadcast_to(bc)
            rank = m.rank[:, None, :].broadcast_to(bc)
            step(dve.tensor_tensor(k, l, mx, ALU.is_ge))
            step(dve.tensor_tensor(k, k, rank, ALU.mult))
            step(dve.tensor_reduce(st[:, 1, :], k, AXX, ALU.max))
            step(dve.tensor_tensor(one, k, st[:, 1, :].unsqueeze(2).broadcast_to(bc), ALU.is_equal))
            step(dve.tensor_scalar(sel, one, -1.0, 1.0, ALU.mult, ALU.add))
            step(dve.tensor_tensor(sel, sel, l, ALU.mult))
            step(dve.scalar_tensor_tensor(k, one, -3.0e38, sel, ALU.mult, ALU.add))
            step(dve.tensor_reduce(st[:, 3, :], k, AXX, ALU.max))
            step(dve.tensor_tensor(k, k, st[:, 3, :].unsqueeze(2).broadcast_to(bc), ALU.is_ge))
            step(dve.tensor_tensor(k, k, rank, ALU.mult))
            step(dve.tensor_reduce(st[:, 1, :], k, AXX, ALU.max))
            step(dve.tensor_tensor(sel, k, st[:, 1, :].unsqueeze(2).broadcast_to(bc), ALU.is_equal))
            step(dve.tensor_tensor(sel, sel, one, ALU.add))
            step(dve.tensor_tensor(l, l, mx, ALU.subtract))
            dve.wait_ge(exp_done, 1)
            step(dve.tensor_tensor(sel, sel, l, ALU.mult))
            step(dve.tensor_reduce(st[:, 1, :], sel, AXX, ALU.add))
            step(dve.reciprocal(st[:, 2, :], st[:, 1, :]))
            step(dve.tensor_tensor(sel, sel, st[:, 2, :].unsqueeze(2).broadcast_to(bc), ALU.mult))
            g4 = m.sel2[:, :].rearrange("p (t e) -> p t e", t=G * S)
            r4 = m.key[:, :].rearrange("p (t e) -> p t e", t=G * S)
            dve.tensor_copy(m.gparts[:, :, 0, :], g4).then_inc(parts_made, 1)
            dve.wait_ge(parts_made, 2)
            step(dve.tensor_tensor(r4, g4, m.gparts[:, :, 0, :], ALU.subtract))
            dve.tensor_copy(m.gparts[:, :, 1, :], r4).then_inc(parts_made, 1)
            dve.wait_ge(parts_made, 3)
            step(dve.tensor_tensor(r4, r4, m.gparts[:, :, 1, :], ALU.subtract))
            dve.tensor_copy(m.gparts[:, :, 2, :], r4).then_inc(parts_made, 1)
            for w in range(E * NCH):
                kk = w // E
                dve.wait_ge(gate_ready, w + 1)
                if w >= 3:
                    dve.wait_ge(out_ready, w - 2)
                dve.tensor_tensor(m.gz[:, w % 3, :], z[:, kk * CH:(kk + 1) * CH], ps[:, 3 + w % 3, :],
                                  ALU.mult).then_inc(gated, 1)
                if w % E == 3 and kk >= 1:
                    add(dve, kk - 1)
            add(dve, NCH - 1)

        @block.scalar
        def _(act):
            act.wait_ge(steps, 16)
            act.activation(m.lg[:, :], m.lg[:, :], ACT.Exp).then_inc(exp_done, 1)
            gt_ps = ps[:, 1:3, :].rearrange("p a n -> p (a n)").bitcast(BF16)
            for h in range(2):
                act.wait_ge(gt_ready, h + 1)
                act.activation(m.gt[:, h * 1024:(h + 1) * 1024], gt_ps[:, h * 1024:(h + 1) * 1024],
                               ACT.Copy).then_inc(gt_copied, 1)

        @block.gpsimd
        def _(pool):
            pool.memset(m.gparts[:, :, 3, :], 0.0).then_inc(parts_made, 1)


def squared_attention(nc, m, sem):
    ps = m.ps
    z = m.z
    vm = m.vm
    vtok = m.tmpA
    exact = [m.tmpB, m.rstd]
    projected = sem("sa_projected")
    silu_done = sem("sa_silu_done")
    cast_done = sem("sa_cast_done")
    split = sem("sa_split")
    stacked = sem("sa_stacked")
    sel_loaded = sem("sa_sel_loaded")
    sel_made = sem("sa_sel_made")
    arranged_ready = sem("sa_arranged_ready")
    arranged = [sem("sa_q_arranged"), sem("sa_k_arranged")]
    v_ready = sem("sa_v_ready")
    v_biased = sem("sa_v_biased")
    v_done = sem("sa_v_done")
    v_masked = sem("sa_v_masked")
    pos_ready = sem("sa_pos_ready")
    pos_copied = sem("sa_pos_copied")
    scores_ready = sem("sa_scores_ready")
    causal_done = sem("sa_causal_done")
    below_squared = sem("sa_below_squared")
    diag_squared = [sem("sa_diag_squared_v"), sem("sa_diag_squared_p")]
    act_done = sem("sa_act_done")
    pv_ready = sem("sa_pv_ready")
    pv_copied = sem("sa_pv_copied")
    order = [(g, j) for g in range(G) for j in range(J)]
    NU = B * AH // 2
    SLOTS = 6
    LAG = 4
    NPART = 3
    arrangement = [(k, j, hp, x) for k in range(NCH) for j in range(J) for hp in range(2) for x in range(2)]

    def arranged_to(w):
        k, j, hp, x = arrangement[w]
        b = j * G + 2 * k
        return m.qkt[:, x, hp, b:b + 2, :].rearrange("p b n -> p (b n)")

    def diagonal(u):
        return m.att[:, u % SLOTS, :, :].rearrange("p k (d n) -> p k d n", n=128)[:, :, 0::2, :]

    with nc.Block() as block:
        @block.sync
        def _(sp):
            sp.dma_start(m.selqk32[:, :], m.d_selqk).then_inc(sel_loaded, 16)
            for x in range(2):
                for p in range(NPART):
                    if p == 0:
                        sp.wait_ge(cast_done, NCH * (x + 1))
                    else:
                        sp.wait_ge(split, NCH * (3 * x + 2) if p == 1 else 3 * NCH * (x + 1))
                    for j in range(J):
                        sp.dma_start(m.qkstack[32 * p:32 * p + 32, x, j, :],
                                     m.qkparts[32 * j:32 * j + 32, x, p, :]).then_inc(stacked, 16)

        @block.tensor
        def _(pe):
            for x in range(2):
                for k in range(NCH):
                    pe.matmul(ps[:, NCH * x + k, :], m.wqkbd[:, x, :], z[:, k * CH:(k + 1) * CH],
                              start=True, stop=True).then_inc(projected, 1)
            for t in range(G * S):
                if t % 4 == 0:
                    pe.wait_ge(silu_done, NCH + t // 4 + 1)
                mm = pe.matmul(ps[:, 4 + t // 4, (t % 4) * 128:(t % 4) * 128 + 128], z[:, t * 128:(t + 1) * 128],
                               m.wvbd[:, :], start=True, stop=True)
                if t % 4 == 3:
                    mm.then_inc(v_ready, 1)
            pe.wait_ge(v_done, NCH)
            for g in range(G):
                for s in range(S):
                    mm = pe.matmul(ps[:, 4 + g // 2, (g % 2) * N:(g % 2) * N + N],
                                   vtok[:, (2 * g + s) * 128:(2 * g + s + 1) * 128], m.relt[:, s, :],
                                   start=(s == 0), stop=(s == S - 1))
                if g % 2:
                    mm.then_inc(pos_ready, 1)
            pe.wait_ge(sel_made, 1)
            pe.wait_ge(stacked, 16 * 2 * NPART * J)
            for w, (k, j, hp, x) in enumerate(arrangement):
                if w >= 4:
                    pe.wait_ge(arranged[x], (w - 4) // 2 + 1)
                pe.matmul(ps[:, w % 4, :], m.selqk[0:32 * NPART, x, hp, :],
                          m.qkstack[0:32 * NPART, x, j, k * CH:(k + 1) * CH],
                          start=True, stop=True).then_inc(arranged_ready, 1)

            def scores(u):
                g, j = order[u // 2]
                b = j * G + g
                if u == 2:
                    pe.wait_ge(pos_copied, NCH)
                if u >= 3:
                    pe.wait_ge(causal_done, u - 2)
                    pe.wait_ge(below_squared, u - 2)
                for s in range(S):
                    for k in range(2):
                        rows = slice(64 * k, 64 * k + 64)
                        mm = pe.matmul(ps[:, 2 * (u % 3) + k, s * N:N + s * 128],
                                       m.qkt[rows, 1, u % 2, b, s * 128:(s + 1) * 128],
                                       m.qkt[rows, 0, u % 2, b, s * 128:N], start=True, stop=True)
                mm.then_inc(scores_ready, 1)

            def values(u):
                g, j = order[u // 2]
                if u % (2 * J) == 0 and g >= 2:
                    pe.wait_ge(pv_copied, g - 1)
                pe.wait_ge(act_done, u + 1)
                rows = slice(32 * j, 32 * j + 32)
                for k in range(2):
                    h = 2 * (u % 2) + k
                    pe.matmul(ps[rows, 6 + g % 2, 0:N], vm[:, (2 * g) * J + j, h, :], m.att[:, u % SLOTS, k, 0:N],
                              start=(h == 0), stop=False)
                    mm = pe.matmul(ps[rows, 6 + g % 2, 128:N], vm[:, (2 * g + 1) * J + j, h, :],
                                   m.att[:, u % SLOTS, k, N:N + 128], start=False, stop=(h == AH - 1))
                mm.then_inc(pv_ready, 1)

            pe.wait_ge(arranged[0], len(arrangement) // 2)
            pe.wait_ge(arranged[1], len(arrangement) // 2)
            for u in range(NU + LAG):
                if u < NU:
                    scores(u)
                if u == LAG:
                    pe.wait_ge(v_masked, 1)
                if u >= LAG:
                    values(u - LAG)

        def copy_out(dve, g):
            dve.wait_ge(pv_ready, 2 * J * (g + 1))
            dve.tensor_copy(m.sa[:, g * N:(g + 1) * N], ps[:, 6 + g % 2, 0:N]).then_inc(pv_copied, 1)

        @block.vector
        def _(dve):
            for x in range(2):
                for k in range(NCH):
                    c = slice(k * CH, (k + 1) * CH)
                    n = 3 * NCH * x
                    dve.wait_ge(cast_done, NCH * x + k + 1)
                    dve.tensor_tensor(exact[x][:, c], exact[x][:, c], m.qkparts[:, x, 0, c],
                                      ALU.subtract).then_inc(split, 1)
                    dve.wait_ge(split, n + 2 * k + 1)
                    dve.tensor_copy(m.qkparts[:, x, 1, c], exact[x][:, c]).then_inc(split, 1)
                for k in range(NCH):
                    c = slice(k * CH, (k + 1) * CH)
                    dve.wait_ge(split, n + 2 * k + 2)
                    dve.tensor_tensor(m.qkparts[:, x, 2, c], exact[x][:, c], m.qkparts[:, x, 1, c],
                                      ALU.subtract).then_inc(split, 1)
            for k in range(NCH):
                dve.wait_ge(v_ready, k + 1)
                dve.tensor_tensor(vtok[:, k * CH:(k + 1) * CH].rearrange("p (a d) -> p a d", d=32),
                                  ps[:, 4 + k, :].rearrange("p (a d) -> p a d", d=32),
                                  m.bv[:, None, :].broadcast_to([128, 16, 32]), ALU.add).then_inc(v_biased, 1)
            for k in range(NCH):
                dve.wait_ge(pos_ready, k + 1)
                dve.tensor_copy(m.pa[:, k * CH:(k + 1) * CH], ps[:, 4 + k, :]).then_inc(pos_copied, 1)
            for w in range(0, len(arrangement), 2):
                dve.wait_ge(arranged_ready, w + 1)
                dve.tensor_copy(arranged_to(w), ps[:, w % 4, :]).then_inc(arranged[0], 1)
            dve.wait_ge(arranged_ready, len(arrangement))
            for u in range(NU):
                dve.wait_ge(scores_ready, u + 1)
                if u >= SLOTS:
                    dve.wait_ge(pv_ready, u - SLOTS + 1)
                dve.tensor_tensor(diagonal(u),
                                  ps[:, 2 * (u % 3):2 * (u % 3) + 2, :]
                                  .rearrange("p k (d n) -> p k d n", n=128)[:, :, 0:3:2, :],
                                  m.causal[:, None, None, :].broadcast_to([128, 2, 2, 128]),
                                  ALU.mult).then_inc(causal_done, 1)
                if u % 2:
                    dve.wait_ge(causal_done, u)
                    dve.tensor_tensor(diagonal(u - 1), diagonal(u - 1), diagonal(u - 1),
                                      ALU.mult).then_inc(diag_squared[0], 1)
                if u % 8 == 7 and u > 8:
                    copy_out(dve, u // 8 - 1)
            copy_out(dve, G - 1)

        @block.scalar
        def _(act):
            for x in range(2):
                for k in range(NCH):
                    c = slice(k * CH, (k + 1) * CH)
                    act.wait_ge(projected, NCH * x + k + 1)
                    act.activation(exact[x][:, c], ps[:, NCH * x + k, :], ACT.Silu,
                                   bias=m.bqk[:, x:x + 1]).then_inc(silu_done, 1)
                    act.wait_ge(silu_done, NCH * x + k + 1)
                    act.activation(m.qkparts[:, x, 0, c], exact[x][:, c], ACT.Copy).then_inc(cast_done, 1)
            for k in range(NCH):
                c = slice(k * CH, (k + 1) * CH)
                act.wait_ge(v_biased, k + 1)
                act.activation(vtok[:, c], vtok[:, c], ACT.Silu).then_inc(v_done, 1)
            for w in range(1, len(arrangement), 2):
                act.wait_ge(arranged_ready, w + 1)
                act.activation(arranged_to(w), ps[:, w % 4, :], ACT.Copy).then_inc(arranged[1], 1)

            def silu(u):
                a = m.att[:, u % SLOTS, :, :].rearrange("p k n -> p (k n)")
                act.wait_ge(diag_squared[u % 2], u // 2 + 1)
                act.wait_ge(below_squared, u + 1)
                act.activation(a, a, ACT.Silu, scale=1.0 / AHD).then_inc(act_done, 1)

            for u in range(NU):
                act.wait_ge(causal_done, u + 1)
                act.activation(m.att[:, u % SLOTS, :, 128:N], ps[:, 2 * (u % 3):2 * (u % 3) + 2, 128:N],
                               ACT.Square).then_inc(below_squared, 1)
                if u >= 2:
                    silu(u - 2)
            silu(NU - 2)
            silu(NU - 1)

        @block.gpsimd
        def _(pool):
            pool.wait_ge(sel_loaded, 16)
            pool.tensor_copy(m.selqk[0:32 * NPART, :, :, :].rearrange("p x a b -> p (x a b)"),
                             m.selqk32[:, :]).then_inc(sel_made, 1)
            pool.wait_ge(v_done, NCH)
            pool.wait_ge(stacked, 16 * 2 * NPART * J)
            pool.tensor_tensor(vm[:, :, :, :], vtok[:, :].rearrange("p (t d) -> p t d", d=32).unsqueeze(2)
                               .broadcast_to([128, G * S * J, AH, 32]),
                               m.headmask[:, None, :, :].broadcast_to([128, G * S * J, AH, 32]),
                               ALU.mult).then_inc(v_masked, 1)
            for u in range(1, NU, 2):
                pool.wait_ge(causal_done, u + 1)
                pool.tensor_tensor(diagonal(u), diagonal(u), diagonal(u), ALU.mult).then_inc(diag_squared[1], 1)

    gamma = [(m.gam[:, i:i + 1], m.bet[:, i:i + 1]) for i in range(2)]
    normalise_tokens(nc, m, sem, "sa_norm", [m.sa, m.pa], [m.sa, m.pa], EPS_A, m.blkmean64, gamma)

    u_ready = sem("sa_u_ready")
    gated = sem("sa_gated")
    f_ready = sem("sa_f_ready")
    relu_done = sem("sa_relu_done")
    summed = sem("sa_summed")
    with nc.Block() as block:
        @block.tensor
        def _(pe):
            for i in range(2):
                for k in range(NCH):
                    pe.matmul(ps[:, 4 * i + k, :], m.wubd[:, i, :], z[:, k * CH:(k + 1) * CH],
                              start=True, stop=True).then_inc(u_ready, 1)
            for k in range(NCH):
                pe.wait_ge(gated, NCH + k + 1)
                for i, part in enumerate((m.sa, m.pa)):
                    mm = pe.matmul(ps[:, k, :], m.wfbd[:, i, :], part[:, k * CH:(k + 1) * CH],
                                   start=(i == 0), stop=(i == 1))
                mm.then_inc(f_ready, 1)

        @block.vector
        def _(dve):
            for i, part in enumerate((m.sa, m.pa)):
                for k in range(NCH):
                    c = slice(k * CH, (k + 1) * CH)
                    dve.wait_ge(u_ready, NCH * i + k + 1)
                    dve.scalar_tensor_tensor(part[:, c], ps[:, 4 * i + k, :], m.bu[:, i:i + 1], part[:, c],
                                             ALU.add, ALU.mult).then_inc(gated, 1)
            for k in range(NCH):
                c = slice(k * CH, (k + 1) * CH)
                dve.tensor_tensor(m.x[:, c], m.x[:, c], z[:, c], ALU.add).then_inc(summed, 1)
            for k in range(NCH):
                c = slice(k * CH, (k + 1) * CH)
                dve.wait_ge(relu_done, k + 1)
                dve.wait_ge(summed, k + 1)
                dve.tensor_tensor(m.x[:, c], m.x[:, c], m.tmpB[:, c], ALU.add).then_inc(summed, 1)

        @block.scalar
        def _(act):
            for k in range(NCH):
                act.wait_ge(f_ready, k + 1)
                act.activation(m.tmpB[:, k * CH:(k + 1) * CH], ps[:, k, :], ACT.Relu,
                               bias=m.bf[:, 0:1]).then_inc(relu_done, 1)


def routed_blocks(nc, m, sem):
    ps = m.ps
    h = m.h
    TOP = 64
    ut, htok, y0 = m.tmpA, m.tmpB, m.sa
    NU = 2 * G
    go = {e: sem("rb_go_" + e) for e in ("sp", "act", "pe")}
    go_dve = sem("rb_go_dve")
    settled = sem("rb_settled")
    probed = sem("rb_probed")
    loaded = sem("rb_loaded")
    NLOAD = 5
    mats_ready = sem("rb_mats_ready")
    mats_masked = sem("rb_mats_masked")
    u_ready = sem("rb_u_ready")
    u_copied = sem("rb_u_copied")
    ht_ready = sem("rb_ht_ready")
    ht_copied = sem("rb_ht_copied")
    s_ready = sem("rb_s_ready")
    max_done = sem("rb_max_done")
    shift = sem("rb_shift")
    shift_ready = sem("rb_shift_ready")
    shift_copied = sem("rb_shift_copied")
    st_ready = sem("rb_st_ready")
    exp_done = sem("rb_exp_done")
    pv_ready = sem("rb_pv_ready")
    inv_done = sem("rb_inv_done")
    y0_done = sem("rb_y0_done")
    y_ready = sem("rb_y_ready")
    y_copied = sem("rb_y_copied")
    z1_ready = sem("rb_z1_ready")
    relu_a = sem("rb_relu_a")
    relu_v = sem("rb_relu_v")
    z2_ready = sem("rb_z2_ready")
    z2_copied = sem("rb_z2_copied")
    ctl = sem("rb_ctl")
    added = sem("rb_added")
    per_block = [loaded, mats_ready, mats_masked, u_ready, u_copied, ht_ready, ht_copied, s_ready, max_done, shift,
                 shift_ready, shift_copied, st_ready, exp_done, pv_ready, inv_done, y0_done, y_ready, y_copied,
                 z1_ready, relu_a, relu_v, z2_ready, z2_copied]

    def state(eng, go_sem, regs):
        eng.wait_ge(go_sem, 1)
        eng.reg_load(regs, m.state[0:1, 0:4])
        eng.sem_clear(go_sem)

    def registers(eng, name):
        return [eng.alloc_register(f"{name}_{r}") for r in ("step", "op", "attends", "feeds")]

    with nc.Block() as block:
        @block.sync
        def _(sp):
            regs = registers(sp, "sp")
            state(sp, go["sp"], regs)
            with sp.While(lambda: sp.snap(regs[0]) < NB):
                at = sp.snap(regs[0], min_val=0, max_val=NB - 1) * NOPS + sp.snap(regs[1], min_val=0, max_val=NOPS - 1)
                at = sp.snap(at, min_val=0, max_val=NB * NOPS - 1)

                def row(t):
                    return t[bass.ds(at, 1)]
                sp.dma_start(m.wsm[:, :, :].rearrange("d k (j c) -> d k j c", j=J),
                             row(m.d_small)[0].rearrange("d (k c) -> d k c", k=4)[:, :, None, :]
                             .broadcast_to([C, 4, J, C])).then_inc(loaded, 16)
                sp.dma_start(m.w1[:, :], row(m.d_w1).broadcast_to([J, C, HID])).then_inc(loaded, 16)
                sp.dma_start(m.w2f[:, :], row(m.d_w2)[0]).then_inc(loaded, 16)
                sp.dma_start(m.b1[:, :], row(m.d_b1)[0]).then_inc(loaded, 16)
                sp.dma_start(m.b2[:, :], row(m.d_b2).broadcast_to([J, C, 1])).then_inc(loaded, 16)
                state(sp, go["sp"], regs)

        @block.tensor
        def _(pe):
            regs = registers(pe, "pe")

            def probe():
                pe.wait_ge(settled, 1)
                pe.transpose(ps[0:1, 0, 0:C], m.hcol[:, 0:1], m.ident[0:C, 0:C]).then_inc(probed, 1)
                pe.sem_clear(settled)

            def attention():
                pe.wait_ge(loaded, 16 * NLOAD)
                for i, (a, b) in enumerate(((0, 1), (2, 3))):
                    mm = pe.matmul(ps[:, i, 0:128], m.wsm[:, a, :], m.wsm[:, b, :],
                                   start=True, stop=True)
                mm.then_inc(mats_ready, 1)
                for q in range(NCH):
                    if q < 2:
                        bank = 2 + q
                    else:
                        bank = q - 2
                        pe.wait_ge(mats_masked, 2)
                    for i in range(4):
                        t = 4 * bank + i
                        mm = pe.transpose(ps[:, bank, i * 128:(i + 1) * 128], h[:, t * 128:(t + 1) * 128], m.ident[:, :])
                    mm.then_inc(ht_ready, 1)
                for k in range(NCH):
                    pe.matmul(ps[:, 4 + k, :], m.sabd[:, :], h[:, k * CH:(k + 1) * CH],
                              start=True, stop=True).then_inc(u_ready, 1)
                for g in range(G):
                    p = g % 2
                    if g == 0:
                        pe.wait_ge(ht_copied, NCH)
                        pe.wait_ge(u_copied, NCH)
                    if g >= 2:
                        pe.wait_ge(max_done, g - 1)
                    for s in range(S):
                        for j in range(J):
                            rows = slice(32 * j, 32 * j + 32)
                            mm = pe.matmul(ps[:, 4 * p + j, s * N:(s + 1) * N],
                                           ut[rows, g * N + s * 128:g * N + (s + 1) * 128],
                                           h[rows, g * N:(g + 1) * N], start=True, stop=True)
                    mm.then_inc(s_ready, 1)
                pe.wait_ge(shift, 6)
                tp = ps[:, 0, 0:128].bitcast(BF16)
                for s in range(S):
                    mm = pe.transpose(tp[:, s * 128:(s + 1) * 128], m.mparts[:, s, :, :].rearrange("p a b -> p (a b)"),
                                      m.identb[:, :])
                mm.then_inc(shift_ready, 1)
                pe.wait_ge(shift_copied, 1)

                def scores(u):
                    g, jp = divmod(u, 2)
                    if u >= 3:
                        pe.wait_ge(exp_done, u - 2)
                    for s in range(S):
                        for i in range(2):
                            j = 2 * jp + i
                            rows = slice(32 * j, 32 * j + 32)
                            o = ps[:, 2 * (u % 3) + i, s * N:(s + 1) * N]
                            pe.matmul(o, h[rows, g * N + s * 128:g * N + (s + 1) * 128], ut[rows, g * N:(g + 1) * N],
                                      start=True, stop=False)
                            b = g * J + j
                            mm = pe.matmul(o, m.selb[:, b:b + 1].broadcast_to([128, 128]), m.mt[:, :],
                                           start=False, stop=True)
                    mm.then_inc(st_ready, 1)

                def values(u):
                    g, jp = divmod(u, 2)
                    if jp == 0 and g >= 2:
                        pe.wait_ge(y0_done, g - 1)
                    pe.wait_ge(exp_done, u + 1)
                    for part in range(2):
                        for i in range(2):
                            j = 2 * jp + i
                            rows = slice(32 * j, 32 * j + 32)
                            for s in range(S):
                                t = 2 * g + s
                                lhsT = htok[:, t * 128 + 32 * j:t * 128 + 32 * j + 32] if part == 0 else m.ones32[:, :]
                                mm = pe.matmul(ps[rows, 6 + g % 2, part * N:(part + 1) * N], lhsT,
                                               m.ex[:, u % 3, (2 * i + s) * N:(2 * i + s + 1) * N],
                                               start=(s == 0), stop=(s == S - 1))
                    mm.then_inc(pv_ready, 1)

                scores(0)
                scores(1)
                for u in range(NU):
                    if u + 2 < NU:
                        scores(u + 2)
                    values(u)
                for k in range(NCH):
                    pe.wait_ge(y0_done, 2 * (k + 1))
                    pe.matmul(ps[:, k, :], m.vobd[:, :], y0[:, k * CH:(k + 1) * CH],
                              start=True, stop=True).then_inc(y_ready, 1)
                pe.wait_ge(y_copied, NCH)

            def feed_forward():
                pe.wait_ge(loaded, 16 * NLOAD)

                def up(w):
                    k, j = divmod(w, J)
                    rows = slice(32 * j, 32 * j + 32)
                    if w >= 6:
                        pe.wait_ge(relu_a if w % 2 == 0 else relu_v, (w - 6) // 2 + 1)
                    pe.matmul(ps[:, w % 6, :], m.w1[rows, :], h[rows, k * CH:(k + 1) * CH],
                              start=True, stop=True).then_inc(z1_ready, 1)

                for w in range(4):
                    up(w)
                for w in range(J * NCH):
                    k, j = divmod(w, J)
                    if w + 4 < J * NCH:
                        up(w + 4)
                    if j == 0 and k >= 2:
                        pe.wait_ge(z2_copied, k - 1)
                    pe.wait_ge(relu_a if w % 2 == 0 else relu_v, w // 2 + 1)
                    mm = pe.matmul(ps[32 * j:32 * j + 32, 6 + k % 2, :], m.w2f[:, :], m.z1[:, w % 6, :],
                                   start=True, stop=True)
                    if j == J - 1:
                        mm.then_inc(z2_ready, 1)
                pe.wait_ge(z2_copied, NCH)

            probe()
            state(pe, go["pe"], regs)
            with pe.While(lambda: pe.snap(regs[0]) < NB):
                with pe.If(pe.snap(regs[2]) > 0):
                    attention()
                with pe.Else():
                    pe.nop()
                with pe.If(pe.snap(regs[3]) > 0):
                    feed_forward()
                with pe.Else():
                    pe.nop()
                probe()
                state(pe, go["pe"], regs)

        @block.scalar
        def _(act):
            regs = registers(act, "act")

            def column():
                act.activation(m.hcol[:, 0:1], h[0:C, 0:1], ACT.Copy).then_inc(settled, 1)

            def attention():
                for k in range(NCH):
                    act.wait_ge(u_ready, k + 1)
                    act.activation(ut[:, k * CH:(k + 1) * CH], ps[:, 4 + k, :], ACT.Copy).then_inc(u_copied, 1)
                act.wait_ge(shift_ready, 1)
                act.activation(m.mt[:, :], ps[:, 0, 0:128].bitcast(BF16), ACT.Copy).then_inc(shift_copied, 1)
                for u in range(NU):
                    r = 2 * (u % 3)
                    act.wait_ge(st_ready, u + 1)
                    if u >= 3:
                        act.wait_ge(pv_ready, u - 2)
                    act.activation(m.ex[:, u % 3, :], ps[:, r:r + 2, :].rearrange("p a n -> p (a n)"),
                                   ACT.Exp).then_inc(exp_done, 1)
                for k in range(NCH):
                    act.wait_ge(y_ready, k + 1)
                    act.activation(h[:, k * CH:(k + 1) * CH], ps[:, k, :], ACT.Copy).then_inc(y_copied, 1)
                act.wait_ge(y_copied, NCH)

            def down(k):
                act.wait_ge(z2_ready, k + 1)
                act.activation(h[:, k * CH:(k + 1) * CH], ps[:, 6 + k % 2, :], ACT.Identity,
                               bias=m.b2[:, 0:1]).then_inc(z2_copied, 1)

            def feed_forward():
                act.wait_ge(loaded, 16 * NLOAD)
                for k in range(NCH):
                    for j in (0, 2):
                        w = J * k + j
                        act.wait_ge(z1_ready, w + 1)
                        if w >= 6:
                            act.wait_ge(z2_ready, (w - 6) // J + 1)
                        act.activation(m.z1[:, w % 6, :], ps[:, w % 6, :], ACT.Relu, bias=m.b1[:, 0:1]).then_inc(relu_a, 1)
                    if k >= 1:
                        down(k - 1)
                down(NCH - 1)
                act.wait_ge(z2_copied, NCH)

            column()
            state(act, go["act"], regs)
            with act.While(lambda: act.snap(regs[0]) < NB):
                with act.If(act.snap(regs[2]) > 0):
                    attention()
                with act.Else():
                    act.nop()
                with act.If(act.snap(regs[3]) > 0):
                    feed_forward()
                with act.Else():
                    act.nop()
                column()
                state(act, go["act"], regs)

        @block.vector
        def _(dve):
            regs = registers(dve, "dve")

            def choose():
                n = 0

                def step(ins):
                    nonlocal n
                    ins.then_inc(ctl, 1)
                    n += 1
                    dve.wait_ge(ctl, n)

                r, key, one, sc = m.crow, m.ckey, m.cone, m.csc
                dve.wait_ge(probed, 1)
                step(dve.tensor_copy(r[:, :], ps[0:1, 0, 0:NOPS]))
                step(dve.tensor_reduce(sc[:, 0:1], r[:, :], AXX, ALU.max))
                step(dve.scalar_tensor_tensor(key[:, :], r[:, :], sc[:, 0:1], m.revop[:, :], ALU.is_ge, ALU.mult))
                step(dve.tensor_reduce(sc[:, 1:2], key[:, :], AXX, ALU.max))
                step(dve.tensor_scalar(one[:, :], key[:, :], sc[:, 1:2], None, ALU.is_equal))
                step(dve.tensor_tensor(m.cprod[:, :, :], m.codes[:, :, :],
                                       one[:, None, :].broadcast_to([1, NB, NOPS]), ALU.mult))
                step(dve.tensor_reduce(m.code[:, :], m.cprod[:, :, :], AXX, ALU.add))
                step(dve.scalar_tensor_tensor(m.cand[:, :], m.code[:, :], 0.5, m.revstep[:, :], ALU.is_gt, ALU.mult))
                step(dve.scalar_tensor_tensor(m.cand[:, :], m.revstep[:, :], m.lim[:, 0:1], m.cand[:, :],
                                              ALU.is_le, ALU.mult))
                step(dve.tensor_reduce(sc[:, 2:3], m.cand[:, :], AXX, ALU.max))
                step(dve.tensor_scalar(sc[:, 2:3], sc[:, 2:3], float(TOP - NB), None, ALU.max))
                step(dve.scalar_tensor_tensor(m.cand[:, :], m.revstep[:, :], sc[:, 2:3], m.code[:, :],
                                              ALU.is_equal, ALU.mult))
                step(dve.tensor_reduce(sc[:, 3:4], m.cand[:, :], AXX, ALU.add))
                step(dve.tensor_scalar(sc[:, 4:5], sc[:, 3:4], 1.5, None, ALU.is_gt))
                dve.tensor_scalar(m.lim[:, :], sc[:, 2:3], -1.0, None, ALU.add).then_inc(ctl, 1)
                dve.tensor_scalar(m.state[:, 0:1], sc[:, 2:3], -1.0, float(TOP), ALU.mult, ALU.add).then_inc(ctl, 1)
                dve.tensor_scalar(m.state[:, 1:2], sc[:, 1:2], -1.0, float(TOP), ALU.mult, ALU.add).then_inc(ctl, 1)
                dve.tensor_copy(m.state[:, 3:4], sc[:, 4:5]).then_inc(ctl, 1)
                dve.scalar_tensor_tensor(m.state[:, 2:3], sc[:, 4:5], -2.0, sc[:, 3:4], ALU.mult,
                                         ALU.add).then_inc(ctl, 1)
                dve.wait_ge(ctl, n + 5)
                for x in per_block + [probed, ctl]:
                    dve.sem_clear(x)
                for x in list(go.values()) + [go_dve]:
                    dve.sem_inc(x, 1)

            def attention():
                dve.wait_ge(mats_ready, 1)
                dve.scalar_tensor_tensor(m.sabd[:, :], ps[:, 0, 0:128], float(C) ** -0.5, m.blkone[:, :],
                                         ALU.mult, ALU.mult).then_inc(mats_masked, 1)
                dve.tensor_tensor(m.vobd[:, :], ps[:, 1, 0:128], m.blkone[:, :], ALU.mult).then_inc(mats_masked, 1)
                for q in range(NCH):
                    bank = (q + 2) % 4
                    dve.wait_ge(ht_ready, q + 1)
                    dve.tensor_copy(htok[:, bank * CH:(bank + 1) * CH], ps[:, bank, :]).then_inc(ht_copied, 1)
                for g in range(G):
                    p = g % 2
                    dve.wait_ge(s_ready, g + 1)
                    dve.tensor_reduce(m.mx[:, g, :, :].rearrange("p j s -> p (j s)"),
                                      ps[:, 4 * p:4 * p + 4, :].rearrange("p j (s m) -> p (j s) m", s=S),
                                      AXX, ALU.max).then_inc(max_done, 1)
                dve.wait_ge(max_done, G)
                mv = m.mx[:, :, :, :].rearrange("p g j s -> p (g j) s").rearrange("p b s -> p s b")
                dve.tensor_scalar(m.negmx[:, :, :], mv, -1.0, None, ALU.mult).then_inc(shift, 1)
                n = 1
                for a in range(3):
                    dve.wait_ge(shift, n)
                    dve.tensor_copy(m.mparts[:, :, a, :], m.negmx[:, :, :]).then_inc(shift, 1)
                    n += 1
                    if a < 2:
                        dve.wait_ge(shift, n)
                        dve.tensor_tensor(m.negmx[:, :, :], m.negmx[:, :, :], m.mparts[:, :, a, :],
                                          ALU.subtract).then_inc(shift, 1)
                        n += 1
                for g in range(G):
                    dve.wait_ge(pv_ready, 2 * (g + 1))
                    dve.reciprocal(m.rd[:, g % 2, :], ps[:, 6 + g % 2, N:2 * N]).then_inc(inv_done, 1)
                    dve.wait_ge(inv_done, g + 1)
                    dve.tensor_tensor(y0[:, g * N:(g + 1) * N], ps[:, 6 + g % 2, 0:N], m.rd[:, g % 2, :],
                                      ALU.mult).then_inc(y0_done, 1)
                dve.wait_ge(y0_done, G)

            def feed_forward():
                dve.wait_ge(loaded, 16 * NLOAD)
                for k in range(NCH):
                    for j in (1, 3):
                        w = J * k + j
                        dve.wait_ge(z1_ready, w + 1)
                        if w >= 6:
                            dve.wait_ge(z2_ready, (w - 6) // J + 1)
                        dve.tensor_scalar(m.z1[:, w % 6, :], ps[:, w % 6, :], m.b1[:, 0:1], 0.0, ALU.add,
                                          ALU.max).then_inc(relu_v, 1)
                dve.wait_ge(relu_v, 2 * NCH)

            choose()
            state(dve, go_dve, regs)
            with dve.While(lambda: dve.snap(regs[0]) < NB):
                with dve.If(dve.snap(regs[2]) > 0):
                    attention()
                with dve.Else():
                    dve.nop()
                with dve.If(dve.snap(regs[3]) > 0):
                    feed_forward()
                with dve.Else():
                    dve.nop()
                choose()
                state(dve, go_dve, regs)

    with nc.Block() as block:
        @block.vector
        def _(dve):
            for k in range(NCH):
                c = slice(k * CH, (k + 1) * CH)
                dve.tensor_tensor(m.x[:, c], m.x[:, c], h[:, c], ALU.add).then_inc(added, 1)

        @block.sync
        def _(sp):
            stored = sem("rb_stored")
            for k in range(NCH):
                sp.wait_ge(added, k + 1)
                for j in range(J):
                    sp.dma_start(m.d_out.rearrange("(g j) c n -> j c g n", j=J)[j, :, 2 * k:2 * k + 2, :],
                                 m.x[32 * j:32 * j + 32, k * CH:(k + 1) * CH].rearrange("c (g n) -> c g n", g=2))\
                        .then_inc(stored, 16)
            sp.wait_ge(stored, 16 * J * NCH)


def place(nc, m, ctx):
    def sb(name, shape, dt=F32):
        return ctx.enter_context(nc.sbuf_tensor(name, shape, dt))

    m.ps = ctx.enter_context(nc.psum_tensor("ps", [128, 8, CH], F32))
    R_ = sb("R", [128, 4 * B * N])
    P_ = sb("P", [128, 2 * COLS])
    Q_ = sb("Q", [128, 2 * COLS])
    m.x = sb("x", [128, COLS])
    m.z = sb("z", [128, COLS])
    m.tmpA = sb("tmpA", [128, COLS])
    m.tmpB, m.rstd = Q_[:, 0:COLS], Q_[:, COLS:2 * COLS]

    def view(at, names, dims, dt=F32, base=R_):
        size = 1
        for d in dims:
            size *= d
        t = base[:, at:at + (size // 2 if dt == BF16 else size)]
        if dt != F32:
            t = t.bitcast(dt)
        if len(dims) == 1:
            return t
        letters = "abcde"[:len(dims)]
        kw = {letters[i]: dims[i] for i in range(1, len(dims))}
        return t.rearrange(f"p ({' '.join(letters)}) -> p {' '.join(letters)}", **kw)

    r = B * N
    m.r0, m.r1, m.r2, m.r3 = (view(i * r, "", [B, N]) for i in range(4))
    m.memv_b = view(0, "", [B, 128], base=P_)
    m.ct = view(0, "", [B, 128], base=Q_)
    m.big = view(0, "", [S, H, CH])
    m.co = view(3 * r + 4608, "", [C // 4, N])
    at = 2 * r
    m.qbd = view(at, "", [LAYERS, ZHEADS, 128]); at += LAYERS * ZHEADS * 128
    m.vt4 = view(at, "", [LAYERS * ZHEADS * 32]); at += LAYERS * ZHEADS * 32
    m.gbd = view(at, "", [G, 128]); at += G * 128
    m.abd = view(at, "", [G, 128]); at += G * 128
    m.pmat = view(at, "", [G, ZHEADS * 32]); at += G * ZHEADS * 32
    m.amat = view(at, "", [G, 32]); at += G * 32
    m.wt = view(at, "", [G, 32]); at += G * 32
    m.rmat = view(at, "", [G, 32]); at += G * 32
    at = 3 * r + COLS + 1024
    m.ewbd = view(at, "", [E, 128])
    m.sele = view(3 * r + 4608 + COLS, "", [E, 128], BF16)
    at = 0
    nl = G * S * J * E
    m.lg = view(at, "", [nl]); at += nl
    m.key = view(at, "", [nl]); at += nl
    m.one1 = view(at, "", [nl]); at += nl
    m.sel2 = view(at, "", [nl]); at += nl
    m.gparts = view(at, "", [G * S, 4, 32], BF16); at += G * S * 64
    m.stat = view(at, "", [4, G * S * J]); at += 4 * G * S * J
    m.gt = view(at, "", [COLS], BF16); at += COLS // 2
    m.gz = view(at, "", [3, CH]); at += 3 * CH
    m.vm = view(2 * r, "", [G * S * J, AH, 32])
    m.qkt = view(0, "", [2, 2, B, N], BF16)
    m.qkparts = view(2 * r, "", [2, 3, COLS], BF16)
    m.qkstack = view(3 * r, "", [2, J, COLS], BF16)
    m.selqk = view(COLS, "", [2, 2, 128], BF16, base=P_)
    m.selqk32 = view(COLS + 256, "", [2 * 2 * 128], base=P_)[0:96]
    m.att = view(3 * r, "", [6, 2, 3 * 128])
    m.sa = view(3 * r + 3 * 1536, "", [COLS])
    m.pa = P_[:, 0:COLS]
    m.h = view(0, "", [COLS])
    m.ex = view(COLS, "", [3, 4 * N])
    m.z1 = view(COLS + 12 * N, "", [6, CH])

    m.ident = sb("ident", [128, 128])
    m.exchange = sb("exchange", [128, 128])
    m.identb = sb("identb", [128, 128], BF16)
    m.blkone = sb("blkone", [128, 128])
    m.blkmean = sb("blkmean", [128, 128])
    m.blkmean64 = sb("blkmean64", [128, 128])
    m.causal = sb("causal", [128, 128])
    m.memmask = sb("memmask", [128, B])
    m.ident32 = sb("ident32", [128, 32])
    m.ol = sb("ol", [128, 23 * W])
    m.orr = sb("orr", [128, 23 * W])
    m.headmask = sb("headmask", [128, AH, 32])
    m.rank = sb("rank", [128, E])
    m.jmask = sb("jmask", [128, J])
    m.selb = sb("selb", [128, B], BF16)
    m.self32 = sb("self32", [128, B])
    m.sele32 = view(6 * COLS, "", [E, 128])
    m.ones32 = sb("ones32", [128, 32])
    m.eps = sb("eps", [128, 2])
    m.wqkv = sb("wqkv", [128, 384])
    m.wo = sb("wo", [128, C])
    m.memk = sb("memk", [128, MEM])
    m.memv = sb("memv", [128, 128])
    m.gcol = sb("gcol", [128, 1])
    m.gs = sb("gs", [128, 1])
    m.bout = sb("bout", [128, 1])
    m.small = sb("small", [128, 4])
    m.bst = sb("bst", [128, 6 * G])
    m.bag = sb("bag", [128, 2 * G])
    m.std8 = sb("std8", [128, G])
    m.inv8 = sb("inv8", [128, G])
    m.kmax = sb("kmax", [128, B])
    m.knegmax = sb("knegmax", [128, B])
    m.ksum = sb("ksum", [128, B])
    m.memsum = sb("memsum", [128, B])
    m.em = sb("em", [128, 128])
    m.emt = sb("emt", [128, 128])
    m.qmax, m.qsum, m.qinv = (m.z[:, i * 256:(i + 1) * 256] for i in range(3))
    m.w2 = view(0, "", [B, C], base=P_)
    m.wcomp = sb("wcomp", [C, CONV_P * CONV_P])
    m.wclass = view(COLS, "", [CLASSES, 2 * R + 1], base=P_)[0:C]
    m.bl = view(0, "", [C, W], base=P_)
    m.br = view(CH, "", [C, W], base=P_)
    m.kmat = view(2 * CH, "", [S, N], base=P_)
    m.kmat_rev = view(COLS + CH, "", [S, N], base=P_)
    m.rwbd = sb("rwbd", [128, J * E])
    m.rb = sb("rb", [128, E])
    m.ebrep = sb("ebrep", [128, C])
    m.ebpart = sb("ebpart", [128, 3, C], BF16)
    m.ebbd = sb("ebbd", [128, 3, 128], BF16)
    m.wqkbd = sb("wqkbd", [128, 2, 128])
    m.wvbd = sb("wvbd", [128, 128])
    m.bqk = sb("bqk", [128, 2])
    m.bv = sb("bv", [128, C])
    m.wubd = sb("wubd", [128, 2, 128])
    m.bu = sb("bu", [128, 2])
    m.gam = sb("gam", [128, 2])
    m.bet = sb("bet", [128, 2])
    m.wfbd = sb("wfbd", [128, 2, 128])
    m.bf = sb("bf", [128, 1])
    m.relt = sb("relt", [128, S, N])
    m.wsm = view(COLS + 12 * N + 6 * CH + 2 * N + 1280, "", [4, 128])[0:C]
    m.w1 = sb("w1", [128, HID])
    m.w2f = sb("w2f", [128, C])
    m.b1 = sb("b1", [128, 1])
    m.b2 = sb("b2", [128, 1])
    m.sabd = view(COLS + 12 * N + 6 * CH + 2 * N + 1024, "", [128])
    m.vobd = view(COLS + 12 * N + 6 * CH + 2 * N + 1152, "", [128])
    m.mx = sb("mx", [128, G, J, S])
    m.negmx = sb("negmx", [128, S, B])
    m.mparts = sb("mparts", [128, S, 4, B], BF16)
    m.mt = sb("mt", [128, S * 128], BF16)
    m.rd = view(COLS + 12 * N + 6 * CH, "", [2, N])
    m.hcol = sb("hcol", [C, 1])
    m.state = sb("state", [1, 4], I32)
    m.crow = sb("crow", [1, NOPS])
    m.ckey = sb("ckey", [1, NOPS])
    m.cone = sb("cone", [1, NOPS])
    m.revop = sb("revop", [1, NOPS])
    m.revstep = sb("revstep", [1, NB])
    m.code = sb("code", [1, NB])
    m.cand = sb("cand", [1, NB])
    m.codes = view(COLS + 1024, "", [NB, NOPS], base=P_)[0:1]
    m.cprod = view(COLS + 12 * N + 6 * CH + 2 * N, "", [NB, NOPS])[0:1]
    m.masks = view(5 * COLS, "", [2, NB * NOPS], I32)[0:1]
    m.csc = sb("csc", [1, 8])
    m.lim = sb("lim", [1, 1])


def load_first(nc, m, sem, d):
    zeroed = sem("ld_zeroed")
    loaded = sem("ld_loaded")
    made = sem("ld_made")
    zero = [m.wvbd, m.rwbd]
    n_zero = len(zero) + 4
    plain = [(m.ident, d.ident), (m.blkone, d.blkone), (m.causal, d.causal), (m.memmask, d.memmask),
             (m.ident32, d.ident32), (m.exchange, d.exchange), (m.ol, d.ol), (m.orr, d.orr), (m.rank, d.rank), (m.jmask, d.jmask),
             (m.self32, d.selb), (m.headmask, d.headmask), (m.revop, d.revop),
             (m.revstep, d.revstep), (m.wo, d.w_out_t), (m.memk, d.mem_k),
             (m.wcomp, d.weight_comp)]

    def whole(t):
        return t[tuple(slice(None) for _ in t.shape)]

    rows = []
    for j in range(J):
        p = slice(32 * j, 32 * j + 32)
        rows += [(m.x[p, :].rearrange("c (g n) -> c g n", g=G), d.x.rearrange("(g j) c n -> j c g n", j=J)[j]),
                 (m.wqkv[p, :], d.w_qkv_t), (m.gcol[p, :], d.g), (m.bout[p, :], d.b_out),
                 (m.gam[p, :], d.ln_gamma), (m.bet[p, :], d.ln_beta), (m.bqk[p, :], d.bqk), (m.bu[p, :], d.bu), (m.bf[p, :], d.bf)]
    rows += [(m.memv[:, :], d.mem_v[None, :, :].broadcast_to([B, MEM, 128])),
             (m.rb[:, :], d.rb.broadcast_to([128, E])), (m.bv[:, :], d.bv.broadcast_to([128, C])),
             (m.ebrep[:, :], d.eb[None, :, :].broadcast_to([128 // E, E, C]))]
    blocks = []
    for j in range(J):
        p, c = slice(32 * j, 32 * j + 32), slice(32 * j, 32 * j + 32)
        blocks += [(m.wvbd[p, c], d.wv), (m.rwbd[p, E * j:E * j + E], d.router_w)]
        for i in range(2):
            blocks += [(m.wubd[p, i, c], d.wu[:, 32 * i:32 * i + 32]), (m.wfbd[p, i, c], d.wf[32 * i:32 * i + 32, :])]
        blocks += [(m.wqkbd[p, 0, c], d.wq), (m.wqkbd[p, 1, c], d.wk)]
    last = d.pos_w.shape[0] - 1
    for s in range(S):
        src = bass.AP(tensor=d.pos_w.tensor, offset=d.pos_w.offset + last - (N - 1) - 128 * s - 127,
                      ap=[[1, 128], [1, N]])
        rows.append((m.relt[:, s, :], src))

    with nc.Block() as block:
        @block.sync
        def _(sp):
            for dst, src in rows:
                sp.dma_start(dst, src).then_inc(loaded, 16)
            sp.wait_ge(zeroed, n_zero)
            for dst, src in blocks[0::2]:
                sp.dma_start(dst, src).then_inc(loaded, 16)
            sp.wait_ge(loaded, 16 * (len(rows) + len(plain) + len(blocks)))

        @block.scalar
        def _(act):
            for dst, src in plain:
                act.dma_start(whole(dst), src).then_inc(loaded, 16)
            act.wait_ge(zeroed, n_zero)
            for dst, src in blocks[1::2]:
                act.dma_start(dst, src).then_inc(loaded, 16)

        @block.gpsimd
        def _(pool):
            for t in zero:
                pool.memset(t[:, :], 0.0).then_inc(zeroed, 1)
            pool.memset(m.wqkbd[:, :, :], 0.0).then_inc(zeroed, 1)
            pool.memset(m.wubd[:, :, :], 0.0).then_inc(zeroed, 1)
            pool.memset(m.wfbd[:, :, :], 0.0).then_inc(zeroed, 1)
            pool.memset(m.mparts[:, :, 3, :], 0.0).then_inc(zeroed, 1)

        @block.vector
        def _(dve):
            n = 0

            def step(ins):
                nonlocal n
                ins.then_inc(made, 1)
                n += 1
                dve.wait_ge(made, n)

            dve.memset(m.eps[:, 0:1], EPS_GN).then_inc(made, 1)
            dve.memset(m.eps[:, 1:2], EPS_A).then_inc(made, 1)
            dve.memset(m.ones32[:, :], 1.0).then_inc(made, 1)
            dve.memset(m.lim[:, :], 64.0).then_inc(made, 1)
            n = 4
            dve.wait_ge(loaded, 16 * (len(rows) + len(plain) + len(blocks)))
            step(dve.tensor_copy(m.identb[:, :], m.ident[:, :]))
            step(dve.tensor_copy(m.selb[:, :], m.self32[:, :]))
            step(dve.tensor_scalar(m.blkmean[:, :], m.blkone[:, :], 1.0 / C, None, ALU.mult))
            step(dve.tensor_scalar(m.blkmean64[:, :], m.blkone[:, :], 0.5 / C, None, ALU.mult))
            for i in range(3):
                step(dve.tensor_copy(m.ebpart[:, i, :], m.ebrep[:, :]))
                step(dve.tensor_tensor(m.ebrep[:, :], m.ebrep[:, :], m.ebpart[:, i, :], ALU.subtract))
                step(dve.tensor_tensor(m.ebbd[:, i, :].rearrange("p (j c) -> p j c", j=J),
                                       m.ebpart[:, i, None, :].broadcast_to([128, J, C]),
                                       m.jmask[:, :, None].broadcast_to([128, J, C]), ALU.mult))


def load_second(nc, m, sem, d):
    zeroed = sem("l2_zeroed")
    loaded = sem("l2_loaded")
    made = sem("l2_made")
    copies = [(m.sele32[:, :, :], d.sele), (m.masks[0:1, 0, :], d.attn_mask), (m.masks[0:1, 1, :], d.ffn_mask)]
    copies += [(m.vt4[32 * j:32 * j + 32, :].rearrange("d (l i) -> d l i", i=32), d.v_t) for j in range(J)]
    for j in range(J):
        p, c = slice(32 * j, 32 * j + 32), slice(32 * j, 32 * j + 32)
        copies += [(m.qbd[p, :, :, c].rearrange("p l h c -> p (l h) c"), d.q_t), (m.ewbd[p, :, c], d.ew)]
        copies.append((m.wt[p, :, :], d.ident32[0:32, None, :].broadcast_to([32, G, 32])))
    for s in range(S):
        for y in range(H // S):
            first = KS // 2 - R
            src = bass.AP(tensor=d.kpe.tensor,
                          offset=d.kpe.offset + (first + y + (S - 1 - s) * (H // S)) * KS + first,
                          ap=[[1, W], [KS, H], [1, W]])
            copies.append((m.kmat_rev[16 * y:16 * y + 16, s, :].rearrange("p (y x) -> p y x", y=H), src))
    with nc.Block() as block:
        @block.gpsimd
        def _(pool):
            pool.memset(m.qbd[:, :, :, :], 0.0).then_inc(zeroed, 1)
            pool.memset(m.ewbd[:, :, :], 0.0).then_inc(zeroed, 1)

        @block.sync
        def _(sp):
            sp.wait_ge(zeroed, 2)
            for dst, src in copies[0::2]:
                sp.dma_start(dst, src).then_inc(loaded, 16)
            sp.wait_ge(loaded, 16 * len(copies))

        @block.scalar
        def _(act):
            act.wait_ge(zeroed, 2)
            for dst, src in copies[1::2]:
                act.dma_start(dst, src).then_inc(loaded, 16)

        @block.vector
        def _(dve):
            n = 0

            def step(ins):
                nonlocal n
                ins.then_inc(made, 1)
                n += 1
                dve.wait_ge(made, n)

            dve.wait_ge(loaded, 16 * len(copies))
            step(dve.tensor_copy(m.sele[:, :, :], m.sele32[:, :, :]))
            cd = m.codes[:, :, :].rearrange("a s o -> a (s o)")
            step(dve.tensor_copy(cd, m.masks[:, 1, :]))
            step(dve.tensor_tensor(cd, cd, cd, ALU.add))
            step(dve.tensor_copy(m.cprod[:, :, :].rearrange("a s o -> a (s o)"), m.masks[:, 0, :]))
            step(dve.tensor_tensor(cd, cd, m.cprod[:, :, :].rearrange("a s o -> a (s o)"), ALU.add))


def conv_attn_hybrid(nc, d):
    m = Mem()
    with ExitStack() as ctx:
        def stage(run, *args):
            sems = []
            with ExitStack() as own:
                def sem(name):
                    sems.append(own.enter_context(nc.semaphore(name)))
                    return sems[-1]
                run(nc, m, sem, *args)
                with nc.Block() as block:
                    @block.gpsimd
                    def _(pool):
                        for s in sems:
                            pool.sem_clear(s)

        place(nc, m, ctx)
        m.scratch_w = nc.dram_tensor("scratch_w", [C, CLASSES, 2 * R + 1], F32, kind="Internal").ap()
        m.scratch_x = nc.dram_tensor("scratch_x", [B, C, N], F32, kind="Internal").ap()
        m.d_out = d.out
        m.d_selqk = d.selqk
        m.d_small, m.d_w1, m.d_w2, m.d_b1, m.d_b2 = d.small4, d.w1, d.w2, d.b1, d.b2
        stage(load_first, d)
        stage(instance_norm, "gn0", m.x, m.z)
        stage(linear_attention)
        stage(load_second, d)
        stage(instance_norm, "gn1", m.x, m.z)
        stage(peripheral_convolution)
        stage(normalise_tokens, "ln1", [m.x], [m.z], EPS_T, m.blkmean)
        stage(linear_transformer)
        stage(normalise_tokens, "ln2", [m.x], [m.z], EPS_T, m.blkmean)
        stage(mixture_of_experts)
        stage(normalise_tokens, "ln3", [m.x], [m.z], EPS_T, m.blkmean)
        stage(squared_attention)
        stage(normalise_tokens, "ln4", [m.x], [m.h], EPS_T, m.blkmean)
        stage(routed_blocks)


def constants():
    import numpy as np
    p = np.arange(128)
    f = np.float32
    out = {"ident": np.eye(128, dtype=f),
           "blkone": (p[:, None] // 32 == p[None, :] // 32).astype(f),
           "causal": (p[:, None] <= p[None, :]).astype(f),
           "memmask": (p[:, None] // MEM == np.arange(B)[None, :]).astype(f),
           "exchange": np.eye(128, dtype=f)[::-1],
           "ident32": (p[:, None] % 32 == np.arange(32)[None, :]).astype(f),
           "rank": np.broadcast_to(np.arange(E, 0, -1), (128, E)).astype(f),
           "revop": (64 - np.arange(NOPS))[None, :].astype(f),
           "revstep": (64 - np.arange(NB))[None, :].astype(f)}
    part, j, e = p // 32, p // E % J, p % E
    live = part < 3
    out["jmask"] = (live[:, None] & (j[:, None] == np.arange(J))).astype(f)
    out["sele"] = (live[:, None, None] & (e[:, None, None] == np.arange(E)[None, :, None])
                   & (j[:, None, None] == p // C)).astype(f)
    out["selb"] = (live[:, None] & (p[:, None] % 32 == np.arange(B))).astype(f)
    out["headmask"] = np.broadcast_to(np.arange(32)[None, :] // AHD == np.arange(AH)[:, None],
                                      (128, AH, 32)).astype(f)
    terms = ((0, 0, 0, 1, 1, 2), (0, 1, 2, 0, 1, 0))
    sel = np.zeros((3, AH, AHD, 2, 2, 2, 8, AHD), f)
    for x in range(2):
        for h in range(AH):
            for term, part_of in enumerate(terms[x]):
                sel[part_of, h, :, x, h // 2, h % 2, term, :] = np.eye(AHD)
    out["selqk"] = sel.reshape(96, 512)
    for name, first, lo in (("ol", 0, -R), ("orr", 1, -R + 8)):
        t = np.zeros((8, 16, 23, 16), f)
        for q in range(8):
            a, b = CLASS_SPANS[first + q]
            for dy in range(max(a, lo), min(b, lo + 22) + 1):
                t[q, :, dy - lo, :] = np.eye(16)[::-1]
        out[name] = t.reshape(128, 23 * 16)
    return out


def kernel(**inputs):
    import numpy as np
    import concourse.bacc as bacc
    from concourse.bass_utils import run_bass_kernel_spmd

    a = {k: np.asarray(v) for k, v in inputs.items()}
    f = "L3_ffn_"
    arrays = {
        "x": a["x"].reshape(B, C, N),
        "g": a["L0_conv_g"].reshape(C, 1),
        "w_qkv_t": a["L0_conv_w_qkv"].T,
        "mem_k": a["L0_conv_mem_kv"][0].reshape(HEADS * DH, MEM),
        "mem_v": a["L0_conv_mem_kv"][1].transpose(2, 0, 1).reshape(MEM, HEADS * DH),
        "w_out_t": a["L0_conv_w_out"].T,
        "b_out": a["L0_conv_b_out"].reshape(C, 1),
        "weight_comp": a["L1_conv_weight_comp"],
        "kpe": a["L1_conv_kpe"].reshape(KS, KS)[::-1, ::-1],
        "v_t": a["L2_attn_v_matrix"].reshape(LAYERS * ZHEADS, 32, 32).transpose(2, 0, 1),
        "q_t": a["L2_attn_q_matrix"].reshape(LAYERS * ZHEADS, 32, 32).transpose(2, 0, 1),
        "router_w": a["L2_ffn_router_w"],
        "rb": a["L2_ffn_router_b"].reshape(1, E),
        "ew": a["L2_ffn_expert_w"].transpose(1, 0, 2),
        "eb": a["L2_ffn_expert_b"],
        "wq": a["L3_attn_Wq"], "wk": a["L3_attn_Wk"],
        "bqk": np.stack([a["L3_attn_bq"], a["L3_attn_bk"]], axis=1),
        "wv": a["L3_attn_Wv"], "bv": a["L3_attn_bv"].reshape(1, C),
        "wu": a["L3_attn_Wu"], "bu": a["L3_attn_bu"].reshape(2, C).T,
        "pos_w": a["L3_attn_pos_w"][::-1],
        "ln_gamma": a["L3_attn_ln_gamma"].reshape(2, C).T,
        "ln_beta": a["L3_attn_ln_beta"].reshape(2, C).T,
        "wf": a["L3_attn_Wf"], "bf": a["L3_attn_bf"].reshape(C, 1),
        "small4": np.concatenate([a[f + "wq"].swapaxes(2, 3), a[f + "wk"].swapaxes(2, 3),
                                  a[f + "wv"].swapaxes(2, 3), a[f + "wo"]], axis=3).reshape(NB * NOPS, C, 4 * C),
        "w1": a[f + "ffn_w1"].reshape(NB * NOPS, C, HID),
        "w2": a[f + "ffn_w2"].reshape(NB * NOPS, HID, C),
        "b1": a[f + "ffn_b1"].reshape(NB * NOPS, HID, 1),
        "b2": a[f + "ffn_b2"].reshape(NB * NOPS, C, 1),
        "attn_mask": a[f + "attn_mask"].astype(np.int32).reshape(1, NB * NOPS),
        "ffn_mask": a[f + "ffn_mask"].astype(np.int32).reshape(1, NB * NOPS),
    }
    arrays.update(constants())
    nc = bacc.Bacc("TRN2", target_bir_lowering=False, num_devices=1)
    d = Mem()
    arrays = {k: np.ascontiguousarray(v) for k, v in arrays.items()}
    for k, v in arrays.items():
        vars(d)[k] = nc.dram_tensor("in_" + k, v.shape, mybir.dt.from_np(v.dtype), kind="ExternalInput").ap()
    d.out = nc.dram_tensor("out_0", (B, C, N), F32, kind="ExternalOutput").ap()
    conv_attn_hybrid(nc, d)
    r = run_bass_kernel_spmd(nc, [{"in_" + k: v for k, v in arrays.items()}], core_ids=[0])
    return r.results[0]["out_0"].reshape(B, C, H, W)
```

```python
import concourse.bass as bass
import numpy as np
from concourse import mybir
from contextlib import ExitStack

F32 = mybir.dt.float32
BF16 = mybir.dt.bfloat16
I32 = mybir.dt.int32
ALU = mybir.AluOpType
ACT = mybir.ActivationFunctionType
AXX = mybir.AxisListType.X

B, C, H, W = 32, 32, 16, 16
N = H * W
J, G = 4, 8
S = N // 128
COLS = G * N
CH = 512
NCH = COLS // CH
HEADS, DH = 4, 32
MEM = 4
KS, CONV_P = 51, 13
R = H - 1
CLASSES = 9
CLASS0 = 2
CLASS_SPANS = [(-15, -8), (-7, -4), (-3, -2), (-1, -1), (0, 0), (1, 1), (2, 3), (4, 7), (8, 15)]
LAYERS, ZHEADS = 4, 8
E = 8
AH, AHD = 4, 8
NB, NOPS, HID = 33, 19, 128

EARLY = 128 + 2 * 23 * W + 384 + C + MEM + 128 + B + 2 + CONV_P ** 2
LASTING = 3 * 128 + AH * 32 + 32 + E + J + E + 2 * C + 9 + 7 * 128 + J * E + NOPS + NB

EPS_GN, EPS_T, EPS_A = 1e-5, 1e-5, 1e-3


class Mem:
    pass


def normalise_tokens(nc, m, sem, name, parts, outs, eps, mean_w, gamma=None):
    n = len(parts)
    mean_ready = sem(name + "_mean_ready")
    centred = sem(name + "_centred")
    squared = sem(name + "_squared")
    var_ready = sem(name + "_var_ready")
    std_ready = sem(name + "_std_ready")
    inverted = sem(name + "_inverted")
    spread = sem(name + "_spread")
    scaled = sem(name + "_scaled")
    ps = m.ps
    sq = [m.tmpA, m.tmpB]

    def ch(t, k):
        return t[:, k * CH:(k + 1) * CH]

    with nc.Block() as block:
        @block.tensor
        def _(pe):
            for k in range(NCH):
                for i in range(n):
                    mm = pe.matmul(ps[:, k, :], mean_w[:, :], ch(parts[i], k), start=(i == 0), stop=(i == n - 1))
                mm.then_inc(mean_ready, 1)
            for k in range(NCH):
                pe.wait_ge(squared, n * (k + 1))
                for g in (2 * k, 2 * k + 1):
                    for i in range(n):
                        mm = pe.matmul(ps[0:B, NCH, 0:N], m.gather[:, g, :], sq[i][:, g * N:(g + 1) * N],
                                       start=(g == 0 and i == 0), stop=(g == G - 1 and i == n - 1))
            mm.then_inc(var_ready, 1)
            pe.wait_ge(inverted, 1)
            for g in range(G):
                pe.matmul(ps[:, g // 2, (g % 2) * N:(g % 2) * N + N], m.scatter[:, g, :], m.rstd[0:B, 0:N],
                          start=True, stop=True).then_inc(spread, 1)

        @block.vector
        def _(dve):
            for k in range(NCH):
                dve.wait_ge(mean_ready, k + 1)
                for i in range(n):
                    dve.tensor_tensor(ch(outs[i], k), ch(parts[i], k), ps[:, k, :], ALU.subtract).then_inc(centred, 1)
            dve.wait_ge(std_ready, 1)
            dve.reciprocal(m.rstd[0:B, 0:N], m.rstd[0:B, N:2 * N]).then_inc(inverted, 1)
            for k in range(NCH):
                dve.wait_ge(spread, 2 * (k + 1))
                for i in range(n):
                    o = ch(outs[i], k)
                    dve.tensor_tensor(o, o, ps[:, k, :], ALU.mult).then_inc(scaled, 1)

        @block.scalar
        def _(act):
            for k in range(NCH):
                for i in range(n):
                    act.wait_ge(centred, n * k + i + 1)
                    act.activation(ch(sq[i], k), ch(outs[i], k), ACT.Square).then_inc(squared, 1)
            act.wait_ge(var_ready, 1)
            act.activation(m.rstd[0:B, N:2 * N], ps[0:B, NCH, 0:N], ACT.Sqrt, bias=eps,
                           scale=1.0 / (C * n)).then_inc(std_ready, 1)
            if gamma:
                for k in range(NCH):
                    for i in range(n):
                        o = ch(outs[i], k)
                        act.wait_ge(scaled, n * k + i + 1)
                        act.activation(o, o, ACT.Identity, bias=gamma[i][1], scale=gamma[i][0])\
                            .then_inc(centred, 1)


def instance_norm(nc, m, sem, name, src, dst, src_loaded, beside):
    stats = sem(name + "_stats")
    moments = sem(name + "_moments")
    std = sem(name + "_std")
    inv = sem(name + "_inv")
    done = sem(name + "_done")
    with nc.Block() as block:
        @block.vector
        def _(dve):
            for g in range(G):
                if src_loaded and g % 2 == 0:
                    dve.wait_ge(src_loaded[g // 2], 16)
                dve.bn_stats(m.bst[:, 6 * g:6 * g + 6], src[:, g * N:(g + 1) * N]).then_inc(stats, 1)
            for g in range(G):
                dve.wait_ge(stats, g + 1)
                dve.bn_aggr(m.bag[:, 2 * g:2 * g + 2], m.bst[:, 6 * g:6 * g + 6]).then_inc(moments, 1)
            dve.wait_ge(std, 1)
            dve.reciprocal(m.inv8[:, :], m.std8[:, :]).then_inc(inv, 1)
            dve.wait_ge(inv, 1)
            for g in range(G):
                c = slice(g * N, (g + 1) * N)
                dve.tensor_scalar(dst[:, c], src[:, c], m.bag[:, 2 * g:2 * g + 1], m.inv8[:, g:g + 1],
                                  ALU.subtract, ALU.mult).then_inc(done, 1)

        @block.scalar
        def _(act):
            act.wait_ge(moments, G)
            act.activation(m.std8[:, :], m.bag[:, 1:2 * G:2], ACT.Sqrt, bias=m.eps[:, 0:1]).then_inc(std, 1)

        @block.sync
        def _(sp):
            beside(sp)


def linear_attention(nc, m, sem):
    ps = m.ps
    UN = G // 2 * J
    ek, ekt, vt, qt, qf = m.r0, m.r1, m.r2, m.r3, m.r0
    xn = m.tmpA
    squared = sem("la_squared")
    norm2_ready = sem("la_norm2_ready")
    norm_ready = sem("la_norm_ready")
    inv_ready = sem("la_inv_ready")
    spread = sem("la_spread")
    xn_ready = sem("la_xn_ready")
    proj_ready = sem("la_proj_ready")
    kmax_ready = sem("la_kmax_ready")
    knegmax_ready = sem("la_knegmax_ready")
    kexp_done = sem("la_kexp_done")
    kt_ready = sem("la_kt_ready")
    kt_copied = sem("la_kt_copied")
    v_copied = sem("la_v_copied")
    qmax_ready = sem("la_qmax_ready")
    qsub_done = sem("la_qsub_done")
    qexp_done = sem("la_qexp_done")
    qsum_ready = sem("la_qsum_ready")
    qinv_ready = sem("la_qinv_ready")
    qnorm_done = sem("la_qnorm_done")
    qt_ready = sem("la_qt_ready")
    qt_copied = sem("la_qt_copied")
    memmax_ready = sem("la_memmax_ready")
    memshift_done = sem("la_memshift_done")
    memexp_done = sem("la_memexp_done")
    memsum = sem("la_memsum")
    memt_ready = sem("la_memt_ready")
    memt_copied = sem("la_memt_copied")
    memv_masked = sem("la_memv_masked")
    ctx_ready = sem("la_ctx_ready")
    ctx_copied = sem("la_ctx_copied")
    w2_ready = sem("la_w2_ready")
    w2_scaled = sem("la_w2_scaled")
    out_ready = sem("la_out_ready")
    added = sem("la_added")

    def bank_free(eng, w):
        p, u = divmod(w - 4, UN)
        if w >= 4:
            if p == 0:
                eng.wait_ge(kexp_done, 2 * (u + 1))
            elif p == 1:
                eng.wait_ge(v_copied, u + 1)
            else:
                eng.wait_ge(qsub_done, u + 1)

    def unit(u):
        return u % 4, 2 * (u // 4)

    with nc.Block() as block:
        @block.tensor
        def _(pe):
            for k in range(NCH):
                pe.wait_ge(squared, k + 1)
                for g in (2 * k, 2 * k + 1):
                    mm = pe.matmul(ps[0:B, 4, 0:N], m.gather[:, g, :], m.tmpB[:, g * N:(g + 1) * N],
                                   start=(g == 0), stop=(g == G - 1))
            mm.then_inc(norm2_ready, 1)
            pe.wait_ge(inv_ready, 2)
            for g in range(G):
                pe.matmul(ps[:, g // 2, (g % 2) * N:(g % 2) * N + N], m.scatter[:, g, :], m.rstd[0:B, 0:N],
                          start=True, stop=True).then_inc(spread, 1)
            pe.wait_ge(xn_ready, NCH)

            def project(w):
                p, u = divmod(w, UN)
                j, g = unit(u)
                rows = slice(32 * j, 32 * j + 32)
                bank_free(pe, w)
                if p == 0:
                    mm = pe.matmul(ps[:, j, :], m.wqkv[rows, 128:256], xn[rows, g * N:(g + 2) * N],
                                   start=True, stop=True)
                else:
                    wcols = m.wqkv[rows, 256:384] if p == 1 else m.wqkv[rows, 0:128]
                    for q in range(4):
                        mm = pe.matmul(ps[:, j, q * 128:(q + 1) * 128],
                                       xn[rows, g * N + q * 128:g * N + (q + 1) * 128], wcols,
                                       start=True, stop=True)
                mm.then_inc(proj_ready, 1)

            def transposes(w):
                p, u = divmod(w, UN)
                j, g = unit(u)
                if p == 0:
                    if u >= 4:
                        pe.wait_ge(kt_copied, u - 3)
                    pe.wait_ge(kexp_done, 2 * (u + 1))
                    src, ready = ek, kt_ready
                else:
                    if u < 4:
                        pe.wait_ge(kt_copied, UN)
                    else:
                        pe.wait_ge(qt_copied, u - 3)
                    pe.wait_ge(qnorm_done, u + 1)
                    src, ready = qt, qt_ready
                for q in range(4):
                    mm = pe.transpose(ps[:, 4 + j, q * 128:(q + 1) * 128],
                                      src[:, j * G + g + q // 2, (q % 2) * 128:(q % 2) * 128 + 128], m.ident[:, :])
                mm.then_inc(ready, 1)

            for w in range(3 * UN + 6):
                if w < 3 * UN:
                    project(w)
                if 4 <= w < UN + 4:
                    transposes(w - 4)
                if w == UN + 5:
                    pe.wait_ge(memexp_done, 1)
                    pe.wait_ge(kt_copied, UN)
                    pe.transpose(ps[:, 4, 0:128], m.em[:, :], m.ident[:, :]).then_inc(memt_ready, 1)
                if w == UN + 6:
                    pe.wait_ge(memt_copied, 1)
                if w >= 2 * UN + 6:
                    transposes(w - 2 * UN - 6 + UN)
            pe.wait_ge(memv_masked, 1)
            pe.wait_ge(v_copied, UN)
            pe.wait_ge(qsub_done, UN)
            for q in range(B // 4):
                bank = q % 4
                if q >= 4:
                    pe.wait_ge(ctx_copied, q - 3)
                for i in range(4):
                    b = 4 * q + i
                    o = ps[:, bank, i * 128:(i + 1) * 128]
                    for s in range(S):
                        pe.matmul(o, vt[:, b, s * 128:(s + 1) * 128], ekt[:, b, s * 128:(s + 1) * 128],
                                  start=(s == 0), stop=False)
                    mm = pe.matmul(o, m.memv_b[:, b, :], m.emt[:, :], start=False, stop=True)
                mm.then_inc(ctx_ready, 1)
            pe.wait_ge(qt_copied, UN)
            for b in range(B):
                if b % 4 == 0:
                    pe.wait_ge(ctx_copied, b // 4 + 1)
                mm = pe.matmul(ps[:, 4 + b // 16, (b % 16) * 32:(b % 16) * 32 + 32], m.ct[:, b, :], m.wo[:, :],
                               start=True, stop=True)
            mm.then_inc(w2_ready, 1)
            pe.wait_ge(w2_scaled, 1)
            for k in range(NCH):
                for h in range(2):
                    for j in range(J):
                        b = j * G + 2 * k + h
                        mm = pe.matmul(ps[32 * j:32 * j + 32, k, h * N:(h + 1) * N], m.w2[:, b, :], qf[:, b, :],
                                       start=True, stop=True)
                mm.then_inc(out_ready, 1)

        @block.vector
        def _(dve):
            own = sem("la_dve")
            dve.tensor_reduce(m.small[:, 0:1], m.memk[:, :], AXX, ALU.max).then_inc(memmax_ready, 1)
            dve.tensor_scalar(m.gs[:, :], m.gcol[:, :], float(C) ** 0.5, None, ALU.mult).then_inc(own, 1)
            dve.wait_ge(norm_ready, 1)
            dve.tensor_scalar(m.rstd[0:B, N:2 * N], m.rstd[0:B, N:2 * N], 1e-12, None, ALU.max).then_inc(inv_ready, 1)
            dve.wait_ge(inv_ready, 1)
            dve.reciprocal(m.rstd[0:B, 0:N], m.rstd[0:B, N:2 * N]).then_inc(inv_ready, 1)
            dve.wait_ge(own, 1)
            for k in range(NCH):
                c = slice(k * CH, (k + 1) * CH)
                dve.wait_ge(spread, 2 * (k + 1))
                dve.scalar_tensor_tensor(xn[:, c], m.z[:, c], m.gs[:, 0:1], ps[:, k, :],
                                         ALU.mult, ALU.mult).then_inc(xn_ready, 1)
            dve.wait_ge(memmax_ready, 1)
            for u in range(UN):
                j, g = unit(u)
                b = j * G + g
                dve.wait_ge(proj_ready, u + 1)
                dve.tensor_reduce(m.kmax[:, b:b + 2], ps[:, j, :].rearrange("p (a n) -> p a n", a=2),
                                  AXX, ALU.max).then_inc(kmax_ready, 1)
                dve.wait_ge(kmax_ready, u + 1)
                dve.tensor_scalar(m.knegmax[:, b:b + 2], m.kmax[:, b:b + 2], m.small[:, 0:1], -1.0,
                                  ALU.max, ALU.mult).then_inc(knegmax_ready, 1)
            dve.wait_ge(knegmax_ready, UN)
            dve.tensor_tensor(m.em[:, :].rearrange("p (b m) -> p b m", m=MEM),
                              m.memk[:, None, :].broadcast_to([128, B, MEM]),
                              m.knegmax[:, :, None].broadcast_to([128, B, MEM]), ALU.add).then_inc(memshift_done, 1)

            def normalise(u):
                j, g = unit(u)
                b = j * G + g
                q = qt[:, b:b + 2, :].rearrange("p b (s h d) -> p (b s h) d", h=HEADS, d=DH)
                st = slice(16 * u, 16 * u + 16)
                dve.wait_ge(qexp_done, u + 1)
                dve.tensor_reduce(m.qsum[:, st], q, AXX, ALU.add).then_inc(qsum_ready, 1)
                dve.wait_ge(qsum_ready, u + 1)
                dve.reciprocal(m.qinv[:, st], m.qsum[:, st]).then_inc(qinv_ready, 1)
                dve.wait_ge(qinv_ready, u + 1)
                dve.tensor_tensor(q, q, m.qinv[:, st].unsqueeze(2).broadcast_to([128, 16, DH]),
                                  ALU.mult).then_inc(qnorm_done, 1)

            for u in range(UN):
                j, g = unit(u)
                b = j * G + g
                p = ps[:, j, :].rearrange("p (a d) -> p a d", d=DH)
                st = slice(16 * u, 16 * u + 16)
                dve.wait_ge(proj_ready, 2 * UN + u + 1)
                dve.tensor_reduce(m.qmax[:, st], p, AXX, ALU.max).then_inc(qmax_ready, 1)
                dve.wait_ge(qmax_ready, u + 1)
                q = qt[:, b:b + 2, :].rearrange("p b (s h d) -> p (b s h) d", h=HEADS, d=DH)
                dve.tensor_tensor(q, p, m.qmax[:, st].unsqueeze(2).broadcast_to([128, 16, DH]),
                                  ALU.subtract).then_inc(qsub_done, 1)
                if u >= 1:
                    normalise(u - 1)
            normalise(UN - 1)
            dve.wait_ge(memexp_done, 1)
            dve.tensor_reduce(m.memsum[:, :], m.em[:, :].rearrange("p (b m) -> p b m", m=MEM), AXX,
                              ALU.add).then_inc(memsum, 1)
            dve.wait_ge(memsum, 1)
            dve.wait_ge(kexp_done, 2 * UN)
            dve.tensor_tensor(m.ksum[:, :], m.ksum[:, :], m.memsum[:, :], ALU.add).then_inc(memsum, 1)
            dve.wait_ge(memsum, 2)
            dve.reciprocal(m.ksum[:, :], m.ksum[:, :]).then_inc(memsum, 1)
            dve.wait_ge(memsum, 3)
            dve.tensor_scalar(m.ksum[:, :], m.ksum[:, :], float(DH) ** -0.5, None, ALU.mult).then_inc(memsum, 1)
            for q in range(B // 4):
                dve.wait_ge(ctx_ready, q + 1)
                dve.tensor_tensor(m.ct[:, 4 * q:4 * q + 4, :], ps[:, q % 4, :].rearrange("p (b d) -> p b d", b=4),
                                  m.blkone[:, None, :].broadcast_to([128, 4, 128]), ALU.mult).then_inc(ctx_copied, 1)
            dve.wait_ge(memsum, 4)
            dve.wait_ge(w2_ready, 1)
            dve.tensor_tensor(m.w2[:, :, :], ps[:, 4:6, :].rearrange("p a (b c) -> p (a b) c", c=C),
                              m.ksum[:, :, None].broadcast_to([128, B, C]), ALU.mult).then_inc(w2_scaled, 1)
            for k in range(NCH):
                c = slice(k * CH, (k + 1) * CH)
                dve.wait_ge(out_ready, k + 1)
                dve.scalar_tensor_tensor(m.x[:, c], ps[:, k, :], m.bout[:, 0:1], m.x[:, c],
                                         ALU.add, ALU.add).then_inc(added, 1)

        @block.scalar
        def _(act):
            for k in range(NCH):
                c = slice(k * CH, (k + 1) * CH)
                act.activation(m.tmpB[:, c], m.z[:, c], ACT.Square).then_inc(squared, 1)
            act.wait_ge(norm2_ready, 1)
            act.activation(m.rstd[0:B, N:2 * N], ps[0:B, 4, 0:N], ACT.Sqrt).then_inc(norm_ready, 1)

            def copy_transposed(p, u):
                j, g = unit(u)
                b = j * G + g
                ready, dst, done = (kt_ready, ekt, kt_copied) if p == 0 else (qt_ready, qf, qt_copied)
                act.wait_ge(ready, u + 1)
                act.activation(dst[:, b:b + 2, :].rearrange("p b n -> p (b n)"), ps[:, 4 + j, :],
                               ACT.Copy).then_inc(done, 1)

            for u in range(UN + 5):
                if u < UN:
                    j, g = unit(u)
                    act.wait_ge(knegmax_ready, u + 1)
                    for i in range(2):
                        b = j * G + g + i
                        act.activation(ek[:, b, :], ps[:, j, i * N:(i + 1) * N], ACT.Exp, bias=m.knegmax[:, b:b + 1],
                                       accum_out=m.ksum[:, b:b + 1]).then_inc(kexp_done, 1)
                if u >= 5:
                    copy_transposed(0, u - 5)
            act.wait_ge(memshift_done, 1)
            act.activation(m.em[:, :], m.em[:, :], ACT.Exp).then_inc(memexp_done, 1)
            for u in range(UN):
                j, g = unit(u)
                b = j * G + g
                act.wait_ge(proj_ready, UN + u + 1)
                act.activation(vt[:, b:b + 2, :].rearrange("p b n -> p (b n)"), ps[:, j, :],
                               ACT.Copy).then_inc(v_copied, 1)
                if u == 6:
                    act.wait_ge(memt_ready, 1)
                    act.activation(m.emt[:, :], ps[:, 4, 0:128], ACT.Copy).then_inc(memt_copied, 1)
            for u in range(UN + 6):
                if u < UN:
                    j, g = unit(u)
                    b = j * G + g
                    act.wait_ge(qsub_done, u + 1)
                    q = qt[:, b:b + 2, :].rearrange("p b n -> p (b n)")
                    act.activation(q, q, ACT.Exp).then_inc(qexp_done, 1)
                if u >= 6:
                    copy_transposed(1, u - 6)

        @block.gpsimd
        def _(pool):
            pool.tensor_tensor(m.memv_b[:, :, :], m.memv[:, None, :].broadcast_to([128, B, 128]),
                               m.memmask[:, :, None].broadcast_to([128, B, 128]), ALU.mult).then_inc(memv_masked, 1)


def peripheral_convolution(nc, m, sem, d):
    ps = m.ps
    zt = m.tmpA
    T = m.big
    yt_ready = sem("cv_zt_ready")
    yt_copied = sem("cv_zt_copied")
    classes = sem("cv_classes")
    stored = sem("cv_stored")
    loaded = sem("cv_loaded")
    t_ready = sem("cv_t_ready")
    t_copied_a = sem("cv_t_copied_a")
    t_copied_v = sem("cv_t_copied_v")
    turned = sem("cv_turned")
    turned_copied = sem("cv_turned_copied")
    made = sem("cv_made")
    rel_loaded = sem("cv_rel_loaded")
    out_ready = sem("cv_out_ready")
    out_copied = sem("cv_out_copied")
    out_stored = sem("cv_out_stored")
    out_loaded = sem("cv_out_loaded")
    added = sem("cv_added")
    NT = H * S

    with nc.Block() as block:
        @block.sync
        def _(sp):
            sp.wait_ge(classes, CLASSES)
            sp.dma_start(m.scratch_w, m.wclass[:, :, :]).then_inc(stored, 16)
            sp.wait_ge(stored, 16)
            for half, dst in enumerate((m.bl, m.br)):
                for q in range(8):
                    src = bass.AP(tensor=m.scratch_w.tensor, offset=m.scratch_w.offset + (q + half) * (2 * R + 1),
                                  ap=[[1, W], [CLASSES * (2 * R + 1), C], [1, W]])
                    sp.dma_start(dst[16 * q:16 * q + 16, :, :], src).then_inc(loaded, 16)
            sp.wait_ge(turned_copied, 1)
            last = d.pos_w.shape[0] - 1
            for s in range(S):
                sp.dma_start(m.relt[:, s, :], toeplitz_rows(d.pos_w, last - (N - 1) - 128 * s - 127, 1,
                                                            (128, [[1, N]]))).then_inc(rel_loaded, 16)
            for h in range(2):
                sp.wait_ge(out_copied, 4 * (h + 1))
                for cc in range(4):
                    dst = m.scratch_x.rearrange("b (ci cc) n -> cc b ci n", cc=4)[cc]
                    sp.dma_start(dst[:, 4 * h:4 * h + 4, :], m.co[32 * cc:32 * cc + 32, 4 * h:4 * h + 4, :])\
                        .then_inc(out_stored, 16)
            sp.wait_ge(out_stored, 8 * 16)
            for j in range(J):
                sp.dma_start(m.tmpB[32 * j:32 * j + 32, :].rearrange("c (g n) -> c g n", g=G),
                             m.scratch_x.rearrange("(g j) c n -> j c g n", j=J)[j]).then_inc(out_loaded, 16)

        @block.gpsimd
        def _(pool):
            wc = m.wcomp[:, :].rearrange("c (a b) -> c a b", a=CONV_P)
            for q, (lo, hi) in enumerate(CLASS_SPANS):
                n = hi - lo + 1
                pool.tensor_copy(m.wclass[:, :, R - hi:R - lo + 1],
                                 wc[:, CLASS0:CLASS0 + CLASSES, CLASS0 + q:CLASS0 + q + 1]
                                 .broadcast_to([C, CLASSES, n])).then_inc(classes, 1)

        @block.tensor
        def _(pe):
            for q in range(NCH):
                for i in range(4):
                    t = 4 * q + i
                    mm = pe.transpose(ps[:, q, i * 128:(i + 1) * 128], m.z[:, t * 128:(t + 1) * 128], m.ident[:, :])
                mm.then_inc(yt_ready, 1)
            pe.matmul(ps[:, 4, :], m.exchange[:, :], m.kmat_rev[:, :, :].rearrange("p s n -> p (s n)"),
                      start=True, stop=True).then_inc(turned, 1)
            pe.wait_ge(loaded, 16 * 16)
            for w in range(NT):
                y, s = divmod(w, S)
                if w < 4:
                    pe.wait_ge(yt_copied, w + 1)
                else:
                    pe.wait_ge(t_copied_a if w % 2 == 0 else t_copied_v, (w - 4) // 2 + 1)
                onehot, weights = ((m.ol, m.bl), (m.orr, m.br))[s]
                pe.matmul(ps[:, w % 4, :], onehot[:, (R - y) * W:(R - y + 8) * W],
                          weights[:, :, :].rearrange("p c x -> p (c x)"), start=True, stop=True).then_inc(t_ready, 1)
            pe.wait_ge(t_copied_a, NT // 2)
            pe.wait_ge(t_copied_v, NT // 2)
            pe.wait_ge(rel_loaded, 16 * S)
            pe.matmul(ps[:, 5, :], m.exchange[:, :], m.relt[:, :, :].rearrange("p s n -> p (s n)"),
                      start=True, stop=True).then_inc(turned, 1)
            for ci in range(C // 4):
                if ci == 1:
                    pe.wait_ge(turned_copied, 2)
                for cc in range(4):
                    c = 4 * ci + cc
                    o = ps[32 * cc:32 * cc + 32, (4 + ci) % 8, 0:N]
                    for s in range(S):
                        lhsT = zt[:, s * G * 128 + c:(s + 1) * G * 128:C]
                        rhs = T[:, s, :, :].rearrange("p y (c x) -> p y c x", c=C)[:, :, c, :]
                        pe.matmul(o, lhsT, rhs, start=(s == 0), stop=False)
                        mm = pe.matmul(o, lhsT, m.kmat[:, s, :], start=False, stop=(s == S - 1))
                mm.then_inc(out_ready, 1)

        @block.scalar
        def _(act):
            for q in range(NCH):
                act.wait_ge(yt_ready, q + 1)
                act.activation(zt[:, :].rearrange("p (s g x) -> p g s x", s=S, g=G)[:, 2 * q:2 * q + 2],
                               ps[:, q, :].rearrange("p (g s x) -> p g s x", g=2, s=S),
                               ACT.Copy).then_inc(yt_copied, 1)
            for w in range(0, NT, 2):
                y, s = divmod(w, S)
                act.wait_ge(t_ready, w + 1)
                act.activation(T[:, s, y, :], ps[:, w % 4, :], ACT.Copy).then_inc(t_copied_a, 1)
            for ci in range(C // 4):
                act.wait_ge(out_ready, ci + 1)
                act.activation(m.co[:, ci, :], ps[:, (4 + ci) % 8, 0:N],
                               ACT.Copy).then_inc(out_copied, 1)

        @block.vector
        def _(dve):
            dve.wait_ge(turned, 1)
            dve.tensor_copy(m.kmat[:, :, :].rearrange("p s n -> p (s n)"), ps[:, 4, :]).then_inc(turned_copied, 1)
            for w in range(1, NT, 2):
                y, s = divmod(w, S)
                dve.wait_ge(t_ready, w + 1)
                dve.tensor_copy(T[:, s, y, :], ps[:, w % 4, :]).then_inc(t_copied_v, 1)
            dve.wait_ge(turned, 2)
            dve.tensor_copy(m.relt[:, :, :].rearrange("p s n -> p (s n)"), ps[:, 5, :]).then_inc(turned_copied, 1)
            prepare(dve, m, made)
            dve.wait_ge(out_loaded, 16 * J)
            for k in range(NCH):
                c = slice(k * CH, (k + 1) * CH)
                dve.tensor_tensor(m.x[:, c], m.x[:, c], m.tmpB[:, c], ALU.add).then_inc(added, 1)


def linear_transformer(nc, m, sem):
    ps = m.ps
    zt = m.tmpA
    zt_ready = sem("lt_zt_ready")
    zt_copied = sem("lt_zt_copied")
    g_ready = sem("lt_g_ready")
    g_masked = sem("lt_g_masked")
    p_ready = sem("lt_p_ready")
    p_copied = sem("lt_p_copied")
    m_ready = sem("lt_m_ready")
    a_made = sem("lt_a_made")
    abd_made = sem("lt_abd_made")
    r_ready = sem("lt_r_ready")
    r_copied = sem("lt_r_copied")
    wt_ready = sem("lt_wt_ready")
    wt_copied = sem("lt_wt_copied")
    wbd_made = sem("lt_wbd_made")
    w_ready = sem("lt_w_ready")
    w_copied = sem("lt_w_copied")
    out_ready = sem("lt_out_ready")
    added = sem("lt_added")
    gbd, abd = m.gbd, m.abd

    def spread(dve, dst, src, done):
        for j in range(J):
            ins = dve.tensor_tensor(dst[:, :, 32 * j:32 * j + 32], src,
                                    m.blkone[:, None, 32 * j:32 * j + 32].broadcast_to([128, G, 32]), ALU.mult)
            ins.then_inc(done, 1)

    with nc.Block() as block:
        @block.tensor
        def _(pe):
            for q in range(NCH):
                for i in range(4):
                    t = 4 * q + i
                    mm = pe.transpose(ps[:, q, i * 128:(i + 1) * 128], m.z[:, t * 128:(t + 1) * 128], m.ident[:, :])
                mm.then_inc(zt_ready, 1)
            for g in range(G):
                if g % 2 == 0:
                    pe.wait_ge(zt_copied, g // 2 + 1)
                for s in range(S):
                    t = 2 * g + s
                    mm = pe.matmul(ps[:, 4 + g // 4, (g % 4) * 128:(g % 4) * 128 + 128],
                                   zt[:, t * 128:(t + 1) * 128], zt[:, t * 128:(t + 1) * 128],
                                   start=(s == 0), stop=(s == S - 1))
            mm.then_inc(g_ready, 1)
            for L in range(LAYERS):
                pe.wait_ge(g_masked, 2 if L == 0 else 2 + J * L)
                for g in range(G):
                    mm = pe.matmul(ps[:, g // 2, (g % 2) * 256:(g % 2) * 256 + 256], gbd[:, g, :],
                                   m.vt4[:, L * 256:(L + 1) * 256], start=True, stop=True)
                    if g % 2:
                        mm.then_inc(p_ready, 1)
                pe.wait_ge(p_copied, NCH * (L + 1))
                for h in range(ZHEADS):
                    mm = pe.matmul(ps[:, 4, 0:256], m.qbd[:, L, h, :],
                                   m.pmat[:, :, h * 32:(h + 1) * 32], start=(h == 0), stop=(h == ZHEADS - 1))
                mm.then_inc(m_ready, 1)
                pe.wait_ge(abd_made, J * (L + 1))
                if L > 0:
                    pe.wait_ge(wt_copied, L)
                if L < LAYERS - 1:
                    for g in range(G):
                        mm = pe.matmul(ps[:, 5, g * 32:(g + 1) * 32], gbd[:, g, :], m.amat[:, g, :],
                                       start=True, stop=True)
                    mm.then_inc(r_ready, 1)
                for g in range(G):
                    mm = pe.matmul(ps[:, 6, g * 32:(g + 1) * 32], abd[:, g, :], m.wt[:, g, :],
                                   start=True, stop=True)
                mm.then_inc(wt_ready, 1)
                if L < LAYERS - 1:
                    pe.wait_ge(r_copied, L + 1)
                    for g in range(G):
                        mm = pe.matmul(ps[:, 7, g * 32:(g + 1) * 32], abd[:, g, :], m.rmat[:, g, :],
                                       start=True, stop=True)
                    mm.then_inc(g_ready, 1)
            pe.wait_ge(wbd_made, J)
            for g in range(G):
                mm = pe.transpose(ps[:, g // 4, (g % 4) * 128:(g % 4) * 128 + 128], abd[:, g, :], m.ident[:, :])
            mm.then_inc(w_ready, 1)
            pe.wait_ge(w_copied, 2)
            for k in range(NCH):
                for h in range(2):
                    g = 2 * k + h
                    mm = pe.matmul(ps[:, 2 + k, h * N:(h + 1) * N], gbd[:, g, :], m.z[:, g * N:(g + 1) * N],
                                   start=True, stop=True)
                mm.then_inc(out_ready, 1)

        @block.vector
        def _(dve):
            dve.wait_ge(g_ready, 1)
            for h in range(2):
                dve.tensor_tensor(gbd[:, 4 * h:4 * h + 4, :], ps[:, 4 + h, :].rearrange("p (g d) -> p g d", g=4),
                                  m.blkone[:, None, :].broadcast_to([128, 4, 128]), ALU.mult).then_inc(g_masked, 1)
            for L in range(LAYERS):
                dve.wait_ge(m_ready, L + 1)
                if L > 0:
                    dve.wait_ge(wt_ready, L)
                    dve.wait_ge(g_ready, L + 1)
                    dve.wait_ge(g_masked, 2 + J * L)
                dve.scalar_tensor_tensor(m.amat[:, :, :], ps[:, 4, 0:256].rearrange("p (g d) -> p g d", g=G),
                                         1.0 / (N * ZHEADS), m.ident32[:, None, :].broadcast_to([128, G, 32]),
                                         ALU.mult, ALU.add).then_inc(a_made, 1)
                dve.wait_ge(a_made, L + 1)
                spread(dve, abd, m.amat[:, :, :], abd_made)
                if L < LAYERS - 1:
                    dve.wait_ge(g_ready, L + 2)
                    spread(dve, gbd, ps[:, 7, 0:256].rearrange("p (g d) -> p g d", g=G), g_masked)
            dve.wait_ge(wt_copied, LAYERS)
            spread(dve, abd, m.wt[:, :, :], wbd_made)
            dve.wait_ge(w_ready, 1)
            for h in range(2):
                dve.tensor_copy(gbd[:, 4 * h:4 * h + 4, :].rearrange("p g d -> p (g d)"),
                                ps[:, h, :]).then_inc(w_copied, 1)
            for k in range(NCH):
                c = slice(k * CH, (k + 1) * CH)
                dve.wait_ge(out_ready, k + 1)
                dve.tensor_tensor(m.x[:, c], m.x[:, c], ps[:, 2 + k, :], ALU.add).then_inc(added, 1)

        @block.scalar
        def _(act):
            for q in range(NCH):
                act.wait_ge(zt_ready, q + 1)
                act.activation(zt[:, q * CH:(q + 1) * CH], ps[:, q, :], ACT.Copy).then_inc(zt_copied, 1)
            for L in range(LAYERS):
                for q in range(NCH):
                    act.wait_ge(p_ready, NCH * L + q + 1)
                    act.activation(m.pmat[:, 2 * q:2 * q + 2, :].rearrange("p g d -> p (g d)"), ps[:, q, :],
                                   ACT.Copy).then_inc(p_copied, 1)
                if L < LAYERS - 1:
                    act.wait_ge(r_ready, L + 1)
                    act.activation(m.rmat[:, :, :].rearrange("p g d -> p (g d)"), ps[:, 5, 0:256],
                                   ACT.Copy).then_inc(r_copied, 1)
                act.wait_ge(wt_ready, L + 1)
                act.activation(m.wt[:, :, :].rearrange("p g d -> p (g d)"), ps[:, 6, 0:256],
                               ACT.Copy).then_inc(wt_copied, 1)


def mixture_of_experts(nc, m, sem):
    ps = m.ps
    z = m.z
    NT = G * S * J
    logits_ready = sem("me_logits_ready")
    steps = sem("me_steps")
    exp_done = sem("me_exp_done")
    parts_made = sem("me_parts_made")
    gt_ready = sem("me_gt_ready")
    gt_copied = sem("me_gt_copied")
    gate_ready = sem("me_gate_ready")
    gated = sem("me_gated")
    out_ready = sem("me_out_ready")
    added = sem("me_added")

    def lots(t):
        return t.rearrange("p (t e) -> p t e", e=E)

    with nc.Block() as block:
        @block.tensor
        def _(pe):
            for t in range(G * S):
                mm = pe.matmul(ps[:, 0, t * 32:(t + 1) * 32], z[:, t * 128:(t + 1) * 128], m.rwbd[:, :],
                               start=True, stop=True)
            mm.then_inc(logits_ready, 1)
            pe.wait_ge(parts_made, 4)
            gt_ps = ps[:, 1:3, :].rearrange("p a n -> p (a n)").bitcast(BF16)
            for t in range(G * S):
                mm = pe.transpose(gt_ps[:, t * 128:(t + 1) * 128], m.gparts[:, t, :, :].rearrange("p a e -> p (a e)"),
                                  m.identb[:, :])
                if t % 8 == 7:
                    mm.then_inc(gt_ready, 1)
            pe.wait_ge(gt_copied, 2)

            def gate(w):
                e, k = w % E, w // E
                if w >= 3:
                    pe.wait_ge(gated, w - 2)
                pe.matmul(ps[:, 3 + w % 3, :], m.sele[:, e, :],
                          m.gt[:, k * CH:(k + 1) * CH], start=True, stop=True).then_inc(gate_ready, 1)

            gate(0)
            gate(1)
            for w in range(E * NCH):
                e, k = w % E, w // E
                if w + 2 < E * NCH:
                    gate(w + 2)
                if e == 0:
                    if k >= 2:
                        pe.wait_ge(added, k - 1)
                    for i in range(3):
                        pe.matmul(ps[:, 6 + k % 2, :], m.ebbd[:, i, :], m.gt[:, k * CH:(k + 1) * CH],
                                  start=(i == 0), stop=False)
                pe.wait_ge(gated, w + 1)
                mm = pe.matmul(ps[:, 6 + k % 2, :], m.ewbd[:, e, :], m.gz[:, w % 3, :], start=False, stop=(e == E - 1))
                mm.then_inc(out_ready, 1)

        def add(dve, k):
            c = slice(k * CH, (k + 1) * CH)
            dve.wait_ge(out_ready, E * (k + 1))
            dve.tensor_tensor(m.x[:, c], m.x[:, c], ps[:, 6 + k % 2, :], ALU.add).then_inc(added, 1)

        @block.vector
        def _(dve):
            n = 0

            def step(ins):
                nonlocal n
                ins.then_inc(steps, 1)
                n += 1
                dve.wait_ge(steps, n)

            l, k, one, sel = (lots(t) for t in (m.lg, m.key, m.one1, m.sel2))
            bc = [128, NT, E]
            st = m.stat
            dve.wait_ge(logits_ready, 1)
            step(dve.tensor_tensor(l, lots(ps[:, 0, :]), m.rb[:, None, :].broadcast_to(bc), ALU.add))
            step(dve.tensor_reduce(st[:, 0, :], l, AXX, ALU.max))
            mx = st[:, 0, :].unsqueeze(2).broadcast_to(bc)
            rank = m.rank[:, None, :].broadcast_to(bc)
            step(dve.tensor_tensor(k, l, mx, ALU.is_ge))
            step(dve.tensor_tensor(k, k, rank, ALU.mult))
            step(dve.tensor_reduce(st[:, 1, :], k, AXX, ALU.max))
            step(dve.tensor_tensor(one, k, st[:, 1, :].unsqueeze(2).broadcast_to(bc), ALU.is_equal))
            step(dve.tensor_scalar(sel, one, -1.0, 1.0, ALU.mult, ALU.add))
            step(dve.tensor_tensor(sel, sel, l, ALU.mult))
            step(dve.scalar_tensor_tensor(k, one, -3.0e38, sel, ALU.mult, ALU.add))
            step(dve.tensor_reduce(st[:, 3, :], k, AXX, ALU.max))
            step(dve.tensor_tensor(k, k, st[:, 3, :].unsqueeze(2).broadcast_to(bc), ALU.is_ge))
            step(dve.tensor_tensor(k, k, rank, ALU.mult))
            step(dve.tensor_reduce(st[:, 1, :], k, AXX, ALU.max))
            step(dve.tensor_tensor(sel, k, st[:, 1, :].unsqueeze(2).broadcast_to(bc), ALU.is_equal))
            step(dve.tensor_tensor(sel, sel, one, ALU.add))
            step(dve.tensor_tensor(l, l, mx, ALU.subtract))
            dve.wait_ge(exp_done, 1)
            step(dve.tensor_tensor(sel, sel, l, ALU.mult))
            step(dve.tensor_reduce(st[:, 1, :], sel, AXX, ALU.add))
            step(dve.reciprocal(st[:, 2, :], st[:, 1, :]))
            step(dve.tensor_tensor(sel, sel, st[:, 2, :].unsqueeze(2).broadcast_to(bc), ALU.mult))
            g4 = m.sel2[:, :].rearrange("p (t e) -> p t e", t=G * S)
            r4 = m.key[:, :].rearrange("p (t e) -> p t e", t=G * S)
            dve.tensor_copy(m.gparts[:, :, 0, :], g4).then_inc(parts_made, 1)
            dve.wait_ge(parts_made, 2)
            step(dve.tensor_tensor(r4, g4, m.gparts[:, :, 0, :], ALU.subtract))
            dve.tensor_copy(m.gparts[:, :, 1, :], r4).then_inc(parts_made, 1)
            dve.wait_ge(parts_made, 3)
            step(dve.tensor_tensor(r4, r4, m.gparts[:, :, 1, :], ALU.subtract))
            dve.tensor_copy(m.gparts[:, :, 2, :], r4).then_inc(parts_made, 1)
            for w in range(E * NCH):
                kk = w // E
                dve.wait_ge(gate_ready, w + 1)
                if w >= 3:
                    dve.wait_ge(out_ready, w - 2)
                dve.tensor_tensor(m.gz[:, w % 3, :], z[:, kk * CH:(kk + 1) * CH], ps[:, 3 + w % 3, :],
                                  ALU.mult).then_inc(gated, 1)
                if w % E == 3 and kk >= 1:
                    add(dve, kk - 1)
            add(dve, NCH - 1)

        @block.scalar
        def _(act):
            act.wait_ge(steps, 16)
            act.activation(m.lg[:, :], m.lg[:, :], ACT.Exp).then_inc(exp_done, 1)
            gt_ps = ps[:, 1:3, :].rearrange("p a n -> p (a n)").bitcast(BF16)
            for h in range(2):
                act.wait_ge(gt_ready, h + 1)
                act.activation(m.gt[:, h * 1024:(h + 1) * 1024], gt_ps[:, h * 1024:(h + 1) * 1024],
                               ACT.Copy).then_inc(gt_copied, 1)

        @block.gpsimd
        def _(pool):
            pool.memset(m.gparts[:, :, 3, :], 0.0).then_inc(parts_made, 1)


def squared_attention(nc, m, sem):
    ps = m.ps
    z = m.z
    vm = m.vm
    vtok = m.tmpA
    exact = [m.tmpB, m.rstd]
    projected = sem("sa_projected")
    silu_done = sem("sa_silu_done")
    cast_done = sem("sa_cast_done")
    split = sem("sa_split")
    stacked = sem("sa_stacked")
    sel_loaded = sem("sa_sel_loaded")
    sel_made = sem("sa_sel_made")
    arranged_ready = sem("sa_arranged_ready")
    arranged = [sem("sa_q_arranged"), sem("sa_k_arranged")]
    v_ready = sem("sa_v_ready")
    v_biased = sem("sa_v_biased")
    v_done = sem("sa_v_done")
    v_masked = sem("sa_v_masked")
    pos_ready = sem("sa_pos_ready")
    pos_copied = sem("sa_pos_copied")
    scores_ready = sem("sa_scores_ready")
    causal_done = sem("sa_causal_done")
    below_squared = sem("sa_below_squared")
    diag_squared = [sem("sa_diag_squared_v"), sem("sa_diag_squared_p")]
    act_done = sem("sa_act_done")
    pv_ready = sem("sa_pv_ready")
    pv_copied = sem("sa_pv_copied")
    order = [(g, j) for g in range(G) for j in range(J)]
    NU = B * AH // 2
    SLOTS = 6
    LAG = 4
    NPART = 3
    arrangement = [(k, j, hp, x) for k in range(NCH) for j in range(J) for hp in range(2) for x in range(2)]

    def arranged_to(w):
        k, j, hp, x = arrangement[w]
        b = j * G + 2 * k
        return m.qkt[:, x, hp, b:b + 2, :].rearrange("p b n -> p (b n)")

    def diagonal(u):
        return m.att[:, u % SLOTS, :, :].rearrange("p k (d n) -> p k d n", n=128)[:, :, 0::2, :]

    with nc.Block() as block:
        @block.sync
        def _(sp):
            sp.dma_start(m.selqk32[:, :], m.d_selqk).then_inc(sel_loaded, 16)
            for x in range(2):
                for p in range(NPART):
                    if p == 0:
                        sp.wait_ge(cast_done, NCH * (x + 1))
                    else:
                        sp.wait_ge(split, NCH * (3 * x + 2) if p == 1 else 3 * NCH * (x + 1))
                    for j in range(J):
                        sp.dma_start(m.qkstack[32 * p:32 * p + 32, x, j, :],
                                     m.qkparts[32 * j:32 * j + 32, x, p, :]).then_inc(stacked, 16)

        @block.tensor
        def _(pe):
            for x in range(2):
                for k in range(NCH):
                    pe.matmul(ps[:, NCH * x + k, :], m.wqkbd[:, x, :], z[:, k * CH:(k + 1) * CH],
                              start=True, stop=True).then_inc(projected, 1)
            for t in range(G * S):
                if t % 4 == 0:
                    pe.wait_ge(silu_done, NCH + t // 4 + 1)
                mm = pe.matmul(ps[:, 4 + t // 4, (t % 4) * 128:(t % 4) * 128 + 128], z[:, t * 128:(t + 1) * 128],
                               m.wvbd[:, :], start=True, stop=True)
                if t % 4 == 3:
                    mm.then_inc(v_ready, 1)
            pe.wait_ge(v_done, NCH)
            for g in range(G):
                for s in range(S):
                    mm = pe.matmul(ps[:, 4 + g // 2, (g % 2) * N:(g % 2) * N + N],
                                   vtok[:, (2 * g + s) * 128:(2 * g + s + 1) * 128], m.relt[:, s, :],
                                   start=(s == 0), stop=(s == S - 1))
                if g % 2:
                    mm.then_inc(pos_ready, 1)
            pe.wait_ge(sel_made, 1)
            pe.wait_ge(stacked, 16 * 2 * NPART * J)
            for w, (k, j, hp, x) in enumerate(arrangement):
                if w >= 4:
                    pe.wait_ge(arranged[x], (w - 4) // 2 + 1)
                pe.matmul(ps[:, w % 4, :], m.selqk[0:32 * NPART, x, hp, :],
                          m.qkstack[0:32 * NPART, x, j, k * CH:(k + 1) * CH],
                          start=True, stop=True).then_inc(arranged_ready, 1)

            def scores(u):
                g, j = order[u // 2]
                b = j * G + g
                if u == 2:
                    pe.wait_ge(pos_copied, NCH)
                if u >= 3:
                    pe.wait_ge(causal_done, u - 2)
                    pe.wait_ge(below_squared, u - 2)
                for s in range(S):
                    for k in range(2):
                        rows = slice(64 * k, 64 * k + 64)
                        mm = pe.matmul(ps[:, 2 * (u % 3) + k, s * N:N + s * 128],
                                       m.qkt[rows, 1, u % 2, b, s * 128:(s + 1) * 128],
                                       m.qkt[rows, 0, u % 2, b, s * 128:N], start=True, stop=True)
                mm.then_inc(scores_ready, 1)

            def values(u):
                g, j = order[u // 2]
                if u % (2 * J) == 0 and g >= 2:
                    pe.wait_ge(pv_copied, g - 1)
                pe.wait_ge(act_done, u + 1)
                rows = slice(32 * j, 32 * j + 32)
                for k in range(2):
                    h = 2 * (u % 2) + k
                    pe.matmul(ps[rows, 6 + g % 2, 0:N], vm[:, (2 * g) * J + j, h, :], m.att[:, u % SLOTS, k, 0:N],
                              start=(h == 0), stop=False)
                    mm = pe.matmul(ps[rows, 6 + g % 2, 128:N], vm[:, (2 * g + 1) * J + j, h, :],
                                   m.att[:, u % SLOTS, k, N:N + 128], start=False, stop=(h == AH - 1))
                mm.then_inc(pv_ready, 1)

            pe.wait_ge(arranged[0], len(arrangement) // 2)
            pe.wait_ge(arranged[1], len(arrangement) // 2)
            for u in range(NU + LAG):
                if u < NU:
                    scores(u)
                if u == LAG:
                    pe.wait_ge(v_masked, 1)
                if u >= LAG:
                    values(u - LAG)

        def copy_out(dve, g):
            dve.wait_ge(pv_ready, 2 * J * (g + 1))
            dve.tensor_copy(m.sa[:, g * N:(g + 1) * N], ps[:, 6 + g % 2, 0:N]).then_inc(pv_copied, 1)

        @block.vector
        def _(dve):
            for x in range(2):
                for k in range(NCH):
                    c = slice(k * CH, (k + 1) * CH)
                    n = 3 * NCH * x
                    dve.wait_ge(cast_done, NCH * x + k + 1)
                    dve.tensor_tensor(exact[x][:, c], exact[x][:, c], m.qkparts[:, x, 0, c],
                                      ALU.subtract).then_inc(split, 1)
                    dve.wait_ge(split, n + 2 * k + 1)
                    dve.tensor_copy(m.qkparts[:, x, 1, c], exact[x][:, c]).then_inc(split, 1)
                for k in range(NCH):
                    c = slice(k * CH, (k + 1) * CH)
                    dve.wait_ge(split, n + 2 * k + 2)
                    dve.tensor_tensor(m.qkparts[:, x, 2, c], exact[x][:, c], m.qkparts[:, x, 1, c],
                                      ALU.subtract).then_inc(split, 1)
            for k in range(NCH):
                dve.wait_ge(v_ready, k + 1)
                dve.tensor_tensor(vtok[:, k * CH:(k + 1) * CH].rearrange("p (a d) -> p a d", d=32),
                                  ps[:, 4 + k, :].rearrange("p (a d) -> p a d", d=32),
                                  m.bv[:, None, :].broadcast_to([128, 16, 32]), ALU.add).then_inc(v_biased, 1)
            for k in range(NCH):
                dve.wait_ge(pos_ready, k + 1)
                dve.tensor_copy(m.pa[:, k * CH:(k + 1) * CH], ps[:, 4 + k, :]).then_inc(pos_copied, 1)
            for w in range(0, len(arrangement), 2):
                dve.wait_ge(arranged_ready, w + 1)
                dve.tensor_copy(arranged_to(w), ps[:, w % 4, :]).then_inc(arranged[0], 1)
            dve.wait_ge(arranged_ready, len(arrangement))
            for u in range(NU):
                dve.wait_ge(scores_ready, u + 1)
                if u >= SLOTS:
                    dve.wait_ge(pv_ready, u - SLOTS + 1)
                dve.tensor_tensor(diagonal(u),
                                  ps[:, 2 * (u % 3):2 * (u % 3) + 2, :]
                                  .rearrange("p k (d n) -> p k d n", n=128)[:, :, 0:3:2, :],
                                  m.causal[:, None, None, :].broadcast_to([128, 2, 2, 128]),
                                  ALU.mult).then_inc(causal_done, 1)
                if u % 2:
                    dve.wait_ge(causal_done, u)
                    dve.tensor_tensor(diagonal(u - 1), diagonal(u - 1), diagonal(u - 1),
                                      ALU.mult).then_inc(diag_squared[0], 1)
                if u % 8 == 7 and u > 8:
                    copy_out(dve, u // 8 - 1)
            copy_out(dve, G - 1)

        @block.scalar
        def _(act):
            for x in range(2):
                for k in range(NCH):
                    c = slice(k * CH, (k + 1) * CH)
                    act.wait_ge(projected, NCH * x + k + 1)
                    act.activation(exact[x][:, c], ps[:, NCH * x + k, :], ACT.Silu,
                                   bias=m.bqk[:, x:x + 1]).then_inc(silu_done, 1)
                    act.wait_ge(silu_done, NCH * x + k + 1)
                    act.activation(m.qkparts[:, x, 0, c], exact[x][:, c], ACT.Copy).then_inc(cast_done, 1)
            for k in range(NCH):
                c = slice(k * CH, (k + 1) * CH)
                act.wait_ge(v_biased, k + 1)
                act.activation(vtok[:, c], vtok[:, c], ACT.Silu).then_inc(v_done, 1)
            for w in range(1, len(arrangement), 2):
                act.wait_ge(arranged_ready, w + 1)
                act.activation(arranged_to(w), ps[:, w % 4, :], ACT.Copy).then_inc(arranged[1], 1)

            def silu(u):
                a = m.att[:, u % SLOTS, :, :].rearrange("p k n -> p (k n)")
                act.wait_ge(diag_squared[u % 2], u // 2 + 1)
                act.wait_ge(below_squared, u + 1)
                act.activation(a, a, ACT.Silu, scale=1.0 / AHD).then_inc(act_done, 1)

            for u in range(NU):
                act.wait_ge(causal_done, u + 1)
                act.activation(m.att[:, u % SLOTS, :, 128:N], ps[:, 2 * (u % 3):2 * (u % 3) + 2, 128:N],
                               ACT.Square).then_inc(below_squared, 1)
                if u >= 2:
                    silu(u - 2)
            silu(NU - 2)
            silu(NU - 1)

        @block.gpsimd
        def _(pool):
            pool.wait_ge(sel_loaded, 16)
            pool.tensor_copy(m.selqk[0:32 * NPART, :, :, :].rearrange("p x a b -> p (x a b)"),
                             m.selqk32[:, :]).then_inc(sel_made, 1)
            pool.wait_ge(v_done, NCH)
            pool.wait_ge(stacked, 16 * 2 * NPART * J)
            pool.tensor_tensor(vm[:, :, :, :], vtok[:, :].rearrange("p (t d) -> p t d", d=32).unsqueeze(2)
                               .broadcast_to([128, G * S * J, AH, 32]),
                               m.headmask[:, None, :, :].broadcast_to([128, G * S * J, AH, 32]),
                               ALU.mult).then_inc(v_masked, 1)
            for u in range(1, NU, 2):
                pool.wait_ge(causal_done, u + 1)
                pool.tensor_tensor(diagonal(u), diagonal(u), diagonal(u), ALU.mult).then_inc(diag_squared[1], 1)

    gamma = [(m.gam[:, i:i + 1], m.bet[:, i:i + 1]) for i in range(2)]
    normalise_tokens(nc, m, sem, "sa_norm", [m.sa, m.pa], [m.sa, m.pa], EPS_A, m.blkmean64, gamma)

    u_ready = sem("sa_u_ready")
    gated = sem("sa_gated")
    f_ready = sem("sa_f_ready")
    relu_done = sem("sa_relu_done")
    summed = sem("sa_summed")
    with nc.Block() as block:
        @block.tensor
        def _(pe):
            for i in range(2):
                for k in range(NCH):
                    pe.matmul(ps[:, 4 * i + k, :], m.wubd[:, i, :], z[:, k * CH:(k + 1) * CH],
                              start=True, stop=True).then_inc(u_ready, 1)
            for k in range(NCH):
                pe.wait_ge(gated, NCH + k + 1)
                for i, part in enumerate((m.sa, m.pa)):
                    mm = pe.matmul(ps[:, k, :], m.wfbd[:, i, :], part[:, k * CH:(k + 1) * CH],
                                   start=(i == 0), stop=(i == 1))
                mm.then_inc(f_ready, 1)

        @block.vector
        def _(dve):
            for i, part in enumerate((m.sa, m.pa)):
                for k in range(NCH):
                    c = slice(k * CH, (k + 1) * CH)
                    dve.wait_ge(u_ready, NCH * i + k + 1)
                    dve.scalar_tensor_tensor(part[:, c], ps[:, 4 * i + k, :], m.bu[:, i:i + 1], part[:, c],
                                             ALU.add, ALU.mult).then_inc(gated, 1)
            for k in range(NCH):
                c = slice(k * CH, (k + 1) * CH)
                dve.tensor_tensor(m.x[:, c], m.x[:, c], z[:, c], ALU.add).then_inc(summed, 1)
            for k in range(NCH):
                c = slice(k * CH, (k + 1) * CH)
                dve.wait_ge(relu_done, k + 1)
                dve.wait_ge(summed, k + 1)
                dve.tensor_tensor(m.x[:, c], m.x[:, c], m.tmpB[:, c], ALU.add).then_inc(summed, 1)

        @block.scalar
        def _(act):
            for k in range(NCH):
                act.wait_ge(f_ready, k + 1)
                act.activation(m.tmpB[:, k * CH:(k + 1) * CH], ps[:, k, :], ACT.Relu,
                               bias=m.bf[:, 0:1]).then_inc(relu_done, 1)


def routed_blocks(nc, m, sem):
    ps = m.ps
    h = m.h
    TOP = 64
    ut, htok, y0 = m.tmpA, m.tmpB, m.sa
    NU = 2 * G
    go = {e: sem("rb_go_" + e) for e in ("sp", "act", "pe")}
    go_dve = sem("rb_go_dve")
    settled = sem("rb_settled")
    probed = sem("rb_probed")
    loaded = sem("rb_loaded")
    NLOAD = 5
    mats_ready = sem("rb_mats_ready")
    mats_masked = sem("rb_mats_masked")
    u_ready = sem("rb_u_ready")
    u_copied = sem("rb_u_copied")
    ht_ready = sem("rb_ht_ready")
    ht_copied = sem("rb_ht_copied")
    s_ready = sem("rb_s_ready")
    max_done = sem("rb_max_done")
    negated = sem("rb_negated")
    exp_done = sem("rb_exp_done")
    t_ready = sem("rb_t_ready")
    t_copied_a = sem("rb_t_copied_a")
    t_copied_v = sem("rb_t_copied_v")
    pv_ready = sem("rb_pv_ready")
    inv_done = sem("rb_inv_done")
    y0_done = sem("rb_y0_done")
    y_ready = sem("rb_y_ready")
    y_copied = sem("rb_y_copied")
    z1_ready = sem("rb_z1_ready")
    relu_a = sem("rb_relu_a")
    relu_v = sem("rb_relu_v")
    z2_ready = sem("rb_z2_ready")
    z2_copied = sem("rb_z2_copied")
    ctl = sem("rb_ctl")
    added = sem("rb_added")
    per_block = [loaded, mats_ready, mats_masked, u_ready, u_copied, ht_ready, ht_copied, s_ready, max_done, negated,
                 exp_done, t_ready, t_copied_a, t_copied_v, pv_ready, inv_done, y0_done, y_ready, y_copied,
                 z1_ready, relu_a, relu_v, z2_ready, z2_copied]

    def state(eng, go_sem, regs):
        eng.wait_ge(go_sem, 1)
        eng.reg_load(regs, m.state[0:1, 0:4])
        eng.sem_clear(go_sem)

    def registers(eng, name):
        return [eng.alloc_register(f"{name}_{r}") for r in ("step", "op", "attends", "feeds")]

    with nc.Block() as block:
        @block.sync
        def _(sp):
            regs = registers(sp, "sp")
            state(sp, go["sp"], regs)
            with sp.While(lambda: sp.snap(regs[0]) < NB):
                at = sp.snap(regs[0], min_val=0, max_val=NB - 1) * NOPS + sp.snap(regs[1], min_val=0, max_val=NOPS - 1)
                at = sp.snap(at, min_val=0, max_val=NB * NOPS - 1)

                def row(t):
                    return t[bass.ds(at, 1)]
                sp.dma_start(m.wsm[:, :, :].rearrange("d k (j c) -> d k j c", j=J),
                             row(m.d_small)[0].rearrange("d (k c) -> d k c", k=4)[:, :, None, :]
                             .broadcast_to([C, 4, J, C])).then_inc(loaded, 16)
                sp.dma_start(m.w1[:, :], row(m.d_w1).broadcast_to([J, C, HID])).then_inc(loaded, 16)
                sp.dma_start(m.w2f[:, :], row(m.d_w2)[0]).then_inc(loaded, 16)
                sp.dma_start(m.b1[:, :], row(m.d_b1)[0]).then_inc(loaded, 16)
                sp.dma_start(m.b2[:, :], row(m.d_b2).broadcast_to([J, C, 1])).then_inc(loaded, 16)
                state(sp, go["sp"], regs)

        @block.tensor
        def _(pe):
            regs = registers(pe, "pe")

            def probe():
                pe.wait_ge(settled, 1)
                pe.transpose(ps[0:1, 0, 0:C], m.hcol[:, 0:1], m.ident[0:C, 0:C]).then_inc(probed, 1)
                pe.sem_clear(settled)

            def attention():
                pe.wait_ge(loaded, 16 * NLOAD)
                for i, (a, b) in enumerate(((0, 1), (2, 3))):
                    mm = pe.matmul(ps[:, i, 0:128], m.wsm[:, a, :], m.wsm[:, b, :],
                                   start=True, stop=True)
                mm.then_inc(mats_ready, 1)
                for q in range(NCH):
                    if q < 2:
                        bank = 2 + q
                    else:
                        bank = q - 2
                        pe.wait_ge(mats_masked, 2)
                    for i in range(4):
                        t = 4 * bank + i
                        mm = pe.transpose(ps[:, bank, i * 128:(i + 1) * 128], h[:, t * 128:(t + 1) * 128], m.ident[:, :])
                    mm.then_inc(ht_ready, 1)
                for k in range(NCH):
                    pe.matmul(ps[:, 4 + k, :], m.sabd[:, :], h[:, k * CH:(k + 1) * CH],
                              start=True, stop=True).then_inc(u_ready, 1)
                def scores(u):
                    g, jp = divmod(u, 2)
                    if u == 0:
                        pe.wait_ge(ht_copied, NCH)
                        pe.wait_ge(u_copied, NCH)
                    if u >= 2:
                        pe.wait_ge(exp_done, 4 * (u - 1))
                    for s in range(S):
                        for i in range(2):
                            rows = slice(32 * (2 * jp + i), 32 * (2 * jp + i) + 32)
                            mm = pe.matmul(ps[:, 2 * (u % 2) + i, s * N:(s + 1) * N],
                                           ut[rows, g * N + s * 128:g * N + (s + 1) * 128],
                                           h[rows, g * N:(g + 1) * N], start=True, stop=True)
                    mm.then_inc(s_ready, 1)

                def transposes(u):
                    pe.wait_ge(exp_done, 4 * (u + 1))
                    if u >= 1:
                        pe.wait_ge(t_copied_a, u)
                        pe.wait_ge(t_copied_v, u)
                    for i in range(2):
                        for s in range(S):
                            for ms in range(S):
                                at = (2 * i + s) * N + ms * 128
                                mm = pe.transpose(ps[:, 4 + i, ms * N + s * 128:ms * N + s * 128 + 128],
                                                  m.ex[:, u % 2, at:at + 128], m.ident[:, :])
                    mm.then_inc(t_ready, 1)

                def values(u):
                    g, jp = divmod(u, 2)
                    if jp == 0 and g >= 2:
                        pe.wait_ge(y0_done, g - 1)
                    pe.wait_ge(t_copied_a, u + 1)
                    pe.wait_ge(t_copied_v, u + 1)
                    for part in range(2):
                        for i in range(2):
                            j = 2 * jp + i
                            rows = slice(32 * j, 32 * j + 32)
                            for s in range(S):
                                t = 2 * g + s
                                lhsT = htok[:, t * 128 + 32 * j:t * 128 + 32 * j + 32] if part == 0 else m.ones32[:, :]
                                mm = pe.matmul(ps[rows, 6 + g % 2, part * N:(part + 1) * N], lhsT,
                                               m.ext[:, u % 2, (2 * i + s) * N:(2 * i + s + 1) * N],
                                               start=(s == 0), stop=(s == S - 1))
                    mm.then_inc(pv_ready, 1)

                scores(0)
                scores(1)
                for u in range(NU):
                    transposes(u)
                    if u + 2 < NU:
                        scores(u + 2)
                    if u >= 1:
                        values(u - 1)
                values(NU - 1)
                for k in range(NCH):
                    pe.wait_ge(y0_done, 2 * (k + 1))
                    pe.matmul(ps[:, k, :], m.vobd[:, :], y0[:, k * CH:(k + 1) * CH],
                              start=True, stop=True).then_inc(y_ready, 1)
                pe.wait_ge(y_copied, NCH)

            def feed_forward():
                pe.wait_ge(loaded, 16 * NLOAD)

                def up(w):
                    k, j = divmod(w, J)
                    rows = slice(32 * j, 32 * j + 32)
                    if w >= 6:
                        pe.wait_ge(relu_a if w % 2 == 0 else relu_v, (w - 6) // 2 + 1)
                    pe.matmul(ps[:, w % 6, :], m.w1[rows, :], h[rows, k * CH:(k + 1) * CH],
                              start=True, stop=True).then_inc(z1_ready, 1)

                for w in range(4):
                    up(w)
                for w in range(J * NCH):
                    k, j = divmod(w, J)
                    if w + 4 < J * NCH:
                        up(w + 4)
                    if j == 0 and k >= 2:
                        pe.wait_ge(z2_copied, k - 1)
                    pe.wait_ge(relu_a if w % 2 == 0 else relu_v, w // 2 + 1)
                    mm = pe.matmul(ps[32 * j:32 * j + 32, 6 + k % 2, :], m.w2f[:, :], m.z1[:, w % 6, :],
                                   start=True, stop=True)
                    if j == J - 1:
                        mm.then_inc(z2_ready, 1)
                pe.wait_ge(z2_copied, NCH)

            probe()
            state(pe, go["pe"], regs)
            with pe.While(lambda: pe.snap(regs[0]) < NB):
                with pe.If(pe.snap(regs[2]) > 0):
                    attention()
                with pe.Else():
                    pe.nop()
                with pe.If(pe.snap(regs[3]) > 0):
                    feed_forward()
                with pe.Else():
                    pe.nop()
                probe()
                state(pe, go["pe"], regs)

        @block.scalar
        def _(act):
            regs = registers(act, "act")

            def column():
                act.activation(m.hcol[:, 0:1], h[0:C, 0:1], ACT.Copy).then_inc(settled, 1)

            def attention():
                for k in range(NCH):
                    act.wait_ge(u_ready, k + 1)
                    act.activation(ut[:, k * CH:(k + 1) * CH], ps[:, 4 + k, :], ACT.Copy).then_inc(u_copied, 1)

                def copy_transposed(u):
                    act.wait_ge(t_ready, u + 1)
                    if u >= 2:
                        act.wait_ge(pv_ready, u - 1)
                    act.activation(m.ext[:, u % 2, 0:2 * N], ps[:, 4, :], ACT.Copy).then_inc(t_copied_a, 1)

                for u in range(NU):
                    act.wait_ge(negated, u + 1)
                    if u >= 2:
                        act.wait_ge(t_ready, u - 1)
                    for i in range(2):
                        for s in range(S):
                            q = 2 * i + s
                            act.activation(m.ex[:, u % 2, q * N:(q + 1) * N],
                                           ps[:, 2 * (u % 2) + i, s * N:(s + 1) * N], ACT.Exp,
                                           bias=m.negmx[:, u, q:q + 1]).then_inc(exp_done, 1)
                    if u >= 1:
                        copy_transposed(u - 1)
                copy_transposed(NU - 1)
                for k in range(NCH):
                    act.wait_ge(y_ready, k + 1)
                    act.activation(h[:, k * CH:(k + 1) * CH], ps[:, k, :], ACT.Copy).then_inc(y_copied, 1)
                act.wait_ge(y_copied, NCH)

            def down(k):
                act.wait_ge(z2_ready, k + 1)
                act.activation(h[:, k * CH:(k + 1) * CH], ps[:, 6 + k % 2, :], ACT.Identity,
                               bias=m.b2[:, 0:1]).then_inc(z2_copied, 1)

            def feed_forward():
                act.wait_ge(loaded, 16 * NLOAD)
                for k in range(NCH):
                    for j in (0, 2):
                        w = J * k + j
                        act.wait_ge(z1_ready, w + 1)
                        if w >= 6:
                            act.wait_ge(z2_ready, (w - 6) // J + 1)
                        act.activation(m.z1[:, w % 6, :], ps[:, w % 6, :], ACT.Relu, bias=m.b1[:, 0:1]).then_inc(relu_a, 1)
                    if k >= 1:
                        down(k - 1)
                down(NCH - 1)
                act.wait_ge(z2_copied, NCH)

            column()
            state(act, go["act"], regs)
            with act.While(lambda: act.snap(regs[0]) < NB):
                with act.If(act.snap(regs[2]) > 0):
                    attention()
                with act.Else():
                    act.nop()
                with act.If(act.snap(regs[3]) > 0):
                    feed_forward()
                with act.Else():
                    act.nop()
                column()
                state(act, go["act"], regs)

        @block.vector
        def _(dve):
            regs = registers(dve, "dve")

            def choose():
                n = 0

                def step(ins):
                    nonlocal n
                    ins.then_inc(ctl, 1)
                    n += 1
                    dve.wait_ge(ctl, n)

                r, key, one, sc = m.crow, m.ckey, m.cone, m.csc
                dve.wait_ge(probed, 1)
                step(dve.tensor_copy(r[:, :], ps[0:1, 0, 0:NOPS]))
                step(dve.tensor_reduce(sc[:, 0:1], r[:, :], AXX, ALU.max))
                step(dve.scalar_tensor_tensor(key[:, :], r[:, :], sc[:, 0:1], m.revop[:, :], ALU.is_ge, ALU.mult))
                step(dve.tensor_reduce(sc[:, 1:2], key[:, :], AXX, ALU.max))
                step(dve.tensor_scalar(one[:, :], key[:, :], sc[:, 1:2], None, ALU.is_equal))
                step(dve.tensor_tensor(m.cprod[:, :, :], m.codes[:, :, :],
                                       one[:, None, :].broadcast_to([1, NB, NOPS]), ALU.mult))
                step(dve.tensor_reduce(m.code[:, :], m.cprod[:, :, :], AXX, ALU.add))
                step(dve.scalar_tensor_tensor(m.cand[:, :], m.code[:, :], 0.5, m.revstep[:, :], ALU.is_gt, ALU.mult))
                step(dve.scalar_tensor_tensor(m.cand[:, :], m.revstep[:, :], m.lim[:, 0:1], m.cand[:, :],
                                              ALU.is_le, ALU.mult))
                step(dve.tensor_reduce(sc[:, 2:3], m.cand[:, :], AXX, ALU.max))
                step(dve.tensor_scalar(sc[:, 2:3], sc[:, 2:3], float(TOP - NB), None, ALU.max))
                step(dve.scalar_tensor_tensor(m.cand[:, :], m.revstep[:, :], sc[:, 2:3], m.code[:, :],
                                              ALU.is_equal, ALU.mult))
                step(dve.tensor_reduce(sc[:, 3:4], m.cand[:, :], AXX, ALU.add))
                step(dve.tensor_scalar(sc[:, 4:5], sc[:, 3:4], 1.5, None, ALU.is_gt))
                dve.tensor_scalar(m.lim[:, :], sc[:, 2:3], -1.0, None, ALU.add).then_inc(ctl, 1)
                dve.tensor_scalar(m.state[:, 0:1], sc[:, 2:3], -1.0, float(TOP), ALU.mult, ALU.add).then_inc(ctl, 1)
                dve.tensor_scalar(m.state[:, 1:2], sc[:, 1:2], -1.0, float(TOP), ALU.mult, ALU.add).then_inc(ctl, 1)
                dve.tensor_copy(m.state[:, 3:4], sc[:, 4:5]).then_inc(ctl, 1)
                dve.scalar_tensor_tensor(m.state[:, 2:3], sc[:, 4:5], -2.0, sc[:, 3:4], ALU.mult,
                                         ALU.add).then_inc(ctl, 1)
                dve.wait_ge(ctl, n + 5)
                for x in per_block + [probed, ctl]:
                    dve.sem_clear(x)
                for x in list(go.values()) + [go_dve]:
                    dve.sem_inc(x, 1)

            def attention():
                dve.wait_ge(mats_ready, 1)
                dve.scalar_tensor_tensor(m.sabd[:, :], ps[:, 0, 0:128], float(C) ** -0.5, m.blkone[:, :],
                                         ALU.mult, ALU.mult).then_inc(mats_masked, 1)
                dve.tensor_tensor(m.vobd[:, :], ps[:, 1, 0:128], m.blkone[:, :], ALU.mult).then_inc(mats_masked, 1)
                for q in range(NCH):
                    bank = (q + 2) % 4
                    dve.wait_ge(ht_ready, q + 1)
                    dve.tensor_copy(htok[:, bank * CH:(bank + 1) * CH], ps[:, bank, :]).then_inc(ht_copied, 1)

                def copy_transposed(u):
                    dve.wait_ge(t_ready, u + 1)
                    if u >= 2:
                        dve.wait_ge(pv_ready, u - 1)
                    dve.tensor_copy(m.ext[:, u % 2, 2 * N:4 * N], ps[:, 5, :]).then_inc(t_copied_v, 1)

                def normalise(g):
                    dve.wait_ge(pv_ready, 2 * (g + 1))
                    dve.reciprocal(m.rd[:, g % 2, :], ps[:, 6 + g % 2, N:2 * N]).then_inc(inv_done, 1)
                    dve.wait_ge(inv_done, g + 1)
                    dve.tensor_tensor(y0[:, g * N:(g + 1) * N], ps[:, 6 + g % 2, 0:N], m.rd[:, g % 2, :],
                                      ALU.mult).then_inc(y0_done, 1)

                for u in range(NU):
                    dve.wait_ge(s_ready, u + 1)
                    b = 2 * (u % 2)
                    dve.tensor_reduce(m.mx[:, u, :], ps[:, b:b + 2, :].rearrange("p i (s m) -> p (i s) m", s=S),
                                      AXX, ALU.max).then_inc(max_done, 1)
                    dve.wait_ge(max_done, u + 1)
                    dve.tensor_scalar(m.negmx[:, u, :], m.mx[:, u, :], -1.0, None, ALU.mult).then_inc(negated, 1)
                    if u >= 1:
                        copy_transposed(u - 1)
                    if u >= 3 and u % 2:
                        normalise((u - 3) // 2)
                copy_transposed(NU - 1)
                normalise(G - 1)
                dve.wait_ge(y0_done, G)

            def feed_forward():
                dve.wait_ge(loaded, 16 * NLOAD)
                for k in range(NCH):
                    for j in (1, 3):
                        w = J * k + j
                        dve.wait_ge(z1_ready, w + 1)
                        if w >= 6:
                            dve.wait_ge(z2_ready, (w - 6) // J + 1)
                        dve.tensor_scalar(m.z1[:, w % 6, :], ps[:, w % 6, :], m.b1[:, 0:1], 0.0, ALU.add,
                                          ALU.max).then_inc(relu_v, 1)
                dve.wait_ge(relu_v, 2 * NCH)

            choose()
            state(dve, go_dve, regs)
            with dve.While(lambda: dve.snap(regs[0]) < NB):
                with dve.If(dve.snap(regs[2]) > 0):
                    attention()
                with dve.Else():
                    dve.nop()
                with dve.If(dve.snap(regs[3]) > 0):
                    feed_forward()
                with dve.Else():
                    dve.nop()
                choose()
                state(dve, go_dve, regs)

    with nc.Block() as block:
        @block.vector
        def _(dve):
            for k in range(NCH):
                c = slice(k * CH, (k + 1) * CH)
                dve.tensor_tensor(m.x[:, c], m.x[:, c], h[:, c], ALU.add).then_inc(added, 1)

        @block.sync
        def _(sp):
            stored = sem("rb_stored")
            for k in range(NCH):
                sp.wait_ge(added, k + 1)
                sp.dma_start(m.d_out.rearrange("(g j) c n -> (j c) g n", j=J)[:, 2 * k:2 * k + 2, :],
                             m.x[:, k * CH:(k + 1) * CH].rearrange("p (g n) -> p g n", g=2)).then_inc(stored, 16)
            sp.wait_ge(stored, 16 * NCH)


def place(nc, m, ctx):
    def sb(name, shape, dt=F32):
        return ctx.enter_context(nc.sbuf_tensor(name, shape, dt))

    m.ps = ctx.enter_context(nc.psum_tensor("ps", [128, 8, CH], F32))
    R_ = sb("R", [128, 4 * B * N])
    P_ = sb("P", [128, 2 * COLS])
    Q_ = sb("Q", [128, 2 * COLS])
    m.x = sb("x", [128, COLS])
    m.z = sb("z", [128, COLS])
    m.tmpA = sb("tmpA", [128, COLS])
    m.tmpB, m.rstd = Q_[:, 0:COLS], Q_[:, COLS:2 * COLS]

    def view(at, names, dims, dt=F32, base=R_):
        size = 1
        for d in dims:
            size *= d
        t = base[:, at:at + (size // 2 if dt == BF16 else size)]
        if dt != F32:
            t = t.bitcast(dt)
        if len(dims) == 1:
            return t
        letters = "abcde"[:len(dims)]
        kw = {letters[i]: dims[i] for i in range(1, len(dims))}
        return t.rearrange(f"p ({' '.join(letters)}) -> p {' '.join(letters)}", **kw)

    r = B * N
    m.r0, m.r1, m.r2, m.r3 = (view(i * r, "", [B, N]) for i in range(4))
    m.memv_b = view(0, "", [B, 128], base=P_)
    m.ct = view(0, "", [B, 128], base=Q_)
    m.big = view(0, "", [S, H, CH])
    m.co = view(3 * r + 4608, "", [C // 4, N])
    at = 2 * r
    m.qv = view(at, "", [LAYERS * ZHEADS * (128 + 32)])
    m.qbd = view(at, "", [LAYERS, ZHEADS, 128]); at += LAYERS * ZHEADS * 128
    m.vt4 = view(at, "", [LAYERS * ZHEADS * 32]); at += LAYERS * ZHEADS * 32
    m.gbd = view(at, "", [G, 128]); at += G * 128
    m.abd = view(at, "", [G, 128]); at += G * 128
    m.pmat = view(at, "", [G, ZHEADS * 32]); at += G * ZHEADS * 32
    m.amat = view(at, "", [G, 32]); at += G * 32
    m.wt = view(at, "", [G, 32]); at += G * 32
    m.rmat = view(at, "", [G, 32]); at += G * 32
    at = 3 * r + COLS + 1024
    m.ewbd = view(at, "", [E, 128])
    m.sele = view(3 * r + 4608 + COLS, "", [E, 128], BF16)
    at = 0
    nl = G * S * J * E
    m.lg = view(at, "", [nl]); at += nl
    m.key = view(at, "", [nl]); at += nl
    m.one1 = view(at, "", [nl]); at += nl
    m.sel2 = view(at, "", [nl]); at += nl
    m.gparts = view(at, "", [G * S, 4, 32], BF16); at += G * S * 64
    m.stat = view(at, "", [4, G * S * J]); at += 4 * G * S * J
    m.gt = view(at, "", [COLS], BF16); at += COLS // 2
    m.gz = view(at, "", [3, CH]); at += 3 * CH
    m.vm = view(2 * r, "", [G * S * J, AH, 32])
    m.qkt = view(0, "", [2, 2, B, N], BF16)
    m.qkparts = view(2 * r, "", [2, 3, COLS], BF16)
    m.qkstack = view(3 * r, "", [2, J, COLS], BF16)
    m.selqk = view(COLS, "", [2, 2, 128], BF16, base=P_)
    m.selqk32 = view(COLS + 256, "", [2 * 2 * 128], base=P_)[0:96]
    m.att = view(3 * r, "", [6, 2, 3 * 128])
    m.sa = view(3 * r + 3 * 1536, "", [COLS])
    m.pa = P_[:, 0:COLS]
    m.h = view(0, "", [COLS])
    m.ex = view(2 * r, "", [2, 4 * N])
    m.ext = view(2 * r + 8 * N, "", [2, 4 * N])
    m.z1 = view(COLS + 12 * N, "", [6, CH])

    def packed(t, dims_of):
        out, at = [], 0
        for dims in dims_of:
            out.append(view(at, "", dims, base=t))
            at += int(np.prod(dims))
        assert at == t.shape[1]
        return out

    m.early = sb("early", [128, EARLY])
    (m.exchange, m.ol, m.orr, m.wqkv, m.wo, m.memk, m.memv, m.memmask, m.gcol, m.bout, wcomp) = packed(
        m.early, [[128], [23 * W], [23 * W], [384], [C], [MEM], [128], [B], [1], [1], [CONV_P * CONV_P]])
    m.wcomp = wcomp[0:C]
    m.lasting = sb("lasting", [128, LASTING])
    (m.ident, m.blkone, m.causal, m.headmask, m.ident32, m.rank, m.jmask, m.rb, m.ebrep, m.bv, m.gam,
     m.bet, m.bu, m.bf, m.bqk, m.wqkbd, m.wvbd, m.rwbd, m.wubd, m.wfbd, revop, revstep) = packed(
        m.lasting, [[128], [128], [128], [AH, 32], [32], [E], [J], [E], [C], [C], [2], [2], [2], [1], [2],
                    [2, 128], [128], [J * E], [2, 128], [2, 128], [NOPS], [NB]])
    m.revop, m.revstep = revop[0:1], revstep[0:1]
    m.gather = sb("gather", [128, G, B])
    m.scatter = sb("scatter", [B, G, 128])
    m.identb = sb("identb", [128, 128], BF16)
    m.blkmean = sb("blkmean", [128, 128])
    m.blkmean64 = sb("blkmean64", [128, 128])
    m.sele32 = view(3 * r + 7168, "", [E, 128])
    m.ones32 = sb("ones32", [128, 32])
    m.eps = sb("eps", [128, 2])
    m.gs = sb("gs", [128, 1])
    m.small = sb("small", [128, 4])
    m.bst = sb("bst", [128, 6 * G])
    m.bag = sb("bag", [128, 2 * G])
    m.std8 = sb("std8", [128, G])
    m.inv8 = sb("inv8", [128, G])
    m.kmax = sb("kmax", [128, B])
    m.knegmax = sb("knegmax", [128, B])
    m.ksum = sb("ksum", [128, B])
    m.memsum = sb("memsum", [128, B])
    m.em = m.blkmean
    m.emt = m.blkmean64
    m.qmax, m.qsum, m.qinv = (m.z[:, i * 256:(i + 1) * 256] for i in range(3))
    m.w2 = view(0, "", [B, C], base=P_)
    m.wclass = view(COLS, "", [CLASSES, 2 * R + 1], base=P_)[0:C]
    m.bl = view(0, "", [C, W], base=P_)
    m.br = view(CH, "", [C, W], base=P_)
    m.kmat = view(2 * CH, "", [S, N], base=P_)
    m.ebpart = sb("ebpart", [128, 3, C], BF16)
    m.ebbd = sb("ebbd", [128, 3, 128], BF16)
    m.relt = sb("relt", [128, S, N])
    m.kmat_rev = m.relt
    m.wsm = view(COLS + 12 * N + 6 * CH + 2 * N + 1280, "", [4, 128])[0:C]
    m.w1 = view(0, "", [HID], base=m.early)
    m.w2f = view(128, "", [C], base=m.early)
    m.b1 = sb("b1", [128, 1])
    m.b2 = sb("b2", [128, 1])
    m.sabd = view(COLS + 12 * N + 6 * CH + 2 * N + 1024, "", [128])
    m.vobd = view(COLS + 12 * N + 6 * CH + 2 * N + 1152, "", [128])
    m.mx = view(160, "", [2 * G, 2 * S], base=m.early)
    m.negmx = view(224, "", [2 * G, 2 * S], base=m.early)
    m.rd = view(COLS + 12 * N + 6 * CH, "", [2, N])
    m.hcol = sb("hcol", [C, 1])
    m.state = sb("state", [1, 4], I32)
    m.crow = sb("crow", [1, NOPS])
    m.ckey = sb("ckey", [1, NOPS])
    m.cone = sb("cone", [1, NOPS])
    m.code = sb("code", [1, NB])
    m.cand = sb("cand", [1, NB])
    m.codes = view(COLS + 1024, "", [NB, NOPS], base=P_)[0:1]
    m.cprod = view(COLS + 12 * N + 6 * CH + 2 * N, "", [NB, NOPS])[0:1]
    m.masks = view(3 * r + 1792, "", [2, NB * NOPS], I32)[0:1]
    m.maskf = view(2 * r + 5120, "", [NB * NOPS])[0:1]
    m.csc = sb("csc", [1, 8])
    m.lim = sb("lim", [1, 1])


def toeplitz_rows(tensor_ap, first, row_step, dims):
    return bass.AP(tensor=tensor_ap.tensor, offset=tensor_ap.offset + first, ap=[[row_step, dims[0]]] + dims[1])


def load_first(nc, m, sem, d):
    x_loaded = [sem(f"ld_x_loaded_{k}") for k in range(NCH)]
    set_up = sem("ld_set_up")
    with nc.Block() as block:
        @block.sync
        def _(sp):
            src = d.x.rearrange("(g j) c n -> (j c) g n", j=J)
            for k in range(NCH):
                sp.dma_start(m.x[:, k * CH:(k + 1) * CH].rearrange("p (g n) -> p g n", g=2),
                             src[:, 2 * k:2 * k + 2, :]).then_inc(x_loaded[k], 16)
            for s in range(S):
                for y in range(H // S):
                    first = KS // 2 - R
                    src = toeplitz_rows(d.kpe, (first + y + (S - 1 - s) * (H // S)) * KS + first, 1,
                                        (W, [[KS, H], [1, W]]))
                    sp.dma_start(m.kmat_rev[16 * y:16 * y + 16, s, :].rearrange("p (y x) -> p y x", y=H),
                                 src).then_inc(m.loaded_kpe, 16)

        @block.scalar
        def _(act):
            act.dma_start(m.gather[:, :, :], d.gather).then_inc(m.loaded, 16)
            act.dma_start(m.scatter[:, :, :], d.scatter).then_inc(m.loaded, 16)
            act.dma_start(m.early[:, :], d.early).then_inc(m.loaded, 16)
            act.dma_start(m.lasting[:, :], d.lasting).then_inc(m.loaded, 16)

        @block.gpsimd
        def _(pool):
            pool.memset(m.ones32[:, :], 1.0).then_inc(set_up, 1)
            pool.memset(m.lim[:, :], 64.0).then_inc(set_up, 1)
            pool.memset(m.eps[:, 0:1], EPS_GN).then_inc(set_up, 1)
            pool.memset(m.eps[:, 1:2], EPS_A).then_inc(set_up, 1)

    instance_norm(nc, m, sem, "gn0", m.x, m.z, x_loaded, lambda sp: sp.wait_ge(m.loaded, 16 * 4))


def load_second(nc, m, sem, d):
    def start(sp):
        sp.dma_start(m.qv[:, :], d.qv).then_inc(m.loaded, 16)
        sp.dma_start(m.ewbd[:, :, :], d.ewbd).then_inc(m.loaded, 16)
        sp.dma_start(m.sele32[:, :, :], d.sele).then_inc(m.loaded, 16)
        sp.dma_start(m.masks[:, :, :], d.masks).then_inc(m.loaded, 16)
        sp.wait_ge(m.loaded_kpe, 16 * S * (H // S))

    instance_norm(nc, m, sem, "gn1", m.x, m.z, None, start)


def prepare(dve, m, made):
    n = 0

    def step(ins):
        nonlocal n
        ins.then_inc(made, 1)
        n += 1
        dve.wait_ge(made, n)

    dve.wait_ge(m.loaded, 16 * 8)
    step(dve.tensor_copy(m.identb[:, :], m.ident[:, :]))
    step(dve.tensor_scalar(m.blkmean[:, :], m.blkone[:, :], 1.0 / C, None, ALU.mult))
    step(dve.tensor_scalar(m.blkmean64[:, :], m.blkone[:, :], 0.5 / C, None, ALU.mult))
    for i in range(3):
        step(dve.tensor_copy(m.ebpart[:, i, :], m.ebrep[:, :]))
        step(dve.tensor_tensor(m.ebrep[:, :], m.ebrep[:, :], m.ebpart[:, i, :], ALU.subtract))
        step(dve.tensor_tensor(m.ebbd[:, i, :].rearrange("p (j c) -> p j c", j=J),
                               m.ebpart[:, i, None, :].broadcast_to([128, J, C]),
                               m.jmask[:, :, None].broadcast_to([128, J, C]), ALU.mult))
    step(dve.tensor_copy(m.sele[:, :, :], m.sele32[:, :, :]))
    step(dve.tensor_copy(m.wt[:, :, :], m.ident32[:, None, :].broadcast_to([128, G, 32])))
    cd = m.codes[:, :, :].rearrange("a s o -> a (s o)")
    step(dve.tensor_copy(cd, m.masks[:, 1, :]))
    step(dve.tensor_tensor(cd, cd, cd, ALU.add))
    step(dve.tensor_copy(m.maskf[:, :], m.masks[:, 0, :]))
    step(dve.tensor_tensor(cd, cd, m.maskf[:, :], ALU.add))


def conv_attn_hybrid(nc, d):
    m = Mem()
    with ExitStack() as ctx:
        def stage(run, *args):
            sems = []
            with ExitStack() as own:
                def sem(name):
                    sems.append(own.enter_context(nc.semaphore(name)))
                    return sems[-1]
                run(nc, m, sem, *args)
                with nc.Block() as block:
                    @block.gpsimd
                    def _(pool):
                        for s in sems:
                            pool.sem_clear(s)

        place(nc, m, ctx)
        m.scratch_w = nc.dram_tensor("scratch_w", [C, CLASSES, 2 * R + 1], F32, kind="Internal").ap()
        m.scratch_x = nc.dram_tensor("scratch_x", [B, C, N], F32, kind="Internal").ap()
        m.d_out = d.out
        m.d_selqk = d.selqk
        m.d_small, m.d_w1, m.d_w2, m.d_b1, m.d_b2 = d.small4, d.w1, d.w2, d.b1, d.b2
        m.loaded = ctx.enter_context(nc.semaphore("loaded"))
        m.loaded_kpe = ctx.enter_context(nc.semaphore("loaded_kpe"))
        stage(load_first, d)
        stage(linear_attention)
        stage(load_second, d)
        stage(peripheral_convolution, d)
        stage(normalise_tokens, "ln1", [m.x], [m.z], EPS_T, m.blkmean)
        stage(linear_transformer)
        stage(normalise_tokens, "ln2", [m.x], [m.z], EPS_T, m.blkmean)
        stage(mixture_of_experts)
        stage(normalise_tokens, "ln3", [m.x], [m.z], EPS_T, m.blkmean)
        stage(squared_attention)
        stage(normalise_tokens, "ln4", [m.x], [m.h], EPS_T, m.blkmean)
        stage(routed_blocks)


def constants():
    import numpy as np
    p = np.arange(128)
    f = np.float32
    out = {"ident": np.eye(128, dtype=f),
           "blkone": (p[:, None] // 32 == p[None, :] // 32).astype(f),
           "causal": (p[:, None] <= p[None, :]).astype(f),
           "memmask": (p[:, None] // MEM == np.arange(B)[None, :]).astype(f),
           "exchange": np.eye(128, dtype=f)[::-1],
           "ident32": (p[:, None] % 32 == np.arange(32)[None, :]).astype(f),
           "rank": np.broadcast_to(np.arange(E, 0, -1), (128, E)).astype(f),
           "revop": (64 - np.arange(NOPS))[None, :].astype(f),
           "revstep": (64 - np.arange(NB))[None, :].astype(f)}
    part, j, e = p // 32, p // E % J, p % E
    live = part < 3
    out["jmask"] = (live[:, None] & (j[:, None] == np.arange(J))).astype(f)
    out["sele"] = (live[:, None, None] & (e[:, None, None] == np.arange(E)[None, :, None])
                   & (j[:, None, None] == p // C)).astype(f)
    b = np.arange(B)
    own = (p[:, None] // C == b[None, :] % J)[:, None, :] & (b[None, None, :] // J == np.arange(G)[None, :, None])
    out["gather"] = own.astype(f)
    out["scatter"] = own.transpose(2, 1, 0).astype(f)
    out["headmask"] = np.broadcast_to(np.arange(32)[None, :] // AHD == np.arange(AH)[:, None],
                                      (128, AH, 32)).astype(f)
    terms = ((0, 0, 0, 1, 1, 2), (0, 1, 2, 0, 1, 0))
    sel = np.zeros((3, AH, AHD, 2, 2, 2, 8, AHD), f)
    for x in range(2):
        for h in range(AH):
            for term, part_of in enumerate(terms[x]):
                sel[part_of, h, :, x, h // 2, h % 2, term, :] = np.eye(AHD)
    out["selqk"] = sel.reshape(96, 512)
    for name, first, lo in (("ol", 0, -R), ("orr", 1, -R + 8)):
        t = np.zeros((8, 16, 23, 16), f)
        for q in range(8):
            a, b = CLASS_SPANS[first + q]
            for dy in range(max(a, lo), min(b, lo + 22) + 1):
                t[q, :, dy - lo, :] = np.eye(16)[::-1]
        out[name] = t.reshape(128, 23 * 16)
    return out


def kernel(**inputs):
    import numpy as np
    import concourse.bacc as bacc
    from concourse.bass_utils import run_bass_kernel_spmd

    a = {k: np.asarray(v) for k, v in inputs.items()}
    f = "L3_ffn_"
    def tile(t):
        return np.tile(t, (J, 1))

    def diagonal(t):
        out = np.zeros((J, C, J, t.shape[1]), t.dtype)
        for j in range(J):
            out[j, :, j] = t
        return out.reshape(128, -1)

    def rows(t, n=128):
        return np.repeat(t.reshape(1, -1), n, axis=0)

    def below(t):
        return np.concatenate([t, np.zeros((128 - t.shape[0], t.shape[1]), t.dtype)])

    c = constants()
    eb, ew = a["L2_ffn_expert_b"], a["L2_ffn_expert_w"]
    wu, wf = a["L3_attn_Wu"], a["L3_attn_Wf"]
    early = [c["exchange"], c["ol"], c["orr"], tile(a["L0_conv_w_qkv"].T), a["L0_conv_w_out"].T,
             a["L0_conv_mem_kv"][0].reshape(HEADS * DH, MEM),
             np.tile(a["L0_conv_mem_kv"][1].transpose(2, 0, 1).reshape(MEM, HEADS * DH), (B, 1)), c["memmask"],
             tile(a["L0_conv_g"].reshape(C, 1)), tile(a["L0_conv_b_out"].reshape(C, 1)),
             below(a["L1_conv_weight_comp"])]
    lasting = [c["ident"], c["blkone"], c["causal"], c["headmask"].reshape(128, -1), c["ident32"], c["rank"],
               c["jmask"], rows(a["L2_ffn_router_b"]), np.tile(eb, (128 // E, 1)), rows(a["L3_attn_bv"]),
               tile(a["L3_attn_ln_gamma"].reshape(2, C).T), tile(a["L3_attn_ln_beta"].reshape(2, C).T),
               tile(a["L3_attn_bu"].reshape(2, C).T), tile(a["L3_attn_bf"].reshape(C, 1)),
               tile(np.stack([a["L3_attn_bq"], a["L3_attn_bk"]], axis=1)),
               diagonal(a["L3_attn_Wq"]), diagonal(a["L3_attn_Wk"]), diagonal(a["L3_attn_Wv"]),
               diagonal(a["L2_ffn_router_w"]), diagonal(wu[:, :C]), diagonal(wu[:, C:]), diagonal(wf[:C]),
               diagonal(wf[C:]), rows(c["revop"]), rows(c["revstep"])]
    z_mats = [a["L2_attn_" + n].reshape(LAYERS * ZHEADS, 32, 32).transpose(0, 2, 1)
              for n in ("q_matrix", "v_matrix")]
    arrays = {
        "x": a["x"].reshape(B, C, N),
        "early": np.concatenate(early, axis=1),
        "lasting": np.concatenate(lasting, axis=1),
        "gather": c["gather"], "scatter": c["scatter"], "sele": c["sele"], "selqk": c["selqk"],
        "kpe": a["L1_conv_kpe"].reshape(KS, KS)[::-1, ::-1],
        "pos_w": a["L3_attn_pos_w"][::-1],
        "qv": np.concatenate([diagonal(t) for t in z_mats[0]]
                             + [tile(z_mats[1].transpose(1, 0, 2).reshape(32, -1))], axis=1),
        "ewbd": np.stack([diagonal(t) for t in ew], axis=1),
        "masks": np.stack([a[f + "attn_mask"], a[f + "ffn_mask"]]).astype(np.int32).reshape(1, 2, NB * NOPS),
        "small4": np.concatenate([a[f + "wq"].swapaxes(2, 3), a[f + "wk"].swapaxes(2, 3),
                                  a[f + "wv"].swapaxes(2, 3), a[f + "wo"]], axis=3).reshape(NB * NOPS, C, 4 * C),
        "w1": a[f + "ffn_w1"].reshape(NB * NOPS, C, HID),
        "w2": a[f + "ffn_w2"].reshape(NB * NOPS, HID, C),
        "b1": a[f + "ffn_b1"].reshape(NB * NOPS, HID, 1),
        "b2": a[f + "ffn_b2"].reshape(NB * NOPS, C, 1),
    }
    nc = bacc.Bacc("TRN2", target_bir_lowering=False, num_devices=1)
    d = Mem()
    arrays = {k: np.ascontiguousarray(v) for k, v in arrays.items()}
    for k, v in arrays.items():
        vars(d)[k] = nc.dram_tensor("in_" + k, v.shape, mybir.dt.from_np(v.dtype), kind="ExternalInput").ap()
    d.out = nc.dram_tensor("out_0", (B, C, N), F32, kind="ExternalOutput").ap()
    conv_attn_hybrid(nc, d)
    r = run_bass_kernel_spmd(nc, [{"in_" + k: v for k, v in arrays.items()}], core_ids=[0])
    return r.results[0]["out_0"].reshape(B, C, H, W)
```

```python
import concourse.bass as bass
import numpy as np
from concourse import mybir
from contextlib import ExitStack

F32 = mybir.dt.float32
BF16 = mybir.dt.bfloat16
I32 = mybir.dt.int32
ALU = mybir.AluOpType
ACT = mybir.ActivationFunctionType
AXX = mybir.AxisListType.X

B, C, H, W = 32, 32, 16, 16
N = H * W
J, G = 4, 8
S = N // 128
COLS = G * N
CH = 512
NCH = COLS // CH
HEADS, DH = 4, 32
MEM = 4
KS, CONV_P = 51, 13
R = H - 1
CLASSES = 9
CLASS0 = 2
CLASS_SPANS = [(-15, -8), (-7, -4), (-3, -2), (-1, -1), (0, 0), (1, 1), (2, 3), (4, 7), (8, 15)]
LAYERS, ZHEADS = 4, 8
E = 8
AH, AHD = 4, 8
NB, NOPS, HID = 33, 19, 128

EARLY = 128 + 2 * 23 * W + 384 + C + MEM + 128 + B + 2 + CONV_P ** 2
LASTING = 3 * 128 + AH * 32 + 32 + E + J + E + 2 * C + 9 + 7 * 128 + J * E + NOPS + NB + 1

EPS_GN, EPS_T, EPS_A = 1e-5, 1e-5, 1e-3


class Mem:
    pass


def token_norm(m, sem, name, parts, outs, eps, mean_w, gamma=None, ready=None):
    n = len(parts)
    mean_ready = sem(name + "_mean_ready")
    centred = sem(name + "_centred")
    squared = sem(name + "_squared")
    var_ready = sem(name + "_var_ready")
    std_ready = sem(name + "_std_ready")
    inverted = sem(name + "_inverted")
    spread = sem(name + "_spread")
    scaled = sem(name + "_scaled")
    shifted = sem(name + "_shifted")
    ps = m.ps
    sq = [m.tmpA, m.tmpB]

    def ch(t, k):
        return t[:, k * CH:(k + 1) * CH]

    def run_pe(pe):
        for k in range(NCH):
            if ready:
                ready(pe, k)
            for i in range(n):
                mm = pe.matmul(ps[:, k, :], mean_w[:, :], ch(parts[i], k), start=(i == 0), stop=(i == n - 1))
            mm.then_inc(mean_ready, 1)
        for k in range(NCH):
            pe.wait_ge(squared, n * (k + 1))
            for g in (2 * k, 2 * k + 1):
                for i in range(n):
                    mm = pe.matmul(ps[0:B, NCH, 0:N], m.gather[:, g, :], sq[i][:, g * N:(g + 1) * N],
                                   start=(g == 0 and i == 0), stop=(g == G - 1 and i == n - 1))
        mm.then_inc(var_ready, 1)
        pe.wait_ge(inverted, 1)
        for g in range(G):
            pe.matmul(ps[:, g // 2, (g % 2) * N:(g % 2) * N + N], m.scatter[:, g, :], m.rstd[0:B, 0:N],
                      start=True, stop=True).then_inc(spread, 1)

    def run_dve(dve):
        for k in range(NCH):
            dve.wait_ge(mean_ready, k + 1)
            if ready:
                ready(dve, k)
            for i in range(n):
                dve.tensor_tensor(ch(outs[i], k), ch(parts[i], k), ps[:, k, :], ALU.subtract).then_inc(centred, 1)
        dve.wait_ge(std_ready, 1)
        dve.reciprocal(m.rstd[0:B, 0:N], m.rstd[0:B, N:2 * N]).then_inc(inverted, 1)
        for k in range(NCH):
            dve.wait_ge(spread, 2 * (k + 1))
            for i in range(n):
                o = ch(outs[i], k)
                dve.tensor_tensor(o, o, ps[:, k, :], ALU.mult).then_inc(scaled, 1)

    def run_act(act):
        for k in range(NCH):
            for i in range(n):
                act.wait_ge(centred, n * k + i + 1)
                act.activation(ch(sq[i], k), ch(outs[i], k), ACT.Square).then_inc(squared, 1)
        act.wait_ge(var_ready, 1)
        act.activation(m.rstd[0:B, N:2 * N], ps[0:B, NCH, 0:N], ACT.Sqrt, bias=eps,
                       scale=1.0 / (C * n)).then_inc(std_ready, 1)
        if gamma:
            for k in range(NCH):
                for i in range(n):
                    o = ch(outs[i], k)
                    act.wait_ge(scaled, n * k + i + 1)
                    act.activation(o, o, ACT.Identity, bias=gamma[i][1], scale=gamma[i][0])\
                        .then_inc(shifted, 1)

    norm = Mem()
    norm.pe, norm.dve, norm.act, norm.done = run_pe, run_dve, run_act, scaled
    norm.shifted = shifted
    return norm


def instance_norm(nc, m, sem, name, src, dst, src_loaded, beside_sp, first_act=None, beside_pool=None, then_act=None):
    stats = sem(name + "_stats")
    moments = sem(name + "_moments")
    std = sem(name + "_std")
    inv = sem(name + "_inv")
    done = sem(name + "_done")
    with nc.Block() as block:
        @block.vector
        def _(dve):
            for g in range(G):
                if src_loaded and g % 2 == 0:
                    dve.wait_ge(src_loaded[g // 2], 16)
                dve.bn_stats(m.bst[:, 6 * g:6 * g + 6], src[:, g * N:(g + 1) * N]).then_inc(stats, 1)
            for g in range(G):
                dve.wait_ge(stats, g + 1)
                dve.bn_aggr(m.bag[:, 2 * g:2 * g + 2], m.bst[:, 6 * g:6 * g + 6]).then_inc(moments, 1)
            dve.wait_ge(std, 1)
            dve.reciprocal(m.inv8[:, :], m.std8[:, :]).then_inc(inv, 1)
            dve.wait_ge(inv, 1)
            for g in range(G):
                c = slice(g * N, (g + 1) * N)
                dve.tensor_scalar(dst[:, c], src[:, c], m.bag[:, 2 * g:2 * g + 1], m.inv8[:, g:g + 1],
                                  ALU.subtract, ALU.mult).then_inc(done, 1)

        @block.scalar
        def _(act):
            if first_act:
                first_act(act)
            act.wait_ge(moments, G)
            act.activation(m.std8[:, :], m.bag[:, 1:2 * G:2], ACT.Sqrt, bias=m.eps[:, 0:1]).then_inc(std, 1)
            if then_act:
                then_act(act)

        @block.sync
        def _(sp):
            beside_sp(sp)

        if beside_pool:
            @block.gpsimd
            def _(pool):
                beside_pool(pool)


def linear_attention(nc, m, sem):
    ps = m.ps
    UN = G // 2 * J
    LAG = 8
    ek, ekt, vt, qt, qf = m.r0, m.r1, m.r2, m.r3, m.r0
    xn = m.tmpA
    squared = sem("la_squared")
    norm2_ready = sem("la_norm2_ready")
    norm_ready = sem("la_norm_ready")
    inv_ready = sem("la_inv_ready")
    spread = sem("la_spread")
    xn_ready = sem("la_xn_ready")
    proj_ready = sem("la_proj_ready")
    wvq_made = sem("la_wvq_made")
    classes = sem("la_classes")
    kmax_ready = sem("la_kmax_ready")
    knegmax_ready = sem("la_knegmax_ready")
    kexp_done = sem("la_kexp_done")
    kt_ready = sem("la_kt_ready")
    kt_copied = sem("la_kt_copied")
    v_copied = sem("la_v_copied")
    qmax_ready = sem("la_qmax_ready")
    qsub_done = sem("la_qsub_done")
    qexp_done = sem("la_qexp_done")
    qsum_ready = sem("la_qsum_ready")
    qinv_ready = sem("la_qinv_ready")
    qnorm_done = sem("la_qnorm_done")
    qt_ready = sem("la_qt_ready")
    qt_copied = sem("la_qt_copied")
    memmax_ready = sem("la_memmax_ready")
    memshift_done = sem("la_memshift_done")
    memexp_done = sem("la_memexp_done")
    memsum = sem("la_memsum")
    memt_ready = sem("la_memt_ready")
    memt_copied = sem("la_memt_copied")
    memv_masked = sem("la_memv_masked")
    ctx_ready = sem("la_ctx_ready")
    ctx_copied = sem("la_ctx_copied")
    w2_ready = sem("la_w2_ready")
    w2_scaled = sem("la_w2_scaled")
    out_ready = sem("la_out_ready")
    added = sem("la_added")

    order = [("k", u) for u in range(UN)] + [(p, u) for u in range(UN) for p in ("q", "v")]

    def bank_free(eng, w):
        if w >= 4:
            p, u = order[w - 4]
            if p == "k":
                eng.wait_ge(kexp_done, 2 * (u + 1))
            elif p == "v":
                eng.wait_ge(v_copied, u + 1)
            else:
                eng.wait_ge(qsub_done, u + 1)

    def unit(u):
        return u % 4, 2 * (u // 4)

    def tile(t, u):
        g, s = divmod(u, S)
        return t[:, :, :].rearrange("p (j g) n -> p j g n", j=J)[:, :, g, s * 128:(s + 1) * 128]

    def by_head(t):
        return t.rearrange("p (j h) -> p j h", j=J)

    with nc.Block() as block:
        @block.tensor
        def _(pe):
            for k in range(NCH):
                pe.wait_ge(squared, k + 1)
                for g in (2 * k, 2 * k + 1):
                    mm = pe.matmul(ps[0:B, 4, 0:N], m.gather[:, g, :], m.tmpB[:, g * N:(g + 1) * N],
                                   start=(g == 0), stop=(g == G - 1))
            mm.then_inc(norm2_ready, 1)
            pe.wait_ge(inv_ready, 2)
            for g in range(G):
                pe.matmul(ps[:, g // 2, (g % 2) * N:(g % 2) * N + N], m.scatter[:, g, :], m.rstd[0:B, 0:N],
                          start=True, stop=True).then_inc(spread, 1)
            pe.wait_ge(xn_ready, NCH)

            def project(w):
                p, u = order[w]
                j, g = unit(u)
                rows = slice(32 * j, 32 * j + 32)
                bank_free(pe, w)
                if p == "k":
                    mm = pe.matmul(ps[:, w % 4, :], m.wqkv[rows, 128:256], xn[rows, g * N:(g + 2) * N],
                                   start=True, stop=True)
                else:
                    if w == UN:
                        pe.wait_ge(wvq_made, 2)
                    mm = pe.matmul(ps[:, w % 4, :], xn[:, u * 128:(u + 1) * 128], m.wvq[:, "vq".index(p), :],
                                   start=True, stop=True)
                mm.then_inc(proj_ready, 1)

            def transposes(p, u):
                j, g = unit(u)
                if p == "k":
                    if u >= 4:
                        pe.wait_ge(kt_copied, u - 3)
                    pe.wait_ge(kexp_done, 2 * (u + 1))
                    src, ready = ek, kt_ready
                else:
                    if u < 4:
                        pe.wait_ge(kt_copied, UN)
                    else:
                        pe.wait_ge(qt_copied, u - 3)
                    pe.wait_ge(qnorm_done, u + 1)
                    src, ready = qt, qt_ready
                for q in range(4):
                    b, s = (j * G + g + q // 2, q % 2) if p == "k" else (q * G + u // S, u % S)
                    mm = pe.transpose(ps[:, 4 + u % 4, q * 128:(q + 1) * 128],
                                      src[:, b, s * 128:(s + 1) * 128], m.ident[:, :])
                mm.then_inc(ready, 1)

            for w in range(3 * UN + LAG):
                if w < 3 * UN:
                    project(w)
                if 4 <= w < UN + 4:
                    transposes("k", w - 4)
                if w == UN + 5:
                    pe.wait_ge(memexp_done, 1)
                    pe.wait_ge(kt_copied, UN)
                    pe.transpose(ps[:, 4, 0:128], m.em[:, :], m.ident[:, :]).then_inc(memt_ready, 1)
                if w == UN + 6:
                    pe.wait_ge(memt_copied, 1)
                if w >= UN + LAG and (w - UN - LAG) % 2 == 0:
                    transposes("q", (w - UN - LAG) // 2)
            pe.wait_ge(memv_masked, 1)
            pe.wait_ge(v_copied, UN)
            pe.wait_ge(qsub_done, UN)
            pe.wait_ge(qt_copied, UN)
            for q in range(B // 4 + 2):
                if q < B // 4:
                    if q >= 4:
                        pe.wait_ge(ctx_copied, q - 3)
                    for i in range(4):
                        b = 4 * q + i
                        o = ps[:, q % 4, i * 128:(i + 1) * 128]
                        for s in range(S):
                            pe.matmul(o, vt[:, b, s * 128:(s + 1) * 128], ekt[:, b, s * 128:(s + 1) * 128],
                                      start=(s == 0), stop=False)
                        mm = pe.matmul(o, m.memv_b[:, b, :], m.emt[:, :], start=False, stop=True)
                    mm.then_inc(ctx_ready, 1)
                if q >= 2:
                    pe.wait_ge(ctx_copied, q - 1)
                    for b in range(4 * (q - 2), 4 * (q - 1)):
                        mm = pe.matmul(ps[:, 4 + b // 16, (b % 16) * 32:(b % 16) * 32 + 32], m.ct[:, b, :],
                                       m.wo[:, :], start=True, stop=True)
            mm.then_inc(w2_ready, 1)
            pe.wait_ge(w2_scaled, 1)
            for k in range(NCH):
                for h in range(2):
                    for j in range(J):
                        b = j * G + 2 * k + h
                        mm = pe.matmul(ps[32 * j:32 * j + 32, k, h * N:(h + 1) * N], m.w2[:, b, :], qf[:, b, :],
                                       start=True, stop=True)
                mm.then_inc(out_ready, 1)

        @block.vector
        def _(dve):
            own = sem("la_dve")
            dve.tensor_reduce(m.small[:, 0:1], m.memk[:, :], AXX, ALU.max).then_inc(memmax_ready, 1)
            dve.tensor_scalar(m.gs[:, :], m.gcol[:, :], float(C) ** 0.5, None, ALU.mult).then_inc(own, 1)
            dve.wait_ge(norm_ready, 1)
            dve.tensor_scalar(m.rstd[0:B, N:2 * N], m.rstd[0:B, N:2 * N], 1e-12, None, ALU.max).then_inc(inv_ready, 1)
            dve.wait_ge(inv_ready, 1)
            dve.reciprocal(m.rstd[0:B, 0:N], m.rstd[0:B, N:2 * N]).then_inc(inv_ready, 1)
            dve.wait_ge(own, 1)
            for k in range(NCH):
                c = slice(k * CH, (k + 1) * CH)
                dve.wait_ge(spread, 2 * (k + 1))
                dve.scalar_tensor_tensor(xn[:, c], m.z[:, c], m.gs[:, 0:1], ps[:, k, :],
                                         ALU.mult, ALU.mult).then_inc(xn_ready, 1)
            dve.wait_ge(memmax_ready, 1)
            for u in range(UN):
                j, g = unit(u)
                b = j * G + g
                dve.wait_ge(proj_ready, u + 1)
                dve.tensor_reduce(m.kmax[:, b:b + 2], ps[:, j, :].rearrange("p (a n) -> p a n", a=2),
                                  AXX, ALU.max).then_inc(kmax_ready, 1)
                dve.wait_ge(kmax_ready, u + 1)
                dve.tensor_scalar(m.knegmax[:, b:b + 2], m.kmax[:, b:b + 2], m.small[:, 0:1], -1.0,
                                  ALU.max, ALU.mult).then_inc(knegmax_ready, 1)
            dve.wait_ge(knegmax_ready, UN)
            dve.tensor_tensor(m.em[:, :].rearrange("p (b m) -> p b m", m=MEM),
                              m.memk[:, None, :].broadcast_to([128, B, MEM]),
                              m.knegmax[:, :, None].broadcast_to([128, B, MEM]), ALU.add).then_inc(memshift_done, 1)

            def normalise(u):
                q = tile(qt, u).rearrange("p j (h d) -> p j h d", h=HEADS)
                st = slice(16 * u, 16 * u + 16)
                dve.wait_ge(qexp_done, u + 1)
                dve.tensor_reduce(by_head(m.qsum[:, st]), q, AXX, ALU.add).then_inc(qsum_ready, 1)
                dve.wait_ge(qsum_ready, u + 1)
                dve.reciprocal(m.qinv[:, st], m.qsum[:, st]).then_inc(qinv_ready, 1)

            for u in range(UN):
                p = ps[:, (UN + 2 * u) % 4, :].rearrange("p (j h d) -> p j h d", j=J, d=DH)
                st = slice(16 * u, 16 * u + 16)
                dve.wait_ge(proj_ready, UN + 2 * u + 1)
                dve.tensor_reduce(by_head(m.qmax[:, st]), p, AXX, ALU.max).then_inc(qmax_ready, 1)
                dve.wait_ge(qmax_ready, u + 1)
                q = tile(qt, u).rearrange("p j (h d) -> p j h d", h=HEADS)
                dve.tensor_tensor(q, p, by_head(m.qmax[:, st]).unsqueeze(3).broadcast_to([128, J, HEADS, DH]),
                                  ALU.subtract).then_inc(qsub_done, 1)
                if u >= 1:
                    normalise(u - 1)
            normalise(UN - 1)
            dve.wait_ge(memexp_done, 1)
            dve.tensor_reduce(m.memsum[:, :], m.em[:, :].rearrange("p (b m) -> p b m", m=MEM), AXX,
                              ALU.add).then_inc(memsum, 1)
            dve.wait_ge(memsum, 1)
            dve.wait_ge(kexp_done, 2 * UN)
            dve.tensor_tensor(m.ksum[:, :], m.ksum[:, :], m.memsum[:, :], ALU.add).then_inc(memsum, 1)
            dve.wait_ge(memsum, 2)
            dve.reciprocal(m.ksum[:, :], m.ksum[:, :]).then_inc(memsum, 1)
            dve.wait_ge(memsum, 3)
            dve.tensor_scalar(m.ksum[:, :], m.ksum[:, :], float(DH) ** -0.5, None, ALU.mult).then_inc(memsum, 1)
            dve.wait_ge(m.classes_stored, 16)
            for q in range(B // 4):
                dve.wait_ge(ctx_ready, q + 1)
                dve.tensor_tensor(m.ct[:, 4 * q:4 * q + 4, :], ps[:, q % 4, :].rearrange("p (b d) -> p b d", b=4),
                                  m.blkone[:, None, :].broadcast_to([128, 4, 128]), ALU.mult).then_inc(ctx_copied, 1)
            dve.wait_ge(memsum, 4)
            dve.wait_ge(w2_ready, 1)
            dve.tensor_tensor(m.w2[:, :, :], ps[:, 4:6, :].rearrange("p a (b c) -> p (a b) c", c=C),
                              m.ksum[:, :, None].broadcast_to([128, B, C]), ALU.mult).then_inc(w2_scaled, 1)
            for k in range(NCH):
                c = slice(k * CH, (k + 1) * CH)
                dve.wait_ge(out_ready, k + 1)
                dve.scalar_tensor_tensor(m.x[:, c], ps[:, k, :], m.bout[:, 0:1], m.x[:, c],
                                         ALU.add, ALU.add).then_inc(added, 1)

        @block.scalar
        def _(act):
            for k in range(NCH):
                c = slice(k * CH, (k + 1) * CH)
                act.activation(m.tmpB[:, c], m.z[:, c], ACT.Square).then_inc(squared, 1)
            act.wait_ge(norm2_ready, 1)
            act.activation(m.rstd[0:B, N:2 * N], ps[0:B, 4, 0:N], ACT.Sqrt).then_inc(norm_ready, 1)

            def copy_transposed(p, u):
                j, g = unit(u)
                b = j * G + g
                if p == 0:
                    act.wait_ge(kt_ready, u + 1)
                    act.activation(ekt[:, b:b + 2, :].rearrange("p b n -> p (b n)"), ps[:, 4 + u % 4, :],
                                   ACT.Copy).then_inc(kt_copied, 1)
                else:
                    act.wait_ge(qt_ready, u + 1)
                    act.activation(tile(qf, u), ps[:, 4 + u % 4, :].rearrange("p (j n) -> p j n", j=J),
                                   ACT.Copy).then_inc(qt_copied, 1)

            for u in range(UN + 5):
                if u < UN:
                    j, g = unit(u)
                    act.wait_ge(knegmax_ready, u + 1)
                    for i in range(2):
                        b = j * G + g + i
                        act.activation(ek[:, b, :], ps[:, j, i * N:(i + 1) * N], ACT.Exp, bias=m.knegmax[:, b:b + 1],
                                       accum_out=m.ksum[:, b:b + 1]).then_inc(kexp_done, 1)
                if u >= 5:
                    copy_transposed(0, u - 5)
            act.wait_ge(memshift_done, 1)
            act.activation(m.em[:, :], m.em[:, :], ACT.Exp).then_inc(memexp_done, 1)
            for u in range(UN + 4):
                if u < UN:
                    act.wait_ge(qsub_done, u + 1)
                    act.activation(tile(qt, u), tile(qt, u), ACT.Exp).then_inc(qexp_done, 1)
                    act.wait_ge(proj_ready, UN + 2 * u + 2)
                    act.activation(tile(vt, u), ps[:, (UN + 2 * u + 1) % 4, :].rearrange("p (j n) -> p j n", j=J),
                                   ACT.Copy).then_inc(v_copied, 1)
                if u == 2:
                    act.wait_ge(memt_ready, 1)
                    act.activation(m.emt[:, :], ps[:, 4, 0:128], ACT.Copy).then_inc(memt_copied, 1)
                if u >= 4:
                    copy_transposed(1, u - 4)

        @block.sync
        def _(sp):
            sp.wait_ge(classes, CLASSES)
            sp.dma_start(m.scratch_w, m.wclass[:, :, :]).then_inc(m.classes_stored, 16)
            sp.wait_ge(m.classes_stored, 16)
            sp.wait_ge(qt_copied, UN)
            for half, dst in enumerate((m.bl, m.br)):
                for q in range(8):
                    src = bass.AP(tensor=m.scratch_w.tensor, offset=m.scratch_w.offset + (q + half) * (2 * R + 1),
                                  ap=[[1, W], [CLASSES * (2 * R + 1), C], [1, W]])
                    sp.dma_start(dst[16 * q:16 * q + 16, :, :], src).then_inc(m.loaded_classes, 16)

        @block.gpsimd
        def _(pool):
            for i, at in enumerate((2 * 128, 0)):
                pool.tensor_tensor(m.wvq[:, i, :].rearrange("p (j n) -> p j n", j=J),
                                   m.wqkv[:, at:at + 128].unsqueeze(1).broadcast_to([128, J, 128]),
                                   m.blkone[:, 0:128:C].unsqueeze(2).broadcast_to([128, J, 128]),
                                   ALU.mult).then_inc(wvq_made, 1)
            wc = m.wcomp[:, :].rearrange("c (a b) -> c a b", a=CONV_P)
            for q, (lo, hi) in enumerate(CLASS_SPANS):
                n = hi - lo + 1
                pool.tensor_copy(m.wclass[:, :, R - hi:R - lo + 1],
                                 wc[:, CLASS0:CLASS0 + CLASSES, CLASS0 + q:CLASS0 + q + 1]
                                 .broadcast_to([C, CLASSES, n])).then_inc(classes, 1)
            pool.tensor_tensor(m.memv_b[:, :, :], m.memv[:, None, :].broadcast_to([128, B, 128]),
                               m.memmask[:, :, None].broadcast_to([128, B, 128]), ALU.mult).then_inc(memv_masked, 1)
            for u in range(UN):
                q = tile(qt, u).rearrange("p j (h d) -> p j h d", h=HEADS)
                pool.wait_ge(qinv_ready, u + 1)
                pool.tensor_tensor(q, q, by_head(m.qinv[:, 16 * u:16 * u + 16]).unsqueeze(3)
                                   .broadcast_to([128, J, HEADS, DH]), ALU.mult).then_inc(qnorm_done, 1)


def peripheral_convolution(nc, m, sem, d):
    ps = m.ps
    zt = m.tmpA
    T = m.big
    yt_ready = sem("cv_zt_ready")
    yt_copied = sem("cv_zt_copied")
    t_ready = sem("cv_t_ready")
    t_copied_a = sem("cv_t_copied_a")
    t_copied_v = sem("cv_t_copied_v")
    turned = sem("cv_turned")
    turned_copied = sem("cv_turned_copied")
    made = sem("cv_made")
    rel_loaded = sem("cv_rel_loaded")
    out_ready = sem("cv_out_ready")
    out_copied = sem("cv_out_copied")
    out_stored = sem("cv_out_stored")
    out_loaded = sem("cv_out_loaded")
    added = sem("cv_added")
    NT = H * S

    with nc.Block() as block:
        @block.sync
        def _(sp):
            sp.wait_ge(turned_copied, 1)
            last = d.pos_w.shape[0] - 1
            for s in range(S):
                sp.dma_start(m.relt[:, s, :], toeplitz_rows(d.pos_w, last - (N - 1) - 128 * s - 127, 1,
                                                            (128, [[1, N]]))).then_inc(rel_loaded, 16)
            for h in range(2):
                sp.wait_ge(out_copied, 4 * (h + 1))
                for cc in range(4):
                    dst = m.scratch_x.rearrange("b (ci cc) n -> cc b ci n", cc=4)[cc]
                    sp.dma_start(dst[:, 4 * h:4 * h + 4, :], m.co[32 * cc:32 * cc + 32, 4 * h:4 * h + 4, :])\
                        .then_inc(out_stored, 16)
            sp.wait_ge(out_stored, 8 * 16)
            sp.dma_start(m.tmpB[:, :].rearrange("p (g n) -> p g n", g=G),
                         m.scratch_x.rearrange("(g j) c n -> (j c) g n", j=J)).then_inc(out_loaded, 16)

        @block.tensor
        def _(pe):
            for q in range(NCH):
                for i in range(4):
                    t = 4 * q + i
                    mm = pe.transpose(ps[:, q, i * 128:(i + 1) * 128], m.z[:, t * 128:(t + 1) * 128], m.ident[:, :])
                mm.then_inc(yt_ready, 1)
            pe.matmul(ps[:, 4, :], m.exchange[:, :], m.kmat_rev[:, :, :].rearrange("p s n -> p (s n)"),
                      start=True, stop=True).then_inc(turned, 1)
            for w in range(NT):
                y, s = divmod(w, S)
                if w < 4:
                    pe.wait_ge(yt_copied, w + 1)
                else:
                    pe.wait_ge(t_copied_a if w % 2 == 0 else t_copied_v, (w - 4) // 2 + 1)
                for i in range(3):
                    mm = pe.matmul(ps[:, w % 4, :], m.onehot[s][:, (R - y) * W:(R - y + 8) * W], m.bparts[s][:, i, :],
                                   start=(i == 0), stop=(i == 2))
                mm.then_inc(t_ready, 1)
            pe.wait_ge(t_copied_a, NT // 2)
            pe.wait_ge(t_copied_v, NT // 2)
            pe.wait_ge(rel_loaded, 16 * S)
            pe.matmul(ps[:, 5, :], m.exchange[:, :], m.relt[:, :, :].rearrange("p s n -> p (s n)"),
                      start=True, stop=True).then_inc(turned, 1)
            for ci in range(C // 4):
                if ci == 1:
                    pe.wait_ge(turned_copied, 2)
                for cc in range(4):
                    c = 4 * ci + cc
                    o = ps[32 * cc:32 * cc + 32, (4 + ci) % 8, 0:N]
                    for s in range(S):
                        lhsT = zt[:, s * G * 128 + c:(s + 1) * G * 128:C]
                        rhs = T[:, s, :, :].rearrange("p y (c x) -> p y c x", c=C)[:, :, c, :]
                        pe.matmul(o, lhsT, rhs, start=(s == 0), stop=False)
                        mm = pe.matmul(o, lhsT, m.kmat[:, s, :], start=False, stop=(s == S - 1))
                mm.then_inc(out_ready, 1)

        @block.scalar
        def _(act):
            for q in range(NCH):
                act.wait_ge(yt_ready, q + 1)
                act.activation(zt[:, :].rearrange("p (s g x) -> p g s x", s=S, g=G)[:, 2 * q:2 * q + 2],
                               ps[:, q, :].rearrange("p (g s x) -> p g s x", g=2, s=S),
                               ACT.Copy).then_inc(yt_copied, 1)
            for w in range(0, NT, 2):
                y, s = divmod(w, S)
                act.wait_ge(t_ready, w + 1)
                act.activation(T[:, s, y, :], ps[:, w % 4, :], ACT.Copy).then_inc(t_copied_a, 1)
            for ci in range(C // 4):
                act.wait_ge(out_ready, ci + 1)
                act.activation(m.co[:, ci, :], ps[:, (4 + ci) % 8, 0:N],
                               ACT.Copy).then_inc(out_copied, 1)

        @block.vector
        def _(dve):
            dve.wait_ge(turned, 1)
            dve.tensor_copy(m.kmat[:, :, :].rearrange("p s n -> p (s n)"), ps[:, 4, :]).then_inc(turned_copied, 1)
            for w in range(1, NT, 2):
                y, s = divmod(w, S)
                dve.wait_ge(t_ready, w + 1)
                dve.tensor_copy(T[:, s, y, :], ps[:, w % 4, :]).then_inc(t_copied_v, 1)
            dve.wait_ge(turned, 2)
            dve.tensor_copy(m.relt[:, :, :].rearrange("p s n -> p (s n)"), ps[:, 5, :]).then_inc(turned_copied, 1)
            prepare(dve, m, made)
            dve.wait_ge(out_loaded, 16)
            for k in range(NCH):
                c = slice(k * CH, (k + 1) * CH)
                dve.tensor_tensor(m.x[:, c], m.x[:, c], m.tmpB[:, c], ALU.add).then_inc(added, 1)


def linear_transformer(nc, m, sem):
    ps = m.ps
    zt = m.tmpA
    HALVES = range(2)
    GH = G // 2

    def pair(name):
        return [sem(f"lt_{name}_{hf}") for hf in HALVES]

    zt_ready = sem("lt_zt_ready")
    zt_copied = sem("lt_zt_copied")
    g_ready = pair("g_ready")
    g_masked = pair("g_masked")
    p_ready = pair("p_ready")
    p_copied = pair("p_copied")
    m_ready = pair("m_ready")
    a_made = pair("a_made")
    abd_made = pair("abd_made")
    r_ready = pair("r_ready")
    r_copied = pair("r_copied")
    wt_ready = pair("wt_ready")
    wt_copied = pair("wt_copied")
    wbd_made = pair("wbd_made")
    w_ready = pair("w_ready")
    w_copied = pair("w_copied")
    out_ready = sem("lt_out_ready")
    added = sem("lt_added")
    gbd, abd = m.gbd, m.abd

    def half(t, hf):
        return t[:, GH * hf:GH * hf + GH]

    def bank_mw(hf):
        return ps[:, 4 + 2 * hf, 0:GH * 32]

    def bank_rg(hf):
        return ps[:, 5 + 2 * hf, 0:GH * 32]

    def by_batch(t):
        return t.rearrange("p (g d) -> p g d", g=GH)

    def spread(dve, dst, src):
        return dve.tensor_tensor(dst.rearrange("p g (j c) -> p g j c", j=J),
                                 src.unsqueeze(2).broadcast_to([128, GH, J, 32]),
                                 m.blkone[:, :].rearrange("p (j c) -> p j c", j=J).unsqueeze(1)
                                 .broadcast_to([128, GH, J, 32]), ALU.mult)

    norm = token_norm(m, sem, "ln1", [m.x], [m.z], EPS_T, m.blkmean)

    with nc.Block() as block:
        @block.tensor
        def _(pe):
            norm.pe(pe)
            for q in range(NCH):
                pe.wait_ge(norm.done, q + 1)
                for i in range(4):
                    t = 4 * q + i
                    mm = pe.transpose(ps[:, q, i * 128:(i + 1) * 128], m.z[:, t * 128:(t + 1) * 128], m.ident[:, :])
                mm.then_inc(zt_ready, 1)
            for g in range(G):
                if g % 2 == 0:
                    pe.wait_ge(zt_copied, g // 2 + 1)
                for s in range(S):
                    t = 2 * g + s
                    mm = pe.matmul(ps[:, 5 + 2 * (g // GH), (g % GH) * 128:(g % GH) * 128 + 128],
                                   zt[:, t * 128:(t + 1) * 128], zt[:, t * 128:(t + 1) * 128],
                                   start=(s == 0), stop=(s == S - 1))
                if g % GH == GH - 1:
                    mm.then_inc(g_ready[g // GH], 1)
            for L in range(LAYERS):
                for hf in HALVES:
                    pe.wait_ge(g_masked[hf], L + 1)
                    for g in range(GH * hf, GH * hf + GH):
                        mm = pe.matmul(ps[:, g // 2, (g % 2) * 256:(g % 2) * 256 + 256], gbd[:, g, :],
                                       m.vt4[:, L * 256:(L + 1) * 256], start=True, stop=True)
                        if g % 2:
                            mm.then_inc(p_ready[hf], 1)
                for hf in HALVES:
                    pe.wait_ge(p_copied[hf], GH // 2 * (L + 1))
                    if L > 0:
                        pe.wait_ge(wt_copied[hf], L)
                    for h in range(ZHEADS):
                        mm = pe.matmul(bank_mw(hf), m.qbd[:, L, h, :], half(m.pmat, hf)[:, :, h * 32:(h + 1) * 32],
                                       start=(h == 0), stop=(h == ZHEADS - 1))
                    mm.then_inc(m_ready[hf], 1)
                for hf in HALVES:
                    pe.wait_ge(abd_made[hf], L + 1)
                    if L < LAYERS - 1:
                        for g in range(GH):
                            mm = pe.matmul(bank_rg(hf)[:, g * 32:(g + 1) * 32], half(gbd, hf)[:, g, :],
                                           half(m.amat, hf)[:, g, :], start=True, stop=True)
                        mm.then_inc(r_ready[hf], 1)
                    for g in range(GH):
                        mm = pe.matmul(bank_mw(hf)[:, g * 32:(g + 1) * 32], half(abd, hf)[:, g, :],
                                       half(m.wt, hf)[:, g, :], start=True, stop=True)
                    mm.then_inc(wt_ready[hf], 1)
                if L < LAYERS - 1:
                    for hf in HALVES:
                        pe.wait_ge(r_copied[hf], L + 1)
                        for g in range(GH):
                            mm = pe.matmul(bank_rg(hf)[:, g * 32:(g + 1) * 32], half(abd, hf)[:, g, :],
                                           half(m.rmat, hf)[:, g, :], start=True, stop=True)
                        mm.then_inc(g_ready[hf], 1)
            for hf in HALVES:
                pe.wait_ge(wbd_made[hf], 1)
                for g in range(GH):
                    mm = pe.transpose(ps[:, hf, g * 128:(g + 1) * 128], half(abd, hf)[:, g, :], m.ident[:, :])
                mm.then_inc(w_ready[hf], 1)
            for k in range(NCH):
                pe.wait_ge(w_copied[k // 2], 1)
                for h in range(2):
                    g = 2 * k + h
                    mm = pe.matmul(ps[:, (2, 3, 4, 6)[k], h * N:(h + 1) * N], gbd[:, g, :], m.z[:, g * N:(g + 1) * N],
                                   start=True, stop=True)
                mm.then_inc(out_ready, 1)

        @block.vector
        def _(dve):
            norm.dve(dve)
            for hf in HALVES:
                dve.wait_ge(g_ready[hf], 1)
                dve.tensor_tensor(half(gbd, hf), by_batch(ps[:, 5 + 2 * hf, :]),
                                  m.blkone[:, None, :].broadcast_to([128, GH, 128]), ALU.mult).then_inc(g_masked[hf], 1)
            for L in range(LAYERS):
                for hf in HALVES:
                    dve.wait_ge(m_ready[hf], L + 1)
                    if L > 0:
                        dve.wait_ge(g_ready[hf], L + 1)
                    dve.scalar_tensor_tensor(half(m.amat, hf), by_batch(bank_mw(hf)), 1.0 / (N * ZHEADS),
                                             m.ident32[:, None, :].broadcast_to([128, GH, 32]),
                                             ALU.mult, ALU.add).then_inc(a_made[hf], 1)
                    dve.wait_ge(a_made[hf], L + 1)
                    spread(dve, half(abd, hf), half(m.amat, hf)).then_inc(abd_made[hf], 1)
                if L < LAYERS - 1:
                    for hf in HALVES:
                        dve.wait_ge(g_ready[hf], L + 2)
                        spread(dve, half(gbd, hf), by_batch(bank_rg(hf))).then_inc(g_masked[hf], 1)
            for hf in HALVES:
                dve.wait_ge(wt_copied[hf], LAYERS)
                spread(dve, half(abd, hf), half(m.wt, hf)).then_inc(wbd_made[hf], 1)
            for hf in HALVES:
                dve.wait_ge(w_ready[hf], 1)
                dve.tensor_copy(half(gbd, hf).rearrange("p g d -> p (g d)"), ps[:, hf, :]).then_inc(w_copied[hf], 1)
            for k in range(NCH):
                c = slice(k * CH, (k + 1) * CH)
                dve.wait_ge(out_ready, k + 1)
                dve.tensor_tensor(m.x[:, c], m.x[:, c], ps[:, (2, 3, 4, 6)[k], :], ALU.add).then_inc(added, 1)

        @block.scalar
        def _(act):
            norm.act(act)
            for q in range(NCH):
                act.wait_ge(zt_ready, q + 1)
                act.activation(zt[:, q * CH:(q + 1) * CH], ps[:, q, :], ACT.Copy).then_inc(zt_copied, 1)
            for L in range(LAYERS):
                for q in range(NCH):
                    hf = q // (NCH // 2)
                    act.wait_ge(p_ready[hf], NCH // 2 * L + q % (NCH // 2) + 1)
                    act.activation(m.pmat[:, 2 * q:2 * q + 2, :].rearrange("p g d -> p (g d)"), ps[:, q, :],
                                   ACT.Copy).then_inc(p_copied[hf], 1)
                for hf in HALVES:
                    if L < LAYERS - 1:
                        act.wait_ge(r_ready[hf], L + 1)
                        act.activation(half(m.rmat, hf), by_batch(bank_rg(hf)), ACT.Copy).then_inc(r_copied[hf], 1)
                    act.wait_ge(wt_ready[hf], L + 1)
                    act.activation(half(m.wt, hf), by_batch(bank_mw(hf)), ACT.Copy).then_inc(wt_copied[hf], 1)


def mixture_of_experts(nc, m, sem):
    ps = m.ps
    z = m.z
    NT = G * S * J
    logits_ready = sem("me_logits_ready")
    steps = sem("me_steps")
    exp_done = sem("me_exp_done")
    parts_made = sem("me_parts_made")
    repeated = sem("me_repeated")
    gt_ready = sem("me_gt_ready")
    gt_copied = sem("me_gt_copied")
    gate_ready = sem("me_gate_ready")
    gated = sem("me_gated")
    out_ready = sem("me_out_ready")
    added = sem("me_added")

    GATE_BANKS, GZ = 6, 8
    steps_of = [(k, grp, j) for k in range(NCH) for grp in range(E // 4) for j in range(J)]
    NW = len(steps_of)

    def lots(t):
        return t.rearrange("p (t e) -> p t e", e=E)

    norm = token_norm(m, sem, "ln2", [m.x], [m.z], EPS_T, m.blkmean)

    with nc.Block() as block:
        @block.tensor
        def _(pe):
            norm.pe(pe)
            for t in range(G * S):
                if t % 4 == 0:
                    pe.wait_ge(norm.done, t // 4 + 1)
                mm = pe.matmul(ps[:, 0, t * 32:(t + 1) * 32], z[:, t * 128:(t + 1) * 128], m.rwbd[:, :],
                               start=True, stop=True)
            mm.then_inc(logits_ready, 1)
            pe.wait_ge(parts_made, 4)
            gt_ps = ps[:, 1:3, :].rearrange("p a n -> p (a n)").bitcast(BF16)
            for t in range(G * S):
                mm = pe.transpose(gt_ps[:, t * 128:(t + 1) * 128], m.gparts[:, t, :, :].rearrange("p a e -> p (a e)"),
                                  m.identb[:, :])
                if t % 8 == 7:
                    mm.then_inc(gt_ready, 1)
            pe.wait_ge(gt_copied, 2)

            def gate(w):
                k, grp, j = steps_of[w]
                if w >= GATE_BANKS:
                    pe.wait_ge(gated, w - GATE_BANKS + 1)
                pe.matmul(ps[:, w % GATE_BANKS, :], m.sele[:, 2 * j + grp, :],
                          m.gt[:, k * CH:(k + 1) * CH], start=True, stop=True).then_inc(gate_ready, 1)

            for w in range(J):
                gate(w)
            for q in range(NW // J):
                for w in range(J * (q + 1), min(J * (q + 2), NW)):
                    gate(w)
                k, grp, _ = steps_of[J * q]
                if grp == 0:
                    if k >= 2:
                        pe.wait_ge(added, k - 1)
                    for i in range(3):
                        pe.matmul(ps[:, 6 + k % 2, :], m.ebbd[:, i, :], m.gt[:, k * CH:(k + 1) * CH],
                                  start=(i == 0), stop=False)
                pe.wait_ge(gated, J * (q + 1))
                for j in range(J):
                    mm = pe.matmul(ps[32 * j:32 * j + 32, 6 + k % 2, :], m.ew4[:, grp, :], m.gz[:, (J * q + j) % GZ, :],
                                   start=False, stop=(grp == 1))
                mm.then_inc(out_ready, 1)

        @block.sync
        def _(sp):
            sp.wait_ge(norm.done, NCH)
            for j in range(J):
                for e in range(4):
                    sp.dma_start(m.zrep[32 * e:32 * e + 32, j, :], z[32 * j:32 * j + 32, :]).then_inc(repeated, 16)

        def add(dve, k):
            c = slice(k * CH, (k + 1) * CH)
            dve.wait_ge(out_ready, 2 * (k + 1))
            dve.tensor_tensor(m.x[:, c], m.x[:, c], ps[:, 6 + k % 2, :], ALU.add).then_inc(added, 1)

        @block.vector
        def _(dve):
            norm.dve(dve)
            n = 0

            def step(ins):
                nonlocal n
                ins.then_inc(steps, 1)
                n += 1
                dve.wait_ge(steps, n)

            l, k, one, sel = (lots(t) for t in (m.lg, m.key, m.one1, m.sel2))
            bc = [128, NT, E]
            st = m.stat
            dve.wait_ge(logits_ready, 1)
            step(dve.tensor_tensor(l, lots(ps[:, 0, :]), m.rb[:, None, :].broadcast_to(bc), ALU.add))
            step(dve.tensor_reduce(st[:, 0, :], l, AXX, ALU.max))
            rank = m.rank[:, None, :].broadcast_to(bc)
            step(dve.tensor_tensor(l, l, st[:, 0, :].unsqueeze(2).broadcast_to(bc), ALU.subtract))
            step(dve.scalar_tensor_tensor(k, l, 0.0, rank, ALU.is_ge, ALU.mult))
            step(dve.tensor_reduce(st[:, 1, :], k, AXX, ALU.max))
            step(dve.tensor_tensor(one, k, st[:, 1, :].unsqueeze(2).broadcast_to(bc), ALU.is_equal))
            step(dve.scalar_tensor_tensor(k, one, -3.0e38, l, ALU.mult, ALU.add))
            step(dve.tensor_reduce(st[:, 3, :], k, AXX, ALU.max))
            step(dve.tensor_tensor(k, k, st[:, 3, :].unsqueeze(2).broadcast_to(bc), ALU.is_ge))
            step(dve.tensor_tensor(k, k, rank, ALU.mult))
            step(dve.tensor_reduce(st[:, 1, :], k, AXX, ALU.max))
            step(dve.tensor_tensor(sel, k, st[:, 1, :].unsqueeze(2).broadcast_to(bc), ALU.is_equal))
            step(dve.tensor_tensor(sel, sel, one, ALU.add))
            dve.wait_ge(exp_done, 1)
            step(dve.tensor_tensor(sel, sel, lots(m.elg), ALU.mult))
            step(dve.tensor_reduce(st[:, 1, :], sel, AXX, ALU.add))
            step(dve.reciprocal(st[:, 2, :], st[:, 1, :]))
            step(dve.tensor_tensor(sel, sel, st[:, 2, :].unsqueeze(2).broadcast_to(bc), ALU.mult))
            g4 = m.sel2[:, :].rearrange("p (t e) -> p t e", t=G * S)
            r4 = m.key[:, :].rearrange("p (t e) -> p t e", t=G * S)
            dve.tensor_copy(m.gparts[:, :, 0, :], g4).then_inc(parts_made, 1)
            dve.wait_ge(parts_made, 2)
            step(dve.tensor_tensor(r4, g4, m.gparts[:, :, 0, :], ALU.subtract))
            dve.tensor_copy(m.gparts[:, :, 1, :], r4).then_inc(parts_made, 1)
            dve.wait_ge(parts_made, 3)
            step(dve.tensor_tensor(r4, r4, m.gparts[:, :, 1, :], ALU.subtract))
            dve.tensor_copy(m.gparts[:, :, 2, :], r4).then_inc(parts_made, 1)
            dve.wait_ge(repeated, 16 * J * 4)
            for w in range(NW):
                k, grp, j = steps_of[w]
                dve.wait_ge(gate_ready, w + 1)
                if w >= GZ and w % J == 0:
                    dve.wait_ge(out_ready, (w - GZ) // J + 1)
                dve.tensor_tensor(m.gz[:, w % GZ, :], m.zrep[:, j, k * CH:(k + 1) * CH], ps[:, w % GATE_BANKS, :],
                                  ALU.mult).then_inc(gated, 1)
                if w % E == E - 1 and k >= 1:
                    add(dve, k - 1)
            add(dve, NCH - 1)

        @block.scalar
        def _(act):
            norm.act(act)
            act.wait_ge(steps, 3)
            act.activation(m.elg[:, :], m.lg[:, :], ACT.Exp).then_inc(exp_done, 1)
            gt_ps = ps[:, 1:3, :].rearrange("p a n -> p (a n)").bitcast(BF16)
            for h in range(2):
                act.wait_ge(gt_ready, h + 1)
                act.activation(m.gt[:, h * 1024:(h + 1) * 1024], gt_ps[:, h * 1024:(h + 1) * 1024],
                               ACT.Copy).then_inc(gt_copied, 1)

        @block.gpsimd
        def _(pool):
            pool.memset(m.gparts[:, :, 3, :], 0.0).then_inc(parts_made, 1)


def squared_attention(nc, m, sem):
    ps = m.ps
    z = m.z
    vm = m.vm
    vtok = m.tmpA
    exact = [m.tmpB, m.rstd]
    projected = sem("sa_projected")
    silu_done = sem("sa_silu_done")
    cast_done = sem("sa_cast_done")
    split = sem("sa_split")
    stacked = sem("sa_stacked")
    sel_loaded = sem("sa_sel_loaded")
    sel_made = sem("sa_sel_made")
    arranged_ready = sem("sa_arranged_ready")
    arranged = [sem("sa_q_arranged"), sem("sa_k_arranged")]
    v_ready = sem("sa_v_ready")
    v_biased = sem("sa_v_biased")
    v_done = sem("sa_v_done")
    v_masked = sem("sa_v_masked")
    pos_ready = sem("sa_pos_ready")
    pos_copied = sem("sa_pos_copied")
    scores_ready = sem("sa_scores_ready")
    causal_done = sem("sa_causal_done")
    below_squared = sem("sa_below_squared")
    diag_squared = [sem("sa_diag_squared_v"), sem("sa_diag_squared_p")]
    act_done = sem("sa_act_done")
    pv_ready = sem("sa_pv_ready")
    pv_copied = sem("sa_pv_copied")
    order = [(g, hp, j) for g in range(G) for hp in range(2) for j in range(J)]
    NU = len(order)
    SLOTS = 8
    LAG = 6
    NPART = 3
    arrangement = [(k, j, hp, x) for k in range(NCH) for j in range(J) for hp in range(2) for x in range(2)]

    def arranged_to(w):
        k, j, hp, x = arrangement[w]
        b = j * G + 2 * k
        return m.qkt[:, x, hp, b:b + 2, :].rearrange("p b n -> p (b n)")

    def diagonal(u):
        return m.att[:, u % SLOTS, :, :].rearrange("p k (d n) -> p k d n", n=128)[:, :, 0::2, :]

    norm = token_norm(m, sem, "ln3", [m.x], [m.z], EPS_T, m.blkmean)

    with nc.Block() as block:
        @block.sync
        def _(sp):
            sp.dma_start(m.selqk32[:, :], m.d_selqk).then_inc(sel_loaded, 16)
            for p in range(NPART):
                if p == 0:
                    sp.wait_ge(cast_done, 2 * NCH)
                else:
                    sp.wait_ge(split, NCH * 5 if p == 1 else NCH * 6)
                for j in range(J):
                    sp.dma_start(m.qkstack[32 * p:32 * p + 32, :, j, :],
                                 m.qkparts[32 * j:32 * j + 32, :, p, :]).then_inc(stacked, 16)

        @block.tensor
        def _(pe):
            norm.pe(pe)
            for x in range(2):
                for k in range(NCH):
                    if x == 0:
                        pe.wait_ge(norm.done, k + 1)
                    pe.matmul(ps[:, NCH * x + k, :], m.wqkbd[:, x, :], z[:, k * CH:(k + 1) * CH],
                              start=True, stop=True).then_inc(projected, 1)
            for t in range(G * S):
                if t % 4 == 0:
                    pe.wait_ge(silu_done, t // 4 + 1)
                mm = pe.matmul(ps[:, t // 4, (t % 4) * 128:(t % 4) * 128 + 128], z[:, t * 128:(t + 1) * 128],
                               m.wvbd[:, :], start=True, stop=True)
                if t % 4 == 3:
                    mm.then_inc(v_ready, 1)
            pe.wait_ge(silu_done, 2 * NCH)
            pe.wait_ge(v_done, NCH)
            for g in range(G):
                for s in range(S):
                    mm = pe.matmul(ps[:, 4 + g // 2, (g % 2) * N:(g % 2) * N + N],
                                   vtok[:, (2 * g + s) * 128:(2 * g + s + 1) * 128], m.relt[:, s, :],
                                   start=(s == 0), stop=(s == S - 1))
                if g % 2:
                    mm.then_inc(pos_ready, 1)
            pe.wait_ge(v_biased, NCH)
            pe.wait_ge(sel_made, 1)
            pe.wait_ge(stacked, 16 * NPART * J)
            for w, (k, j, hp, x) in enumerate(arrangement):
                if w >= 4:
                    pe.wait_ge(arranged[x], (w - 4) // 2 + 1)
                pe.matmul(ps[:, w % 4, :], m.selqk[0:32 * NPART, x, hp, :],
                          m.qkstack[0:32 * NPART, x, j, k * CH:(k + 1) * CH],
                          start=True, stop=True).then_inc(arranged_ready, 1)

            def scores(u):
                g, hp, j = order[u]
                b = j * G + g
                if u == 2:
                    pe.wait_ge(pos_copied, NCH)
                if u >= 3:
                    pe.wait_ge(causal_done, u - 2)
                    pe.wait_ge(below_squared, u - 2)
                for s in range(S):
                    for k in range(2):
                        rows = slice(64 * k, 64 * k + 64)
                        mm = pe.matmul(ps[:, 2 * (u % 3) + k, s * N:N + s * 128],
                                       m.qkt[rows, 1, hp, b, s * 128:(s + 1) * 128],
                                       m.qkt[rows, 0, hp, b, s * 128:N], start=True, stop=True)
                mm.then_inc(scores_ready, 1)

            def values(u0):
                g = order[u0][0]
                if u0 % (2 * J) == 0 and g >= 2:
                    pe.wait_ge(pv_copied, g - 1)
                pe.wait_ge(act_done, u0 + 2)
                for k in range(2):
                    for s in range(S):
                        for u in (u0, u0 + 1):
                            g, hp, j = order[u]
                            h = 2 * hp + k
                            at = 0 if s == 0 else N
                            mm = pe.matmul(ps[32 * j:32 * j + 32, 6 + g % 2, s * 128:N], vm[:, (2 * g + s) * J + j, h, :],
                                           m.att[:, u % SLOTS, k, at:at + N - s * 128],
                                           start=(h == 0 and s == 0), stop=(h == AH - 1 and s == S - 1))
                            if k == 1 and s == S - 1:
                                mm.then_inc(pv_ready, 1)

            pe.wait_ge(arranged[0], len(arrangement) // 2)
            pe.wait_ge(arranged[1], len(arrangement) // 2)
            for u in range(0, NU + LAG, 2):
                if u < NU:
                    scores(u)
                    scores(u + 1)
                if u == LAG:
                    pe.wait_ge(v_masked, 1)
                if u >= LAG:
                    values(u - LAG)

        def copy_out(dve, g):
            dve.wait_ge(pv_ready, 2 * J * (g + 1))
            dve.tensor_copy(m.sa[:, g * N:(g + 1) * N], ps[:, 6 + g % 2, 0:N]).then_inc(pv_copied, 1)

        @block.vector
        def _(dve):
            norm.dve(dve)
            for x in range(2):
                for k in range(NCH):
                    c = slice(k * CH, (k + 1) * CH)
                    n = 3 * NCH * x
                    dve.wait_ge(cast_done, NCH * x + k + 1)
                    dve.tensor_tensor(exact[x][:, c], exact[x][:, c], m.qkparts[:, x, 0, c],
                                      ALU.subtract).then_inc(split, 1)
                    dve.wait_ge(split, n + 2 * k + 1)
                    dve.tensor_copy(m.qkparts[:, x, 1, c], exact[x][:, c]).then_inc(split, 1)
                for k in range(NCH):
                    c = slice(k * CH, (k + 1) * CH)
                    dve.wait_ge(split, n + 2 * k + 2)
                    dve.tensor_tensor(m.qkparts[:, x, 2, c], exact[x][:, c], m.qkparts[:, x, 1, c],
                                      ALU.subtract).then_inc(split, 1)
                if x == 0:
                    for k in range(NCH):
                        dve.wait_ge(v_ready, k + 1)
                        dve.tensor_tensor(vtok[:, k * CH:(k + 1) * CH].rearrange("p (a d) -> p a d", d=32),
                                          ps[:, k, :].rearrange("p (a d) -> p a d", d=32),
                                          m.bv[:, None, :].broadcast_to([128, 16, 32]), ALU.add).then_inc(v_biased, 1)
            for k in range(NCH):
                dve.wait_ge(pos_ready, k + 1)
                dve.tensor_copy(m.pa[:, k * CH:(k + 1) * CH], ps[:, 4 + k, :]).then_inc(pos_copied, 1)
            for w in range(0, len(arrangement), 2):
                dve.wait_ge(arranged_ready, w + 1)
                dve.tensor_copy(arranged_to(w), ps[:, w % 4, :]).then_inc(arranged[0], 1)
            dve.wait_ge(arranged_ready, len(arrangement))
            for u in range(NU):
                dve.wait_ge(scores_ready, u + 1)
                if u >= SLOTS:
                    dve.wait_ge(pv_ready, u - SLOTS + 1)
                dve.tensor_tensor(diagonal(u),
                                  ps[:, 2 * (u % 3):2 * (u % 3) + 2, :]
                                  .rearrange("p k (d n) -> p k d n", n=128)[:, :, 0:3:2, :],
                                  m.causal[:, None, None, :].broadcast_to([128, 2, 2, 128]),
                                  ALU.mult).then_inc(causal_done, 1)
                if u % 2:
                    dve.wait_ge(causal_done, u)
                    dve.tensor_tensor(diagonal(u - 1), diagonal(u - 1), diagonal(u - 1),
                                      ALU.mult).then_inc(diag_squared[0], 1)
                if u % 8 == 7 and u > 8:
                    copy_out(dve, u // 8 - 1)
            copy_out(dve, G - 1)

        @block.scalar
        def _(act):
            norm.act(act)
            for x in range(2):
                for k in range(NCH):
                    c = slice(k * CH, (k + 1) * CH)
                    act.wait_ge(projected, NCH * x + k + 1)
                    act.activation(exact[x][:, c], ps[:, NCH * x + k, :], ACT.Silu,
                                   bias=m.bqk[:, x:x + 1]).then_inc(silu_done, 1)
                    act.wait_ge(silu_done, NCH * x + k + 1)
                    act.activation(m.qkparts[:, x, 0, c], exact[x][:, c], ACT.Copy).then_inc(cast_done, 1)
            for k in range(NCH):
                c = slice(k * CH, (k + 1) * CH)
                act.wait_ge(v_biased, k + 1)
                act.activation(vtok[:, c], vtok[:, c], ACT.Silu).then_inc(v_done, 1)
            for w in range(1, len(arrangement), 2):
                act.wait_ge(arranged_ready, w + 1)
                act.activation(arranged_to(w), ps[:, w % 4, :], ACT.Copy).then_inc(arranged[1], 1)

            def silu(u):
                a = m.att[:, u % SLOTS, :, :].rearrange("p k n -> p (k n)")
                act.wait_ge(diag_squared[u % 2], u // 2 + 1)
                act.wait_ge(below_squared, u + 1)
                act.activation(a, a, ACT.Silu, scale=1.0 / AHD).then_inc(act_done, 1)

            for u in range(NU):
                act.wait_ge(causal_done, u + 1)
                act.activation(m.att[:, u % SLOTS, :, 128:N], ps[:, 2 * (u % 3):2 * (u % 3) + 2, 128:N],
                               ACT.Square).then_inc(below_squared, 1)
                if u >= 2:
                    silu(u - 2)
            silu(NU - 2)
            silu(NU - 1)

        @block.gpsimd
        def _(pool):
            pool.wait_ge(sel_loaded, 16)
            pool.tensor_copy(m.selqk[0:32 * NPART, :, :, :].rearrange("p x a b -> p (x a b)"),
                             m.selqk32[:, :]).then_inc(sel_made, 1)
            pool.wait_ge(v_done, NCH)
            pool.wait_ge(stacked, 16 * NPART * J)
            pool.tensor_tensor(vm[:, :, :, :], vtok[:, :].rearrange("p (t d) -> p t d", d=32).unsqueeze(2)
                               .broadcast_to([128, G * S * J, AH, 32]),
                               m.headmask[:, None, :, :].broadcast_to([128, G * S * J, AH, 32]),
                               ALU.mult).then_inc(v_masked, 1)
            for u in range(1, NU, 2):
                pool.wait_ge(causal_done, u + 1)
                pool.tensor_tensor(diagonal(u), diagonal(u), diagonal(u), ALU.mult).then_inc(diag_squared[1], 1)

    gamma = [(m.gam[:, i:i + 1], m.bet[:, i:i + 1]) for i in range(2)]
    norm = token_norm(m, sem, "sa_norm", [m.sa, m.pa], [m.sa, m.pa], EPS_A, m.blkmean64, gamma)

    u_ready = sem("sa_u_ready")
    gated = sem("sa_gated")
    f_ready = sem("sa_f_ready")
    relu_done = sem("sa_relu_done")
    summed = sem("sa_summed")
    both = ((1, m.pa), (0, m.sa))
    last_norm = token_norm(m, sem, "ln4", [m.x], [m.h], EPS_T, m.blkmean,
                           ready=lambda eng, k: eng.wait_ge(summed, NCH + k + 1))
    with nc.Block() as block:
        @block.tensor
        def _(pe):
            norm.pe(pe)
            for i, _ in both:
                for k in range(NCH):
                    if i == 0:
                        pe.wait_ge(norm.done, 2 * (k + 1))
                    pe.matmul(ps[:, 4 * i + k, :], m.wubd[:, i, :], z[:, k * CH:(k + 1) * CH],
                              start=True, stop=True).then_inc(u_ready, 1)
            for k in range(NCH):
                pe.wait_ge(gated, NCH + k + 1)
                for i, part in enumerate((m.sa, m.pa)):
                    mm = pe.matmul(ps[:, k, :], m.wfbd[:, i, :], part[:, k * CH:(k + 1) * CH],
                                   start=(i == 0), stop=(i == 1))
                mm.then_inc(f_ready, 1)
            last_norm.pe(pe)

        @block.vector
        def _(dve):
            norm.dve(dve)
            for w, (i, part) in enumerate(both):
                for k in range(NCH):
                    c = slice(k * CH, (k + 1) * CH)
                    dve.wait_ge(norm.shifted, 2 * k + i + 1)
                    dve.wait_ge(u_ready, NCH * w + k + 1)
                    dve.scalar_tensor_tensor(part[:, c], ps[:, 4 * i + k, :], m.bu[:, i:i + 1], part[:, c],
                                             ALU.add, ALU.mult).then_inc(gated, 1)
            for k in range(NCH):
                c = slice(k * CH, (k + 1) * CH)
                dve.tensor_tensor(m.x[:, c], m.x[:, c], z[:, c], ALU.add).then_inc(summed, 1)
            for k in range(NCH):
                c = slice(k * CH, (k + 1) * CH)
                dve.wait_ge(relu_done, k + 1)
                dve.wait_ge(summed, k + 1)
                dve.tensor_tensor(m.x[:, c], m.x[:, c], m.tmpB[:, c], ALU.add).then_inc(summed, 1)
            last_norm.dve(dve)

        @block.scalar
        def _(act):
            norm.act(act)
            for k in range(NCH):
                act.wait_ge(f_ready, k + 1)
                act.activation(m.tmpB[:, k * CH:(k + 1) * CH], ps[:, k, :], ACT.Relu,
                               bias=m.bf[:, 0:1]).then_inc(relu_done, 1)
            last_norm.act(act)


def routed_blocks(nc, m, sem):
    ps = m.ps
    h = m.h
    TOP = 64
    ut, htok, y0 = m.tmpA, m.tmpB, m.sa
    NU = 2 * G
    go = {e: sem("rb_go_" + e) for e in ("sp", "pe", "act")}
    go_dve = sem("rb_go_dve")
    settled = sem("rb_settled")
    matrices = sem("rb_matrices")
    dve_through = sem("rb_dve_through")
    cleared = sem("rb_cleared")
    probed = sem("rb_probed")
    loaded = sem("rb_loaded")
    NLOAD = 3
    up_loaded = sem("rb_up_loaded")
    mats_ready = sem("rb_mats_ready")
    mats_masked = sem("rb_mats_masked")
    u_ready = sem("rb_u_ready")
    u_copied = sem("rb_u_copied")
    ht_ready = sem("rb_ht_ready")
    ht_copied = sem("rb_ht_copied")
    s_ready = sem("rb_s_ready")
    max_done = sem("rb_max_done")
    negated = sem("rb_negated")
    exp_done = sem("rb_exp_done")
    t_ready = sem("rb_t_ready")
    t_copied_a = sem("rb_t_copied_a")
    t_copied_v = sem("rb_t_copied_v")
    pv_ready = sem("rb_pv_ready")
    inv_done = sem("rb_inv_done")
    y0_done = sem("rb_y0_done")
    y_ready = sem("rb_y_ready")
    y_copied = sem("rb_y_copied")
    z1_ready = sem("rb_z1_ready")
    relu_a = sem("rb_relu_a")
    relu_v = sem("rb_relu_v")
    z2_ready = sem("rb_z2_ready")
    z2_copied = sem("rb_z2_copied")
    ctl = sem("rb_ctl")
    added = sem("rb_added")
    per_block = [loaded, up_loaded, matrices, mats_ready, mats_masked, u_ready, u_copied, ht_ready, ht_copied, s_ready, max_done, negated,
                 exp_done, t_ready, t_copied_a, t_copied_v, pv_ready, inv_done, y0_done, y_ready, y_copied,
                 z1_ready, relu_a, relu_v, z2_ready, z2_copied]

    def state(eng, go_sem, regs):
        eng.wait_ge(go_sem, 1)
        eng.reg_load(regs, m.state[0:1, 0:3])
        eng.sem_clear(go_sem)

    def registers(eng, name):
        return [eng.alloc_register(f"{name}_{r}") for r in ("step", "op", "code")]

    with nc.Block() as block:
        @block.sync
        def _(sp):
            regs = registers(sp, "sp")
            state(sp, go["sp"], regs)
            with sp.While(lambda: sp.snap(regs[0]) < NB):
                at = sp.snap(regs[0], min_val=0, max_val=NB - 1) * NOPS + sp.snap(regs[1], min_val=0, max_val=NOPS - 1)
                at = sp.snap(at, min_val=0, max_val=NB * NOPS - 1)

                def row(t):
                    return t[bass.ds(at, 1)]
                sp.dma_start(m.w1[:, :], row(m.d_w1).broadcast_to([J, C, HID])).then_inc(up_loaded, 16)
                sp.dma_start(m.wsm[:, :, :].rearrange("d k (j c) -> d k j c", j=J),
                             row(m.d_small)[0].rearrange("d (k c) -> d k c", k=4)[:, :, None, :]
                             .broadcast_to([C, 4, J, C])).then_inc(matrices, 16)
                sp.dma_start(m.w2f[:, :], row(m.d_w2)[0]).then_inc(loaded, 16)
                sp.dma_start(m.b1[:, :], row(m.d_b1)[0]).then_inc(loaded, 16)
                sp.dma_start(m.b2[:, :], row(m.d_b2).broadcast_to([J, C, 1])).then_inc(loaded, 16)
                state(sp, go["sp"], regs)

        @block.tensor
        def _(pe):
            regs = registers(pe, "pe")

            def probe():
                pe.wait_ge(settled, 1)
                pe.transpose(ps[0:1, 0, 0:C], h[0:C, 0:1], m.ident[0:C, 0:C]).then_inc(probed, 1)
                pe.sem_clear(settled)

            def attention():
                for q in range(NCH):
                    for i in range(4):
                        t = 4 * q + i
                        mm = pe.transpose(ps[:, q, i * 128:(i + 1) * 128], h[:, t * 128:(t + 1) * 128], m.ident[:, :])
                    mm.then_inc(ht_ready, 1)
                pe.wait_ge(matrices, 16)
                for i, (a, b) in enumerate(((0, 1), (2, 3))):
                    mm = pe.matmul(ps[:, 6 + i, 0:128], m.wsm[:, a, :], m.wsm[:, b, :],
                                   start=True, stop=True)
                mm.then_inc(mats_ready, 1)
                pe.wait_ge(mats_masked, 2)
                for k in range(NCH):
                    pe.matmul(ps[:, 4 + k, :], m.sabd[:, :], h[:, k * CH:(k + 1) * CH],
                              start=True, stop=True).then_inc(u_ready, 1)
                def scores(u):
                    g, jp = divmod(u, 2)
                    if u == 0:
                        pe.wait_ge(ht_copied, NCH)
                    if u % 4 == 0:
                        pe.wait_ge(u_copied, u // 4 + 1)
                    if u >= 2:
                        pe.wait_ge(exp_done, 4 * (u - 1))
                    for s in range(S):
                        for i in range(2):
                            rows = slice(32 * (2 * jp + i), 32 * (2 * jp + i) + 32)
                            mm = pe.matmul(ps[:, 2 * (u % 2) + i, s * N:(s + 1) * N],
                                           ut[rows, g * N + s * 128:g * N + (s + 1) * 128],
                                           h[rows, g * N:(g + 1) * N], start=True, stop=True)
                    mm.then_inc(s_ready, 1)

                def transposes(u):
                    pe.wait_ge(exp_done, 4 * (u + 1))
                    if u == 0:
                        pe.wait_ge(u_copied, NCH)
                    if u >= 1:
                        pe.wait_ge(t_copied_a, u)
                        pe.wait_ge(t_copied_v, u)
                    for i in range(2):
                        for s in range(S):
                            for ms in range(S):
                                at = (2 * i + s) * N + ms * 128
                                mm = pe.transpose(ps[:, 4 + i, ms * N + s * 128:ms * N + s * 128 + 128],
                                                  m.ex[:, u % 2, at:at + 128], m.ident[:, :])
                    mm.then_inc(t_ready, 1)

                def values(u):
                    g, jp = divmod(u, 2)
                    if jp == 0 and g >= 2:
                        pe.wait_ge(y0_done, g - 1)
                    pe.wait_ge(t_copied_a, u + 1)
                    pe.wait_ge(t_copied_v, u + 1)
                    for part in range(2):
                        for s in range(S):
                            t = 2 * g + s
                            for i in range(2):
                                j = 2 * jp + i
                                rows = slice(32 * j, 32 * j + 32)
                                lhsT = htok[:, t * 128 + 32 * j:t * 128 + 32 * j + 32] if part == 0 else m.ones32[:, :]
                                mm = pe.matmul(ps[rows, 6 + g % 2, part * N:(part + 1) * N], lhsT,
                                               m.ext[:, u % 2, (2 * i + s) * N:(2 * i + s + 1) * N],
                                               start=(s == 0), stop=(s == S - 1))
                    mm.then_inc(pv_ready, 1)

                scores(0)
                scores(1)
                for u in range(NU):
                    transposes(u)
                    if u + 2 < NU:
                        scores(u + 2)
                    if u >= 1:
                        values(u - 1)
                values(NU - 1)
                for k in range(NCH):
                    pe.wait_ge(y0_done, 2 * (k + 1))
                    pe.matmul(ps[:, k, :], m.vobd[:, :], y0[:, k * CH:(k + 1) * CH],
                              start=True, stop=True).then_inc(y_ready, 1)
                pe.wait_ge(y_copied, NCH)

            def feed_forward():
                pe.wait_ge(up_loaded, 16)

                def up(w):
                    k, j = divmod(w, J)
                    rows = slice(32 * j, 32 * j + 32)
                    if w >= 6:
                        pe.wait_ge(relu_a if w % 2 == 0 else relu_v, (w - 6) // 2 + 1)
                    pe.matmul(ps[:, w % 6, :], m.w1[rows, :], h[rows, k * CH:(k + 1) * CH],
                              start=True, stop=True).then_inc(z1_ready, 1)

                for w in range(J):
                    up(w)
                for k in range(NCH):
                    for w in range(J * (k + 1), min(J * (k + 2), J * NCH)):
                        up(w)
                    if k == 0:
                        pe.wait_ge(loaded, 16 * NLOAD)
                    if k >= 2:
                        pe.wait_ge(z2_copied, k - 1)
                    pe.wait_ge(relu_a, 2 * (k + 1))
                    pe.wait_ge(relu_v, 2 * (k + 1))
                    for j in range(J):
                        mm = pe.matmul(ps[32 * j:32 * j + 32, 6 + k % 2, :], m.w2f[:, :], m.z1[:, (J * k + j) % 8, :],
                                       start=True, stop=True)
                    mm.then_inc(z2_ready, 1)
                pe.wait_ge(z2_copied, NCH)

            probe()
            state(pe, go["pe"], regs)
            with pe.While(lambda: pe.snap(regs[0]) < NB):
                with pe.If(pe.snap(regs[2]) > 1):
                    attention()
                with pe.Else():
                    pe.nop()
                with pe.If(pe.snap(regs[2]) < 3):
                    feed_forward()
                with pe.Else():
                    pe.nop()
                probe()
                state(pe, go["pe"], regs)

        @block.scalar
        def _(act):
            regs = registers(act, "act")

            def clear(loads=False):
                act.sem_inc(settled, 1)
                act.wait_ge(probed, 1)
                act.wait_ge(dve_through, 1)
                if loads:
                    act.wait_ge(matrices, 16)
                    act.wait_ge(up_loaded, 16)
                    act.wait_ge(loaded, 16 * NLOAD)
                for x in per_block:
                    act.sem_clear(x)
                act.sem_inc(cleared, 1)

            def attention():
                for k in range(NCH):
                    act.wait_ge(u_ready, k + 1)
                    act.activation(ut[:, k * CH:(k + 1) * CH], ps[:, 4 + k, :], ACT.Copy).then_inc(u_copied, 1)

                def copy_transposed(u):
                    act.wait_ge(t_ready, u + 1)
                    if u >= 2:
                        act.wait_ge(pv_ready, u - 1)
                    act.activation(m.ext[:, u % 2, 0:2 * N], ps[:, 4, :], ACT.Copy).then_inc(t_copied_a, 1)
                    if u % 2:
                        act.activation(m.ext[:, u % 2, 2 * N:4 * N], ps[:, 5, :], ACT.Copy).then_inc(t_copied_v, 1)

                for u in range(NU):
                    act.wait_ge(negated, u + 1)
                    if u >= 2:
                        act.wait_ge(t_ready, u - 1)
                    for i in range(2):
                        for s in range(S):
                            q = 2 * i + s
                            act.activation(m.ex[:, u % 2, q * N:(q + 1) * N],
                                           ps[:, 2 * (u % 2) + i, s * N:(s + 1) * N], ACT.Exp,
                                           bias=m.negmx[:, u, q:q + 1]).then_inc(exp_done, 1)
                    if u >= 1:
                        copy_transposed(u - 1)
                copy_transposed(NU - 1)
                for k in range(NCH):
                    act.wait_ge(y_ready, k + 1)
                    act.activation(h[:, k * CH:(k + 1) * CH], ps[:, k, :], ACT.Copy).then_inc(y_copied, 1)
                act.wait_ge(y_copied, NCH)

            def down(k):
                act.wait_ge(z2_ready, k + 1)
                act.activation(h[:, k * CH:(k + 1) * CH], ps[:, 6 + k % 2, :], ACT.Identity,
                               bias=m.b2[:, 0:1]).then_inc(z2_copied, 1)

            def feed_forward():
                act.wait_ge(loaded, 16 * NLOAD)
                for k in range(NCH):
                    for j in (0, 2):
                        w = J * k + j
                        act.wait_ge(z1_ready, w + 1)
                        if w >= 8:
                            act.wait_ge(z2_ready, (w - 8) // J + 1)
                        act.activation(m.z1[:, w % 8, :], ps[:, w % 6, :], ACT.Relu, bias=m.b1[:, 0:1]).then_inc(relu_a, 1)
                    if k >= 1:
                        down(k - 1)
                down(NCH - 1)
                act.wait_ge(z2_copied, NCH)

            clear()
            state(act, go["act"], regs)
            with act.While(lambda: act.snap(regs[0]) < NB):
                with act.If(act.snap(regs[2]) > 1):
                    attention()
                with act.Else():
                    act.nop()
                with act.If(act.snap(regs[2]) < 3):
                    feed_forward()
                with act.Else():
                    act.nop()
                clear(loads=True)
                state(act, go["act"], regs)

        @block.vector
        def _(dve):
            regs = registers(dve, "dve")

            def choose():
                n = 0

                def step(ins):
                    nonlocal n
                    ins.then_inc(ctl, 1)
                    n += 1
                    dve.wait_ge(ctl, n)

                r, key, one, sc = ps[0:1, 0, 0:NOPS], m.ckey, m.cone, m.csc
                dve.sem_inc(dve_through, 1)
                step(dve.scalar_tensor_tensor(m.ahead[:, :], m.revstep[:, :], m.lim[:, 0:1], m.revstep[:, :],
                                              ALU.is_le, ALU.mult))
                dve.wait_ge(probed, 1)
                step(dve.tensor_reduce(sc[:, 0:1], r, AXX, ALU.max))
                step(dve.scalar_tensor_tensor(key[:, :], r, sc[:, 0:1], m.revop[:, :], ALU.is_ge, ALU.mult))
                step(dve.tensor_reduce(sc[:, 1:2], key[:, :], AXX, ALU.max))
                step(dve.tensor_scalar(one[:, :], key[:, :], sc[:, 1:2], None, ALU.is_equal))
                step(dve.tensor_tensor(m.cprod[:, :, :], m.codes[:, :, :],
                                       one[:, None, :].broadcast_to([1, NB + 1, NOPS]), ALU.mult))
                step(dve.tensor_reduce(m.code[:, :], m.cprod[:, :, :], AXX, ALU.add))
                step(dve.scalar_tensor_tensor(m.cand[:, :], m.code[:, :], 0.5, m.ahead[:, :], ALU.is_gt, ALU.mult))
                step(dve.tensor_reduce(sc[:, 2:3], m.cand[:, :], AXX, ALU.max))
                step(dve.scalar_tensor_tensor(m.cand[:, :], m.revstep[:, :], sc[:, 2:3], m.code[:, :],
                                              ALU.is_equal, ALU.mult))
                dve.tensor_reduce(sc[:, 3:4], m.cand[:, :], AXX, ALU.add).then_inc(ctl, 1)
                dve.tensor_scalar(m.lim[:, :], sc[:, 2:3], -1.0, None, ALU.add).then_inc(ctl, 1)
                dve.tensor_scalar(m.state[:, 0:1], sc[:, 2:3], -1.0, float(TOP), ALU.mult, ALU.add).then_inc(ctl, 1)
                dve.tensor_scalar(m.state[:, 1:2], sc[:, 1:2], -1.0, float(TOP), ALU.mult, ALU.add).then_inc(ctl, 1)
                dve.wait_ge(ctl, n + 1)
                dve.tensor_copy(m.state[:, 2:3], sc[:, 3:4]).then_inc(ctl, 1)
                dve.wait_ge(ctl, n + 5)
                dve.wait_ge(cleared, 1)
                for x in (probed, dve_through, cleared, ctl):
                    dve.sem_clear(x)
                for x in list(go.values()) + [go_dve]:
                    dve.sem_inc(x, 1)

            def attention():
                for q in range(NCH):
                    dve.wait_ge(ht_ready, q + 1)
                    dve.tensor_copy(htok[:, q * CH:(q + 1) * CH], ps[:, q, :]).then_inc(ht_copied, 1)
                dve.wait_ge(mats_ready, 1)
                dve.scalar_tensor_tensor(m.sabd[:, :], ps[:, 6, 0:128], float(C) ** -0.5, m.blkone[:, :],
                                         ALU.mult, ALU.mult).then_inc(mats_masked, 1)
                dve.tensor_tensor(m.vobd[:, :], ps[:, 7, 0:128], m.blkone[:, :], ALU.mult).then_inc(mats_masked, 1)

                def copy_transposed(u):
                    dve.wait_ge(t_ready, u + 1)
                    if u >= 2:
                        dve.wait_ge(pv_ready, u - 1)
                    dve.tensor_copy(m.ext[:, u % 2, 2 * N:4 * N], ps[:, 5, :]).then_inc(t_copied_v, 1)

                def normalise(g):
                    dve.wait_ge(pv_ready, 2 * (g + 1))
                    dve.reciprocal(m.rd[:, g % 2, :], ps[:, 6 + g % 2, N:2 * N]).then_inc(inv_done, 1)
                    dve.wait_ge(inv_done, g + 1)
                    dve.tensor_tensor(y0[:, g * N:(g + 1) * N], ps[:, 6 + g % 2, 0:N], m.rd[:, g % 2, :],
                                      ALU.mult).then_inc(y0_done, 1)

                for u in range(NU):
                    dve.wait_ge(s_ready, u + 1)
                    b = 2 * (u % 2)
                    dve.tensor_reduce(m.mx[:, u, :], ps[:, b:b + 2, :].rearrange("p i (s m) -> p (i s) m", s=S),
                                      AXX, ALU.max).then_inc(max_done, 1)
                    dve.wait_ge(max_done, u + 1)
                    dve.tensor_scalar(m.negmx[:, u, :], m.mx[:, u, :], -1.0, None, ALU.mult).then_inc(negated, 1)
                    if u % 2:
                        copy_transposed(u - 1)
                    if u >= 4 and u % 2 == 0:
                        normalise((u - 4) // 2)
                normalise(G - 2)
                normalise(G - 1)
                dve.wait_ge(y0_done, G)

            def feed_forward():
                dve.wait_ge(loaded, 16 * NLOAD)
                for k in range(NCH):
                    for j in (1, 3):
                        w = J * k + j
                        dve.wait_ge(z1_ready, w + 1)
                        if w >= 8:
                            dve.wait_ge(z2_ready, (w - 8) // J + 1)
                        dve.tensor_scalar(m.z1[:, w % 8, :], ps[:, w % 6, :], m.b1[:, 0:1], 0.0, ALU.add,
                                          ALU.max).then_inc(relu_v, 1)
                dve.wait_ge(relu_v, 2 * NCH)

            choose()
            state(dve, go_dve, regs)
            with dve.While(lambda: dve.snap(regs[0]) < NB):
                with dve.If(dve.snap(regs[2]) > 1):
                    attention()
                with dve.Else():
                    dve.nop()
                with dve.If(dve.snap(regs[2]) < 3):
                    feed_forward()
                with dve.Else():
                    dve.nop()
                choose()
                state(dve, go_dve, regs)

    with nc.Block() as block:
        @block.vector
        def _(dve):
            for k in range(NCH):
                c = slice(k * CH, (k + 1) * CH)
                dve.tensor_tensor(m.x[:, c], m.x[:, c], h[:, c], ALU.add).then_inc(added, 1)

        @block.sync
        def _(sp):
            stored = sem("rb_stored")
            for k in range(NCH):
                sp.wait_ge(added, k + 1)
                sp.dma_start(m.d_out.rearrange("(g j) c n -> (j c) g n", j=J)[:, 2 * k:2 * k + 2, :],
                             m.x[:, k * CH:(k + 1) * CH].rearrange("p (g n) -> p g n", g=2)).then_inc(stored, 16)
            sp.wait_ge(stored, 16 * NCH)


def place(nc, m, ctx):
    def sb(name, shape, dt=F32):
        return ctx.enter_context(nc.sbuf_tensor(name, shape, dt))

    m.ps = ctx.enter_context(nc.psum_tensor("ps", [128, 8, CH], F32))
    R_ = sb("R", [128, 4 * B * N])
    P_ = sb("P", [128, 2 * COLS])
    Q_ = sb("Q", [128, 2 * COLS])
    m.x = sb("x", [128, COLS])
    m.z = sb("z", [128, COLS])
    m.tmpA = sb("tmpA", [128, COLS])
    m.tmpB, m.rstd = Q_[:, 0:COLS], Q_[:, COLS:2 * COLS]

    def view(at, names, dims, dt=F32, base=R_):
        size = 1
        for d in dims:
            size *= d
        t = base[:, at:at + (size // 2 if dt == BF16 else size)]
        if dt != F32:
            t = t.bitcast(dt)
        if len(dims) == 1:
            return t
        letters = "abcde"[:len(dims)]
        kw = {letters[i]: dims[i] for i in range(1, len(dims))}
        return t.rearrange(f"p ({' '.join(letters)}) -> p {' '.join(letters)}", **kw)

    r = B * N
    m.r0, m.r1, m.r2, m.r3 = (view(i * r, "", [B, N]) for i in range(4))
    m.memv_b = view(0, "", [B, 128], base=P_)
    m.wvq = view(COLS + 1024, "", [2, 512], base=Q_)
    m.ct = view(0, "", [B, 128], base=Q_)
    m.big = view(0, "", [S, H, CH])
    m.co = view(3 * r + 4608, "", [C // 4, N])
    at = 2 * r
    m.qv = view(at, "", [LAYERS * ZHEADS * (128 + 32)])
    m.qbd = view(at, "", [LAYERS, ZHEADS, 128]); at += LAYERS * ZHEADS * 128
    m.vt4 = view(at, "", [LAYERS * ZHEADS * 32]); at += LAYERS * ZHEADS * 32
    m.gbd = view(at, "", [G, 128]); at += G * 128
    m.abd = view(at, "", [G, 128]); at += G * 128
    m.pmat = view(at, "", [G, ZHEADS * 32]); at += G * ZHEADS * 32
    m.amat = view(at, "", [G, 32]); at += G * 32
    m.wt = view(at, "", [G, 32]); at += G * 32
    m.rmat = view(at, "", [G, 32]); at += G * 32
    at = 3 * r + COLS + 1024
    m.ew4 = view(at, "", [E // 4, C])
    m.zrep = view(r, "", [J, COLS])
    m.sele = view(3 * r + 4608 + COLS, "", [E, 128], BF16)
    at = 0
    nl = G * S * J * E
    m.lg = view(at, "", [nl]); at += nl
    m.elg = view(at, "", [nl]); at += nl
    m.key = view(at, "", [nl]); at += nl
    m.one1 = view(at, "", [nl]); at += nl
    m.sel2 = view(at, "", [nl]); at += nl
    m.gparts = view(at, "", [G * S, 4, 32], BF16); at += G * S * 64
    m.stat = view(at, "", [4, G * S * J]); at += 4 * G * S * J
    m.gt = view(at, "", [COLS], BF16); at += COLS // 2
    m.gz = view(2 * r, "", [8, CH])
    m.vm = view(2 * r, "", [G * S * J, AH, 32])
    m.qkt = view(0, "", [2, 2, B, N], BF16)
    m.qkparts = view(2 * r, "", [2, 3, COLS], BF16)
    m.qkstack = view(3 * r, "", [2, J, COLS], BF16)
    m.selqk = view(COLS, "", [2, 2, 128], BF16, base=P_)
    m.selqk32 = view(COLS + 256, "", [2 * 2 * 128], base=P_)[0:96]
    m.att = view(3 * r, "", [8, 2, 3 * 128])
    m.sa = view(3 * r + 8 * 768, "", [COLS])
    m.pa = P_[:, 0:COLS]
    m.h = view(0, "", [COLS])
    m.ex = view(2 * r, "", [2, 4 * N])
    m.ext = view(2 * r + 8 * N, "", [2, 4 * N])
    m.z1 = view(2 * r - 8 * CH, "", [8, CH])

    def packed(t, dims_of):
        out, at = [], 0
        for dims in dims_of:
            out.append(view(at, "", dims, base=t))
            at += int(np.prod(dims))
        assert at == t.shape[1]
        return out

    m.early = sb("early", [128, EARLY])
    (m.exchange, m.ol, m.orr, m.wqkv, m.wo, m.memk, m.memv, m.memmask, m.gcol, m.bout, wcomp) = packed(
        m.early, [[128], [23 * W], [23 * W], [384], [C], [MEM], [128], [B], [1], [1], [CONV_P * CONV_P]])
    m.wcomp = wcomp[0:C]
    m.lasting = sb("lasting", [128, LASTING])
    (m.ident, m.blkone, m.causal, m.headmask, m.ident32, m.rank, m.jmask, m.rb, m.ebrep, m.bv, m.gam,
     m.bet, m.bu, m.bf, m.bqk, m.wqkbd, m.wvbd, m.rwbd, m.wubd, m.wfbd, revop, revstep) = packed(
        m.lasting, [[128], [128], [128], [AH, 32], [32], [E], [J], [E], [C], [C], [2], [2], [2], [1], [2],
                    [2, 128], [128], [J * E], [2, 128], [2, 128], [NOPS], [NB + 1]])
    m.revop, m.revstep = revop[0:1], revstep[0:1]
    m.gather = sb("gather", [128, G, B])
    m.scatter = sb("scatter", [B, G, 128])
    m.identb = sb("identb", [128, 128], BF16)
    m.blkmean = sb("blkmean", [128, 128])
    m.blkmean64 = sb("blkmean64", [128, 128])
    m.sele32 = view(3 * r + 7168, "", [E, 128])
    m.ones32 = sb("ones32", [128, 32])
    m.eps = sb("eps", [128, 2])
    m.gs = sb("gs", [128, 1])
    m.small = sb("small", [128, 4])
    m.bst = sb("bst", [128, 6 * G])
    m.bag = sb("bag", [128, 2 * G])
    m.std8 = sb("std8", [128, G])
    m.inv8 = sb("inv8", [128, G])
    m.kmax = sb("kmax", [128, B])
    m.knegmax = sb("knegmax", [128, B])
    m.ksum = sb("ksum", [128, B])
    m.memsum = sb("memsum", [128, B])
    m.em = m.blkmean
    m.emt = m.blkmean64
    m.qmax, m.qsum, m.qinv = (m.z[:, i * 256:(i + 1) * 256] for i in range(3))
    m.w2 = view(0, "", [B, C], base=P_)
    m.wclass = view(COLS + 512, "", [CLASSES, 2 * R + 1], base=Q_)[0:C]
    m.bl = view(3 * r, "", [C, W])
    m.br = view(3 * r + CH, "", [C, W])
    m.bparts = (view(0, "", [3, CH], BF16, base=P_), view(3 * r + 3200, "", [3, CH], BF16))
    m.onehot = (view(3 * r + 3200 + 768, "", [23 * W], BF16), view(3 * r + 3200 + 768 + 192, "", [23 * W], BF16))
    m.kmat = view(2 * CH, "", [S, N], base=P_)
    m.ebpart = sb("ebpart", [128, 3, C], BF16)
    m.ebbd = sb("ebbd", [128, 3, 128], BF16)
    m.relt = sb("relt", [128, S, N])
    m.kmat_rev = m.relt
    m.wsm = view(COLS + 12 * N + 6 * CH + 2 * N + 1280, "", [4, 128])[0:C]
    m.w1 = view(0, "", [HID], base=m.early)
    m.w2f = view(128, "", [C], base=m.early)
    m.b1 = sb("b1", [128, 1])
    m.b2 = sb("b2", [128, 1])
    m.sabd = view(COLS + 12 * N + 6 * CH + 2 * N + 1024, "", [128])
    m.vobd = view(COLS + 12 * N + 6 * CH + 2 * N + 1152, "", [128])
    m.mx = view(160, "", [2 * G, 2 * S], base=m.early)
    m.negmx = view(224, "", [2 * G, 2 * S], base=m.early)
    m.rd = view(COLS + 12 * N + 6 * CH, "", [2, N])
    m.state = sb("state", [1, 4], I32)
    m.ckey = sb("ckey", [1, NOPS])
    m.cone = sb("cone", [1, NOPS])
    m.code = sb("code", [1, NB + 1])
    m.cand = sb("cand", [1, NB + 1])
    m.ahead = sb("ahead", [1, NB + 1])
    m.codes = view(COLS + 1024, "", [NB + 1, NOPS], base=P_)[0:1]
    m.cprod = view(COLS + 12 * N + 6 * CH + 2 * N, "", [NB + 1, NOPS])[0:1]
    m.masks = view(3 * r + 1792, "", [2, NB * NOPS], I32)[0:1]
    m.maskf = view(2 * r + 5120, "", [NB * NOPS])[0:1]
    m.maskaf = view(2 * r + 5120 + 1024, "", [NB * NOPS])[0:1]
    m.csc = sb("csc", [1, 8])
    m.lim = sb("lim", [1, 1])


def toeplitz_rows(tensor_ap, first, row_step, dims):
    return bass.AP(tensor=tensor_ap.tensor, offset=tensor_ap.offset + first, ap=[[row_step, dims[0]]] + dims[1])


def load_first(nc, m, sem, d):
    x_loaded = [sem(f"ld_x_loaded_{k}") for k in range(NCH)]
    set_up = sem("ld_set_up")

    def start_sp(sp):
        src = d.x.rearrange("(g j) c n -> (j c) g n", j=J)
        for k in range(NCH):
            sp.dma_start(m.x[:, k * CH:(k + 1) * CH].rearrange("p (g n) -> p g n", g=2),
                         src[:, 2 * k:2 * k + 2, :]).then_inc(x_loaded[k], 16)
        for s in range(S):
            for y in range(H // S):
                first = KS // 2 - R
                src = toeplitz_rows(d.kpe, (first + y + (S - 1 - s) * (H // S)) * KS + first, 1,
                                    (W, [[KS, H], [1, W]]))
                sp.dma_start(m.kmat_rev[16 * y:16 * y + 16, s, :].rearrange("p (y x) -> p y x", y=H),
                             src).then_inc(m.loaded_kpe, 16)
        sp.wait_ge(m.loaded, 16 * 4)

    def start_act(act):
        act.dma_start(m.gather[:, :, :], d.gather).then_inc(m.loaded, 16)
        act.dma_start(m.scatter[:, :, :], d.scatter).then_inc(m.loaded, 16)
        act.dma_start(m.early[:, :], d.early).then_inc(m.loaded, 16)
        act.dma_start(m.lasting[:, :], d.lasting).then_inc(m.loaded, 16)
        act.wait_ge(set_up, 4)

    def set_values(pool):
        pool.memset(m.eps[:, 0:1], EPS_GN).then_inc(set_up, 1)
        pool.memset(m.eps[:, 1:2], EPS_A).then_inc(set_up, 1)
        pool.memset(m.ones32[:, :], 1.0).then_inc(set_up, 1)
        pool.memset(m.lim[:, :], 64.0).then_inc(set_up, 1)

    instance_norm(nc, m, sem, "gn0", m.x, m.z, x_loaded, start_sp, start_act, set_values)


def load_second(nc, m, sem, d):
    def start(sp):
        sp.dma_start(m.qv[:, :], d.qv).then_inc(m.loaded, 16)
        sp.dma_start(m.ew4[:, :, :], d.ew4).then_inc(m.loaded, 16)
        sp.dma_start(m.sele32[:, :, :], d.sele).then_inc(m.loaded, 16)
        sp.dma_start(m.masks[:, :, :], d.masks).then_inc(m.loaded, 16)
        sp.wait_ge(m.loaded_kpe, 16 * S * (H // S))

    cast = sem("l2_cast")
    left = sem("l2_left")
    rest = [t[:, :, :].rearrange("p c x -> p (c x)") for t in (m.bl, m.br)]

    def first_parts(act):
        for s, t in enumerate((m.ol, m.orr)):
            act.activation(m.onehot[s][:, :], t[:, :], ACT.Copy).then_inc(cast, 1)
        act.wait_ge(m.loaded_classes, 16 * 16)
        for s in range(2):
            act.activation(m.bparts[s][:, 0, :], rest[s], ACT.Copy).then_inc(cast, 1)

    def second_parts(act):
        for s in range(2):
            act.wait_ge(left, s + 1)
            act.activation(m.bparts[s][:, 1, :], rest[s], ACT.Copy).then_inc(cast, 1)

    def leave(pool):
        pool.wait_ge(m.loaded_classes, 16 * 16)
        for s in range(2):
            pool.wait_ge(cast, s + 3)
            pool.tensor_tensor(rest[s], rest[s], m.bparts[s][:, 0, :], ALU.subtract).then_inc(left, 1)
        for s in range(2):
            pool.wait_ge(cast, s + 5)
            pool.tensor_tensor(m.bparts[s][:, 2, :], rest[s], m.bparts[s][:, 1, :], ALU.subtract).then_inc(left, 1)

    instance_norm(nc, m, sem, "gn1", m.x, m.z, None, start, first_parts, leave, second_parts)


def prepare(dve, m, made):
    n = 0

    def step(ins):
        nonlocal n
        ins.then_inc(made, 1)
        n += 1
        dve.wait_ge(made, n)

    dve.wait_ge(m.loaded, 16 * 8)
    step(dve.tensor_copy(m.identb[:, :], m.ident[:, :]))
    step(dve.tensor_scalar(m.blkmean[:, :], m.blkone[:, :], 1.0 / C, None, ALU.mult))
    step(dve.tensor_scalar(m.blkmean64[:, :], m.blkone[:, :], 0.5 / C, None, ALU.mult))
    for i in range(3):
        step(dve.tensor_copy(m.ebpart[:, i, :], m.ebrep[:, :]))
        step(dve.tensor_tensor(m.ebrep[:, :], m.ebrep[:, :], m.ebpart[:, i, :], ALU.subtract))
        step(dve.tensor_tensor(m.ebbd[:, i, :].rearrange("p (j c) -> p j c", j=J),
                               m.ebpart[:, i, None, :].broadcast_to([128, J, C]),
                               m.jmask[:, :, None].broadcast_to([128, J, C]), ALU.mult))
    step(dve.tensor_copy(m.sele[:, :, :], m.sele32[:, :, :]))
    step(dve.tensor_copy(m.wt[:, :, :], m.ident32[:, None, :].broadcast_to([128, G, 32])))
    cd = m.codes[:, 0:NB, :].rearrange("a s o -> a (s o)")
    step(dve.memset(m.codes[:, NB:NB + 1, :], 1.0))
    step(dve.tensor_copy(cd, m.masks[:, 1, :]))
    step(dve.tensor_copy(m.maskf[:, :], m.masks[:, 0, :]))
    step(dve.tensor_tensor(m.maskaf[:, :], m.maskf[:, :], cd, ALU.mult))
    step(dve.scalar_tensor_tensor(cd, m.maskf[:, :], 3.0, cd, ALU.mult, ALU.add))
    step(dve.scalar_tensor_tensor(cd, m.maskaf[:, :], -2.0, cd, ALU.mult, ALU.add))


def conv_attn_hybrid(nc, d):
    m = Mem()
    with ExitStack() as ctx:
        def stages(*runs, last=False):
            sems = []
            with ExitStack() as own:
                def sem(name):
                    sems.append(own.enter_context(nc.semaphore(name)))
                    return sems[-1]
                for run, *args in runs:
                    run(nc, m, sem, *args)
                if not last:
                    with nc.Block() as block:
                        @block.gpsimd
                        def _(pool):
                            for s in sems[0::4]:
                                pool.sem_clear(s)

                        @block.vector
                        def _(dve):
                            for s in sems[1::4]:
                                dve.sem_clear(s)

                        @block.scalar
                        def _(act):
                            for s in sems[2::4]:
                                act.sem_clear(s)

                        @block.tensor
                        def _(pe):
                            for s in sems[3::4]:
                                pe.sem_clear(s)

        place(nc, m, ctx)
        m.scratch_w = nc.dram_tensor("scratch_w", [C, CLASSES, 2 * R + 1], F32, kind="Internal").ap()
        m.scratch_x = nc.dram_tensor("scratch_x", [B, C, N], F32, kind="Internal").ap()
        m.d_out = d.out
        m.d_selqk = d.selqk
        m.d_small, m.d_w1, m.d_w2, m.d_b1, m.d_b2 = d.small4, d.w1, d.w2, d.b1, d.b2
        m.loaded = ctx.enter_context(nc.semaphore("loaded"))
        m.loaded_classes = ctx.enter_context(nc.semaphore("loaded_classes"))
        m.classes_stored = ctx.enter_context(nc.semaphore("classes_stored"))
        m.loaded_kpe = ctx.enter_context(nc.semaphore("loaded_kpe"))
        stages((load_first, d), (linear_attention,), (load_second, d), (peripheral_convolution, d),
               (linear_transformer,))
        stages((mixture_of_experts,), (squared_attention,),
               (routed_blocks,), last=True)


def constants():
    import numpy as np
    p = np.arange(128)
    f = np.float32
    out = {"ident": np.eye(128, dtype=f),
           "blkone": (p[:, None] // 32 == p[None, :] // 32).astype(f),
           "causal": (p[:, None] <= p[None, :]).astype(f),
           "memmask": (p[:, None] // MEM == np.arange(B)[None, :]).astype(f),
           "exchange": np.eye(128, dtype=f)[::-1],
           "ident32": (p[:, None] % 32 == np.arange(32)[None, :]).astype(f),
           "rank": np.broadcast_to(np.arange(E, 0, -1), (128, E)).astype(f),
           "revop": (64 - np.arange(NOPS))[None, :].astype(f),
           "revstep": (64 - np.arange(NB + 1))[None, :].astype(f)}
    part, j, e = p // 32, p // E % J, p % E
    live = part < 3
    out["jmask"] = (live[:, None] & (j[:, None] == np.arange(J))).astype(f)
    q = np.arange(2 * J)
    out["sele"] = (live[:, None, None] & (j[:, None, None] == q[None, :, None] // 2)
                   & (e[:, None, None] == 4 * (q[None, :, None] % 2) + p // C)).astype(f)
    b = np.arange(B)
    own = (p[:, None] // C == b[None, :] % J)[:, None, :] & (b[None, None, :] // J == np.arange(G)[None, :, None])
    out["gather"] = own.astype(f)
    out["scatter"] = own.transpose(2, 1, 0).astype(f)
    out["headmask"] = np.broadcast_to(np.arange(32)[None, :] // AHD == np.arange(AH)[:, None],
                                      (128, AH, 32)).astype(f)
    terms = ((0, 0, 0, 1, 1, 2), (0, 1, 2, 0, 1, 0))
    sel = np.zeros((3, AH, AHD, 2, 2, 2, 8, AHD), f)
    for x in range(2):
        for h in range(AH):
            for term, part_of in enumerate(terms[x]):
                sel[part_of, h, :, x, h // 2, h % 2, term, :] = np.eye(AHD)
    out["selqk"] = sel.reshape(96, 512)
    for name, first, lo in (("ol", 0, -R), ("orr", 1, -R + 8)):
        t = np.zeros((8, 16, 23, 16), f)
        for q in range(8):
            a, b = CLASS_SPANS[first + q]
            for dy in range(max(a, lo), min(b, lo + 22) + 1):
                t[q, :, dy - lo, :] = np.eye(16)[::-1]
        out[name] = t.reshape(128, 23 * 16)
    return out


def kernel(**inputs):
    import numpy as np
    import concourse.bacc as bacc
    from concourse.bass_utils import run_bass_kernel_spmd

    a = {k: np.asarray(v) for k, v in inputs.items()}
    f = "L3_ffn_"
    def tile(t):
        return np.tile(t, (J, 1))

    def diagonal(t):
        out = np.zeros((J, C, J, t.shape[1]), t.dtype)
        for j in range(J):
            out[j, :, j] = t
        return out.reshape(128, -1)

    def rows(t, n=128):
        return np.repeat(t.reshape(1, -1), n, axis=0)

    def below(t):
        return np.concatenate([t, np.zeros((128 - t.shape[0], t.shape[1]), t.dtype)])

    c = constants()
    eb, ew = a["L2_ffn_expert_b"], a["L2_ffn_expert_w"]
    wu, wf = a["L3_attn_Wu"], a["L3_attn_Wf"]
    early = [c["exchange"], c["ol"], c["orr"], tile(a["L0_conv_w_qkv"].T), a["L0_conv_w_out"].T,
             a["L0_conv_mem_kv"][0].reshape(HEADS * DH, MEM),
             np.tile(a["L0_conv_mem_kv"][1].transpose(2, 0, 1).reshape(MEM, HEADS * DH), (B, 1)), c["memmask"],
             tile(a["L0_conv_g"].reshape(C, 1)), tile(a["L0_conv_b_out"].reshape(C, 1)),
             below(a["L1_conv_weight_comp"])]
    lasting = [c["ident"], c["blkone"], c["causal"], c["headmask"].reshape(128, -1), c["ident32"], c["rank"],
               c["jmask"], rows(a["L2_ffn_router_b"]), np.tile(eb, (128 // E, 1)), rows(a["L3_attn_bv"]),
               tile(a["L3_attn_ln_gamma"].reshape(2, C).T), tile(a["L3_attn_ln_beta"].reshape(2, C).T),
               tile(a["L3_attn_bu"].reshape(2, C).T), tile(a["L3_attn_bf"].reshape(C, 1)),
               tile(np.stack([a["L3_attn_bq"], a["L3_attn_bk"]], axis=1)),
               diagonal(a["L3_attn_Wq"]), diagonal(a["L3_attn_Wk"]), diagonal(a["L3_attn_Wv"]),
               diagonal(a["L2_ffn_router_w"]), diagonal(wu[:, :C]), diagonal(wu[:, C:]), diagonal(wf[:C]),
               diagonal(wf[C:]), rows(c["revop"]), rows(c["revstep"])]
    z_mats = [a["L2_attn_" + n].reshape(LAYERS * ZHEADS, 32, 32).transpose(0, 2, 1)
              for n in ("q_matrix", "v_matrix")]
    arrays = {
        "x": a["x"].reshape(B, C, N),
        "early": np.concatenate(early, axis=1),
        "lasting": np.concatenate(lasting, axis=1),
        "gather": c["gather"], "scatter": c["scatter"], "sele": c["sele"], "selqk": c["selqk"],
        "kpe": a["L1_conv_kpe"].reshape(KS, KS)[::-1, ::-1],
        "pos_w": a["L3_attn_pos_w"][::-1],
        "qv": np.concatenate([diagonal(t) for t in z_mats[0]]
                             + [tile(z_mats[1].transpose(1, 0, 2).reshape(32, -1))], axis=1),
        "ew4": ew.reshape(E // 4, 4 * C, C).transpose(1, 0, 2),
        "masks": np.stack([a[f + "attn_mask"], a[f + "ffn_mask"]]).astype(np.int32).reshape(1, 2, NB * NOPS),
        "small4": np.concatenate([a[f + "wq"].swapaxes(2, 3), a[f + "wk"].swapaxes(2, 3),
                                  a[f + "wv"].swapaxes(2, 3), a[f + "wo"]], axis=3).reshape(NB * NOPS, C, 4 * C),
        "w1": a[f + "ffn_w1"].reshape(NB * NOPS, C, HID),
        "w2": a[f + "ffn_w2"].reshape(NB * NOPS, HID, C),
        "b1": a[f + "ffn_b1"].reshape(NB * NOPS, HID, 1),
        "b2": a[f + "ffn_b2"].reshape(NB * NOPS, C, 1),
    }
    nc = bacc.Bacc("TRN2", target_bir_lowering=False, num_devices=1)
    d = Mem()
    arrays = {k: np.ascontiguousarray(v) for k, v in arrays.items()}
    for k, v in arrays.items():
        vars(d)[k] = nc.dram_tensor("in_" + k, v.shape, mybir.dt.from_np(v.dtype), kind="ExternalInput").ap()
    d.out = nc.dram_tensor("out_0", (B, C, N), F32, kind="ExternalOutput").ap()
    conv_attn_hybrid(nc, d)
    r = run_bass_kernel_spmd(nc, [{"in_" + k: v for k, v in arrays.items()}], core_ids=[0])
    return r.results[0]["out_0"].reshape(B, C, H, W)
```
